# Optimizing a Trainium2 kernel written in Bass

```python
import numpy as np
import jax
import jax.numpy as jnp

def _softmax(x, axis=-1):
    return jax.nn.softmax(x, axis=axis)

def _gelu(x):
    return jax.nn.gelu(x, approximate=True)

def _silu(x):
    return jax.nn.silu(x)

def _sigmoid(x):
    return jax.nn.sigmoid(x)

def _layernorm(x, axis=-1, eps=1e-05):
    m = jnp.mean(x, axis=axis, keepdims=True)
    v = jnp.var(x, axis=axis, keepdims=True)
    return (x - m) / jnp.sqrt(v + eps)

def _scatter_add(tgt, idx, src, axis=0):
    return tgt.at[idx].add(src)

def _segment_sum(src, seg, n):
    return jax.ops.segment_sum(src, seg, n)
kernel_name = 'mk_gnn_ffn_d1_gnn_r16_d39c63'

def setup_inputs(seed: int=0):
    np.random.seed(seed)
    _w = jnp.asarray

    def _rec_inputs():
        import jax
        import jax.numpy as jnp
        _gk = jax.random.key(seed)
        x = -0.000202 + 1 * jax.random.normal(jax.random.fold_in(_gk, 1), (6250, 256), jnp.float32)
        src = jax.random.randint(jax.random.fold_in(_gk, 2), (100000,), 0, 6250, jnp.int32)
        dst = jnp.minimum((6250 * jax.random.uniform(jax.random.fold_in(_gk, 3), (100000,)) ** 2.0).astype(jnp.int32), 99999)
        _o = jnp.argsort(dst, stable=True)
        src = src[_o]
        dst = dst[_o]
        return (x, src, dst)
    x, src, dst = _rec_inputs()

    def _L0_gnn_setup():
        import jax, jax.numpy as jnp
        import numpy as np
        N_NODES = 25000
        N_EDGES = 25000
        D_IN = 256
        D_OUT = 256
        HEADS = 8
        HEAD_DIM = D_OUT // HEADS
        NEG_SLOPE = 0.2
        LN_EPS = 1e-05

        def layer_norm(x, g, b):
            mu = jnp.mean(x, axis=-1, keepdims=True)
            var = jnp.mean((x - mu) ** 2, axis=-1, keepdims=True)
            return (x - mu) * jax.lax.rsqrt(var + LN_EPS) * g + b

        def gelu_tanh(x):
            c = np.sqrt(2.0 / np.pi).astype(np.float32)
            return 0.5 * x * (1.0 + jnp.tanh(c * (x + 0.044715 * x ** 3)))
        key = jax.random.key(seed)
        ks = jax.random.split(key, 16)
        s_in = 1.0 / np.sqrt(D_IN)
        s_out = 1.0 / np.sqrt(D_OUT)
        s_ff = 1.0 / np.sqrt(4 * D_OUT)
        return {'x': jax.random.normal(ks[0], (N_NODES, D_IN), jnp.float32), 'edge_index': jax.random.randint(ks[1], (2, N_EDGES), 0, N_NODES, jnp.int64), 'W': jax.random.normal(ks[2], (D_IN, HEADS * HEAD_DIM), jnp.float32) * s_in, 'att_src': jax.random.normal(ks[3], (HEADS, HEAD_DIM), jnp.float32) * s_out, 'att_dst': jax.random.normal(ks[4], (HEADS, HEAD_DIM), jnp.float32) * s_out, 'bias': jnp.zeros((D_OUT,), jnp.float32), 'W_res': jax.random.normal(ks[5], (D_IN, D_OUT), jnp.float32) * s_in, 'ln1_g': jnp.ones((D_IN,), jnp.float32), 'ln1_b': jnp.zeros((D_IN,), jnp.float32), 'ln2_g': jnp.ones((D_OUT,), jnp.float32), 'ln2_b': jnp.zeros((D_OUT,), jnp.float32), 'ffn_w1': jax.random.normal(ks[6], (D_OUT, 4 * D_OUT), jnp.float32) * s_out, 'ffn_b1': jnp.zeros((4 * D_OUT,), jnp.float32), 'ffn_w2': jax.random.normal(ks[7], (4 * D_OUT, D_OUT), jnp.float32) * s_ff, 'ffn_b2': jnp.zeros((D_OUT,), jnp.float32)}
    _L0_gnn_all = _L0_gnn_setup()
    _L0_gnn_in = {k: v for k, v in _L0_gnn_all.items() if k in ('W', 'att_src', 'att_dst', 'bias', 'W_res', 'ln1_g', 'ln1_b', 'ln2_g', 'ln2_b', 'ffn_w1', 'ffn_b1', 'ffn_w2', 'ffn_b2')}
    del _L0_gnn_all

    def _L0_ffn_setup():
        import jax, jax.numpy as jnp
        import numpy as np
        TOP_K = 2
        LN_EPS = 1e-05
        key = jax.random.key(seed)
        ks = jax.random.split(key, 8)
        B, S, D, E, H = (16, 1024, 256, 8, 1024)
        x = jax.random.normal(ks[0], (B, S, D), dtype=jnp.float32)
        Wr = jax.random.normal(ks[1], (D, E), dtype=jnp.float32) * 0.1
        br = jnp.zeros((E,), dtype=jnp.float32)
        ln_g = jnp.ones((E, D), dtype=jnp.float32)
        ln_b = jnp.zeros((E, D), dtype=jnp.float32)
        W1 = jax.random.normal(ks[2], (E, D, H), dtype=jnp.float32) * (1.0 / np.sqrt(D))
        b1 = jnp.zeros((E, H), dtype=jnp.float32)
        W2 = jax.random.normal(ks[3], (E, H, D), dtype=jnp.float32) * (1.0 / np.sqrt(H))
        b2 = jnp.zeros((E, D), dtype=jnp.float32)
        return {'x': x, 'Wr': Wr, 'br': br, 'ln_g': ln_g, 'ln_b': ln_b, 'W1': W1, 'b1': b1, 'W2': W2, 'b2': b2}
    _L0_ffn_all = _L0_ffn_setup()
    _L0_ffn_in = {k: v for k, v in _L0_ffn_all.items() if k in ('Wr', 'br', 'ln_g', 'ln_b', 'W1', 'b1', 'W2', 'b2')}
    del _L0_ffn_all
    return {'x': x, 'src': src, 'dst': dst, 'L0_gnn_W': _L0_gnn_in['W'], 'L0_gnn_att_src': _L0_gnn_in['att_src'], 'L0_gnn_att_dst': _L0_gnn_in['att_dst'], 'L0_gnn_bias': _L0_gnn_in['bias'], 'L0_gnn_W_res': _L0_gnn_in['W_res'], 'L0_gnn_ln1_g': _L0_gnn_in['ln1_g'], 'L0_gnn_ln1_b': _L0_gnn_in['ln1_b'], 'L0_gnn_ln2_g': _L0_gnn_in['ln2_g'], 'L0_gnn_ln2_b': _L0_gnn_in['ln2_b'], 'L0_gnn_ffn_w1': _L0_gnn_in['ffn_w1'], 'L0_gnn_ffn_b1': _L0_gnn_in['ffn_b1'], 'L0_gnn_ffn_w2': _L0_gnn_in['ffn_w2'], 'L0_gnn_ffn_b2': _L0_gnn_in['ffn_b2'], 'L0_ffn_Wr': _L0_ffn_in['Wr'], 'L0_ffn_br': _L0_ffn_in['br'], 'L0_ffn_ln_g': _L0_ffn_in['ln_g'], 'L0_ffn_ln_b': _L0_ffn_in['ln_b'], 'L0_ffn_W1': _L0_ffn_in['W1'], 'L0_ffn_b1': _L0_ffn_in['b1'], 'L0_ffn_W2': _L0_ffn_in['W2'], 'L0_ffn_b2': _L0_ffn_in['b2']}

def reference(x, src, dst, L0_gnn_W, L0_gnn_att_src, L0_gnn_att_dst, L0_gnn_bias, L0_gnn_W_res, L0_gnn_ln1_g, L0_gnn_ln1_b, L0_gnn_ln2_g, L0_gnn_ln2_b, L0_gnn_ffn_w1, L0_gnn_ffn_b1, L0_gnn_ffn_w2, L0_gnn_ffn_b2, L0_ffn_Wr, L0_ffn_br, L0_ffn_ln_g, L0_ffn_ln_b, L0_ffn_W1, L0_ffn_b1, L0_ffn_W2, L0_ffn_b2):
    import jax
    import jax.numpy as jnp

    def _L0_gnn_ref(x, edge_index, W, att_src, att_dst, bias, W_res, ln1_g, ln1_b, ln2_g, ln2_b, ffn_w1, ffn_b1, ffn_w2, ffn_b2):
        import jax, jax.numpy as jnp
        import numpy as np
        N_NODES = 25000
        N_EDGES = 25000
        D_IN = 256
        D_OUT = 256
        HEADS = 8
        HEAD_DIM = D_OUT // HEADS
        NEG_SLOPE = 0.2
        LN_EPS = 1e-05

        def layer_norm(x, g, b):
            mu = jnp.mean(x, axis=-1, keepdims=True)
            var = jnp.mean((x - mu) ** 2, axis=-1, keepdims=True)
            return (x - mu) * jax.lax.rsqrt(var + LN_EPS) * g + b

        def gelu_tanh(x):
            c = np.sqrt(2.0 / np.pi).astype(np.float32)
            return 0.5 * x * (1.0 + jnp.tanh(c * (x + 0.044715 * x ** 3)))
        N = x.shape[0]
        xn = layer_norm(x, ln1_g, ln1_b)
        loops = jnp.arange(N, dtype=edge_index.dtype)
        src = jnp.concatenate([edge_index[0], loops])
        dst = jnp.concatenate([edge_index[1], loops])
        h = (xn @ W).reshape(N, HEADS, HEAD_DIM)
        a_src = jnp.einsum('nhd,hd->nh', h, att_src)
        a_dst = jnp.einsum('nhd,hd->nh', h, att_dst)
        e = jax.nn.leaky_relu(a_src[src] + a_dst[dst], NEG_SLOPE)
        emax = jax.ops.segment_max(e, dst, num_segments=N)
        ee = jnp.exp(e - emax[dst])
        denom = jax.ops.segment_sum(ee, dst, num_segments=N)
        alpha = ee / denom[dst]
        msg = h[src] * alpha[:, :, None]
        agg = jax.ops.segment_sum(msg, dst, num_segments=N)
        out = agg.reshape(N, HEADS * HEAD_DIM) + xn @ W_res + bias
        out = layer_norm(out, ln2_g, ln2_b)
        ff = gelu_tanh(out @ ffn_w1 + ffn_b1) @ ffn_w2 + ffn_b2
        return out + ff

    def _L0_ffn_ref(x, Wr, br, ln_g, ln_b, W1, b1, W2, b2):
        import jax, jax.numpy as jnp
        import numpy as np
        TOP_K = 2
        LN_EPS = 1e-05
        B, S, D = x.shape
        N = B * S
        xt = x.reshape(N, D)
        logits = xt @ Wr + br
        probs = jax.nn.softmax(logits, axis=-1)
        top_p, top_idx = jax.lax.top_k(probs, TOP_K)
        weights = top_p / top_p.sum(axis=-1, keepdims=True)
        mu = xt.mean(axis=-1, keepdims=True)
        var = ((xt - mu) ** 2).mean(axis=-1, keepdims=True)
        xn = (xt - mu) * jax.lax.rsqrt(var + LN_EPS)
        xe = xn[None, :, :] * ln_g[:, None, :] + ln_b[:, None, :]
        h = jax.nn.gelu(jnp.einsum('end,edh->enh', xe, W1) + b1[:, None, :], approximate=False)
        y = jnp.einsum('enh,ehd->end', h, W2) + b2[:, None, :]
        y_tok = jnp.transpose(y, (1, 0, 2))
        sel = jnp.take_along_axis(y_tok, top_idx[:, :, None], axis=1)
        out = (weights[:, :, None] * sel).sum(axis=1)
        return out.reshape(B, S, D)
    edge_index = jnp.stack([src, dst])
    x = x + _L0_gnn_ref(_layernorm(x, axis=-1), edge_index, L0_gnn_W, L0_gnn_att_src, L0_gnn_att_dst, L0_gnn_bias, L0_gnn_W_res, L0_gnn_ln1_g, L0_gnn_ln1_b, L0_gnn_ln2_g, L0_gnn_ln2_b, L0_gnn_ffn_w1, L0_gnn_ffn_b1, L0_gnn_ffn_w2, L0_gnn_ffn_b2)
    x = x + _L0_ffn_ref(_layernorm(x, axis=-1)[None], L0_ffn_Wr, L0_ffn_br, L0_ffn_ln_g, L0_ffn_ln_b, L0_ffn_W1, L0_ffn_b1, L0_ffn_W2, L0_ffn_b2)[0]
    return x

_drawn_inputs = setup_inputs


def setup_inputs(seed=0):
    import zlib

    import numpy as np

    out = dict(_drawn_inputs(seed))
    spreads = {'L0_gnn_bias': (0.0, 0.1),
     'L0_gnn_ln1_g': (1.0, 0.2),
     'L0_gnn_ln1_b': (0.0, 0.1),
     'L0_gnn_ln2_g': (1.0, 0.2),
     'L0_gnn_ln2_b': (0.0, 0.1),
     'L0_gnn_ffn_b1': (0.0, 0.1),
     'L0_gnn_ffn_b2': (0.0, 0.1),
     'L0_ffn_br': (0.0, 0.1),
     'L0_ffn_ln_g': (1.0, 0.2),
     'L0_ffn_ln_b': (0.0, 0.1),
     'L0_ffn_b1': (0.0, 0.1),
     'L0_ffn_b2': (0.0, 0.1)}
    factors = {}
    for name, (base, spread) in spreads.items():
        noise = np.random.default_rng([zlib.crc32(name.encode()), seed]).standard_normal(out[name].shape)
        drawn = base * np.exp(spread * noise) if base else spread * noise
        out[name] = jnp.asarray(drawn.astype(out[name].dtype))
    for name, factor in factors.items():
        out[name] = (out[name] * factor).astype(out[name].dtype)
    return out
```

```python
from contextlib import ExitStack

import concourse.bass as bass
from concourse import mybir

F32 = mybir.dt.float32
I32 = mybir.dt.int32
U32 = mybir.dt.uint32
ALU = mybir.AluOpType
ACT = mybir.ActivationFunctionType
AX = mybir.AxisListType

P = 128
BIG = 1.0e30
EPS = 1e-5
SLOPE = 0.2


class Counter:

    def __init__(self, nc, ctx, name):
        self.sem, self.value = ctx.enter_context(nc.semaphore(name)), 0

    def mark(self, instruction, by=1):
        instruction.then_inc(self.sem, by)
        self.value += by
        return self.sem, self.value


def wait(engine, *tokens):
    for token in tokens:
        if token is not None:
            engine.wait_ge(*token)


def build(nc, x, src, dst, gW, att_src, att_dst, g_bias, gW_res, ln1_g, ln1_b, ln2_g, ln2_b,
          f_w1, f_b1, f_w2, f_b2, Wr, br, ln_g, ln_b, W1, b1, W2, b2, out):
    N, D = x.shape
    HEADS, HD = att_src.shape
    HID = f_w1.shape[1]
    E = Wr.shape[1]
    KC = D // P
    MC = HID // P
    NT = -(-N // P)
    NB = -(-NT // 4)
    EB = 256
    NEB = dst.shape[0] // EB
    WIN = NT + 1
    GS = 8
    NG = -(-(NEB + NT - 1) // GS)
    NSTEP = NG * GS
    NK = -(-NSTEP // P)
    GT = 2 * GS
    HC = HD + 1
    AGG = HEADS * HC
    ROW = AGG + HEADS
    WROW = ROW + HEADS
    last_rows = N - (NT - 1) * P

    ctx = ExitStack()
    with ctx:
        def sb(name, shape, dt=F32):
            return ctx.enter_context(nc.sbuf_tensor(name, shape, dt))

        def counter(name):
            return Counter(nc, ctx, name)

        def dram(name, shape, dt=F32):
            return nc.dram_tensor(name, shape, dt, kind="Internal").ap()

        pe, dve, act, pool, sp = nc.tensor, nc.vector, nc.scalar, nc.gpsimd, nc.sync

        node_table = dram("node_table", [NT * P, ROW])
        residual = dram("residual", [NT * P, D])
        step_new = dram("step_new", [NK * P, EB])
        step_last = dram("step_last", [NK * P, EB])
        x1_dram = dram("x1", [NT * P, D])
        slots_total = (2 * N + E * 255) // 256 * 256
        slot_rows = dram("slot_rows", [slots_total, D])
        slot_out = dram("slot_out", [slots_total, D])
        step_win = dram("step_win", [NK * P, 1], I32)

        c_ld = counter("const_loads")
        c_pool = counter("pool_done")
        vA, aA, pA = counter("dve_nodes"), counter("act_nodes"), counter("pe_nodes")
        vB, pB = counter("dve_prep"), counter("pe_prep")
        vC, aC, pC = counter("dve_edges"), counter("act_edges"), counter("pe_edges")
        c_x = [counter(f"x_loaded{i}") for i in range(3)]
        c_tab, c_res = counter("table_written"), counter("residual_written")
        c_prep = counter("prep_dma")

        bank = [ctx.enter_context(nc.psum_tensor(f"bank{i}", [P, 512], F32)) for i in range(8)]

        ident = sb("ident", [P, P])
        iota_row = sb("iota_row", [P, P])
        ones = sb("ones", [P, P])
        zero = sb("zero", [P, D])
        neg_half = sb("neg_half", [P, 8])
        arena = sb("arena", [P, 33280])

        def part(offset, *shape):
            size = 1
            for s in shape:
                size *= s
            flat = arena[:, offset:offset + size]
            if len(shape) == 1:
                return flat
            names = "abcd"[:len(shape)]
            return flat.rearrange(f"p ({' '.join(names)}) -> p {' '.join(names)}",
                                  **{n: s for n, s in zip(names, shape)})

        win = part(0, WIN, WROW)
        GATH = WIN * WROW
        gath = [part(GATH + i * GT * ROW, GT, ROW) for i in range(3)]
        OH0 = GATH + 3 * GT * ROW
        onehot = [part(OH0 + i * GT * P, GT, P) for i in range(2)]
        OT0 = OH0 + 2 * GT * P
        onehot_t = part(OT0, GT, P)
        assert OT0 + GT * P <= 33280, OT0 + GT * P

        WORK = 10240
        work = sb("work", [P, WORK])

        def work_part(offset, *shape):
            size = 1
            for d in shape:
                size *= d
            names = "abcd"[:len(shape)]
            return work[:, offset:offset + size].rearrange(
                f"p ({' '.join(names)}) -> p {' '.join(names)}", **{n: d for n, d in zip(names, shape)})

        xs = [part(GATH + i * 4 * D, 4, D) for i in range(3)]
        o = GATH + 12 * D
        xnT = [part(o + i * KC * 512, KC, 512) for i in range(2)]
        o += 2 * KC * 512
        res_st = [part(o + i * 4 * D, 4, D) for i in range(2)]
        o += 8 * D
        Wc = part(o, KC, D + 2 * HEADS)
        o += KC * (D + 2 * HEADS)
        Wres = part(o, KC, D)
        o += KC * D
        att = part(o, 2, D)
        att_tmp = part(o + 2 * D, D)
        bias_b = part(o + 3 * D, D)

        src_col = sb("src_col", [P, NK * P, 2], I32)
        dst_col = sb("dst_col", [P, NK * P, 2])
        last_col = sb("last_col", [P, NK * P, 2])
        win_row = sb("win_row", [1, NSTEP], I32)

        t_c0 = c_pool.mark(pool.memset(ident[:, :], 0.0))
        c_pool.mark(pool.memset(ones[:, :], 1.0))
        c_pool.mark(pool.memset(neg_half[:, :], -0.5))
        wait(pool, t_c0)
        c_pool.mark(pool.affine_select(out=ident[:, :], in_=ident[:, :], compare_op=ALU.not_equal,
                                       fill=1.0, base=0, pattern=[[-1, P]], channel_multiplier=1))
        iota_i = part(OT0, P).bitcast(I32)
        t_i = c_pool.mark(pool.iota(iota_i, pattern=[[1, P]], base=0, channel_multiplier=0))
        wait(dve, t_i)
        t_const = vB.mark(dve.tensor_copy(iota_row[:, :], iota_i))
        ident_ready = (c_pool.sem, c_pool.value)

        def load(dst_ap, src_ap, c=None):
            return (c or c_ld).mark(sp.dma_start(dst_ap, src_ap), 16)

        g1 = sb("g1", [P, 2, KC])
        for k in range(KC):
            load(Wc[:, k, 0:D], gW[k * P:(k + 1) * P, :])
            load(Wres[:, k, :], gW_res[k * P:(k + 1) * P, :])
        with nc.allow_non_contiguous_dma(reason="a few small vectors, one element per partition"):
            load(g1[:, 0, :], ln1_g.rearrange("(k p) -> p k", p=P))
            load(g1[:, 1, :], ln1_b.rearrange("(k p) -> p k", p=P))
        load(att[:, 0, :], att_src.rearrange("h d -> (h d)").unsqueeze(0).to_broadcast([P, D]))
        load(att[:, 1, :], att_dst.rearrange("h d -> (h d)").unsqueeze(0).to_broadcast([P, D]))
        weights_loaded = load(bias_b, g_bias.unsqueeze(0).to_broadcast([P, D]))

        wait(dve, weights_loaded)
        for k in range(KC):
            for s in range(2):
                t = vA.mark(dve.tensor_tensor(att_tmp, Wc[:, k, 0:D], att[:, s, :], ALU.mult))
                wait(dve, t)
                t_att = vA.mark(dve.tensor_reduce(Wc[:, k, D + s * HEADS:D + (s + 1) * HEADS],
                                                  att_tmp.rearrange("p (h d) -> p h d", d=HD),
                                                  AX.X, ALU.add))
                wait(dve, t_att)
        t_wc = t_att
        t_ones = vA.mark(dve.memset(win[:, :, 0:AGG].rearrange("p w (h c) -> p w h c", c=HC)[:, :, :, HD:HC], 1.0))
        wait(dve, t_ones)
        t_padw = vA.mark(dve.memset(win[:, NT, :], 0.0))
        t_xpad = None
        stats = sb("stats", [P, 4, 6])
        mv = sb("mv", [P, 4, 2])
        rstd = sb("rstd", [P, 4])

        def layer_norm(tiles, c, ready, stats, mv, rstd):
            n = len(tiles)
            wait(dve, ready)
            for j, xt in enumerate(tiles):
                t = c.mark(dve.bn_stats(stats[:, j, :], xt))
            wait(dve, t)
            for j in range(n):
                t = c.mark(dve.bn_aggr(mv[:, j, :], stats[:, j, :]))
            wait(dve, t)
            t = c.mark(dve.tensor_scalar(mv[:, 0:n, 1], mv[:, 0:n, 1], EPS, None, ALU.add))
            wait(pool, t)
            t = c_pool.mark(pool.tensor_tensor(rstd[:, 0:n], mv[:, 0:n, 1], neg_half[:, 0:n], ALU.pow))
            wait(dve, t)
            for j, xt in enumerate(tiles):
                t = c.mark(dve.tensor_scalar(xt, xt, mv[:, j, 0:1], rstd[:, j:j + 1], ALU.subtract, ALU.mult))
            return t

        def tiles_of(b):
            return min(4, NT - 4 * b)

        x_free, xnT_free, res_free = [None] * 3, [None] * 2, [None] * 2
        loadedA, normedA = {}, {}

        def a_load(b):
            n, buf = tiles_of(b), xs[b % 3]
            wait(sp, x_free[b % 3])
            if b == NB - 1:
                wait(dve, x_free[b % 3])
                t = vA.mark(dve.memset(buf[:, n - 1, :], 0.0))
                wait(sp, t)
                if n > 1:
                    c_x[b % 3].mark(sp.dma_start(buf[:, 0:n - 1, :], x[4 * b * P:(NT - 1) * P, :].rearrange("(t p) d -> p t d", p=P)), 16)
                loadedA[b] = c_x[b % 3].mark(sp.dma_start(buf[0:last_rows, n - 1, :], x[(NT - 1) * P:N, :]), 16)
            else:
                loadedA[b] = c_x[b % 3].mark(sp.dma_start(buf[:, 0:n, :], x[4 * b * P:(4 * b + n) * P, :].rearrange("(t p) d -> p t d", p=P)), 16)

        def a_norm(b):
            n, buf = tiles_of(b), xs[b % 3]
            t = layer_norm([buf[:, j, :] for j in range(n)], vA, loadedA[b], stats, mv, rstd)
            normedA[b] = layer_norm([buf[:, j, :] for j in range(n)], vA, t, stats, mv, rstd)

        bank_free = [None] * 8
        xnT_ready = {}

        def a_turn(b):
            n, buf = tiles_of(b), xs[b % 3]
            wait(pe, normedA[b], ident_ready)
            for k in range(KC):
                bk = 2 * (b % 2) + k
                wait(pe, bank_free[bk])
                for j in range(n):
                    ins = pe.transpose(bank[bk][:, j * P:(j + 1) * P], buf[:, j, k * P:(k + 1) * P], ident[:, :])
                t = pA.mark(ins)
                wait(act, t, weights_loaded, xnT_free[b % 2])
                xnT_ready[b] = bank_free[bk] = aA.mark(act.activation(
                    xnT[b % 2][:, k, 0:n * P], bank[bk][:, 0:n * P], ACT.Identity,
                    scale=g1[:, 0, k:k + 1], bias=g1[:, 1, k:k + 1]))
            x_free[b % 3] = t

        def a_project(b):
            n = tiles_of(b)
            wait(pe, xnT_ready[b], t_wc)
            wait(act, t_ones)
            for j in range(n):
                w = 4 * b + j
                bh, br_ = 4 + (j % 2), 6 + (j % 2)
                wait(pe, bank_free[bh])
                for k in range(KC):
                    ins = pe.matmul(bank[bh][:, 0:D + 2 * HEADS], xnT[b % 2][:, k, j * P:(j + 1) * P],
                                    Wc[:, k, :], start=(k == 0), stop=(k == KC - 1))
                t_h = pA.mark(ins)
                wait(pe, bank_free[br_])
                for k in range(KC):
                    ins = pe.matmul(bank[br_][:, 0:D], xnT[b % 2][:, k, j * P:(j + 1) * P],
                                    Wres[:, k, :], start=(k == 0), stop=(k == KC - 1))
                t_r = pA.mark(ins)
                wait(act, t_h)
                aA.mark(act.copy(win[:, w, 0:AGG].rearrange("p (h c) -> p h c", c=HC)[:, :, 0:HD],
                                 bank[bh][:, 0:D].rearrange("p (h d) -> p h d", d=HD)))
                t_w = bank_free[bh] = aA.mark(act.copy(win[:, w, AGG:WROW], bank[bh][:, D:D + 2 * HEADS]))
                wait(dve, t_r, res_free[b % 2] if j == 0 else None)
                t_rs = bank_free[br_] = vA.mark(dve.tensor_tensor(res_st[b % 2][:, j, :], bank[br_][:, 0:D], bias_b, ALU.add))
            xnT_free[b % 2] = t_r
            wait(sp, t_w, t_ones)
            rows = slice(4 * b * P, (4 * b + n) * P)
            c_tab.mark(sp.dma_start(node_table[rows, :].rearrange("(t p) c -> p t c", p=P),
                                    win[:, 4 * b:4 * b + n, 0:ROW]), 16)
            wait(sp, t_rs)
            c_r = c_resb[b % 2]
            res_free[b % 2] = c_r.mark(sp.dma_start(residual[rows, :].rearrange("(t p) c -> p t c", p=P),
                                                    res_st[b % 2][:, 0:n, :]), 16)

        c_resb = [counter(f"residual_written{i}") for i in range(2)]

        dst_rows = dst.rearrange("(b e) -> b e", e=EB)
        src_rows = src.rearrange("(b e) -> b e", e=EB)
        PB0 = OH0
        first = part(PB0, NEB).bitcast(I32)
        first_w = part(PB0 + 400, NEB)
        iota_b = part(PB0 + 800, 400).bitcast(I32)
        le = part(PB0 + 1200, NEB)
        count = sb("count", [P, 4 * 5])
        kcol = sb("kcol", [P, NK], I32)
        tk_i = sb("tk_i", [P, NK], I32)
        wk_i = sb("wk_i", [P, NK], I32)
        rows_i = part(PB0 + 1600, NK, EB).bitcast(I32)
        rows_s = part(PB0 + 1600 + NK * EB, NK, EB)
        rows_d = part(PB0 + 1600 + 2 * NK * EB, NK, EB + 2)
        rows_n = part(PB0 + 1600 + 3 * NK * EB + 16, NK, EB)
        assert PB0 + 1600 + 4 * NK * EB + 16 <= OT0 + GT * P
        c_rows = counter("step_rows")
        c_scr = counter("step_scratch")

        def b_prep():
            with nc.allow_non_contiguous_dma(reason="one element per edge block"):
                t_f = load(first[0:1, :], dst_rows[:, 0:1].rearrange("b o -> o b"), c_prep)
            t_i1 = c_pool.mark(pool.iota(iota_b[0:1, 0:NEB], pattern=[[1, NEB]], base=0, channel_multiplier=0))
            t_i2 = c_pool.mark(pool.iota(kcol[:, :], pattern=[[P, NK]], base=0, channel_multiplier=1))
            wait(dve, t_f, t_i1, t_i2)
            t = vB.mark(dve.tensor_single_scalar(first[0:1, :], first[0:1, :], 7, ALU.arith_shift_right))
            wait(dve, t)
            t = vB.mark(dve.tensor_scalar(first_w[0:1, :], first[0:1, :], float(NT - 1), None, ALU.min))
            wait(dve, t)
            t = vB.mark(dve.memset(first_w[0:1, 0:1], 0.0))
            wait(dve, t)
            t = vB.mark(dve.tensor_tensor(first_w[0:1, :], first_w[0:1, :], iota_b[0:1, 0:NEB], ALU.add))
            wait(pe, t, ident_ready)
            t = pB.mark(pe.matmul(bank[7][:, 0:NEB], ones[0:1, :], first_w[0:1, :], start=True, stop=True))
            wait(dve, t)
            kf, tf, wf = count[:, 0:NK], count[:, NK:2 * NK], count[:, 2 * NK:3 * NK]
            t = vB.mark(dve.tensor_copy(kf, kcol[:, :]))
            wait(dve, t)
            for c in range(NK):
                t = vB.mark(dve.tensor_scalar(le, bank[7][:, 0:NEB], kf[:, c:c + 1], None, ALU.is_le))
                wait(dve, t)
                t = vB.mark(dve.tensor_reduce(tf[:, c:c + 1], le, AX.X, ALU.add))
                wait(dve, t)
            t = vB.mark(dve.tensor_scalar(tf, tf, -1.0, None, ALU.add))
            wait(dve, t)
            t_tk = vB.mark(dve.tensor_copy(tk_i[:, :], tf))
            t = vB.mark(dve.tensor_tensor(wf, kf, tf, ALU.subtract))
            wait(dve, t)
            t_wk = vB.mark(dve.tensor_copy(wk_i[:, :], wf))
            t_w128 = vB.mark(dve.tensor_scalar(kf, wf, float(P), None, ALU.mult))
            wait(sp, t_wk)
            with nc.allow_non_contiguous_dma(reason="one element per step"):
                t = load(step_win.rearrange("(c p) o -> p (c o)", p=P), wk_i[:, :], c_prep)
                wait(sp, t)
                t_win = load(win_row[:, :], step_win[0:NSTEP, :].rearrange("k o -> o k"), c_prep)
            wait(pool, t_tk)
            for c in range(NK):
                c_rows.mark(pool.indirect_dma_start(rows_i[:, c, :], None, dst_rows, bass.IndirectOffsetOnAxis(ap=tk_i[:, c:c + 1], axis=0)), 16)
                t = c_rows.mark(pool.indirect_dma_start(rows_s[:, c, :].bitcast(I32), None, src_rows, bass.IndirectOffsetOnAxis(ap=tk_i[:, c:c + 1], axis=0)), 16)
            wait(dve, t, t_w128)
            t = vB.mark(dve.memset(rows_d[:, :, :], -1.0e6))
            wait(dve, t)
            for c in range(NK):
                t = vB.mark(dve.tensor_scalar(rows_d[:, c, 1:EB + 1], rows_i[:, c, :], kf[:, c:c + 1], None, ALU.subtract))
            wait(dve, t)
            src_f = rows_i[:, :, :].bitcast(F32)
            t_sf = vB.mark(dve.tensor_copy(src_f, rows_s.bitcast(I32)))
            for c in range(NK):
                t = vB.mark(dve.tensor_tensor(rows_n[:, c, :], rows_d[:, c, 1:EB + 1], rows_d[:, c, 0:EB], ALU.not_equal))
            wait(dve, t)
            t_new = vB.mark(dve.tensor_scalar(rows_n, rows_n, -BIG, None, ALU.mult))
            wait(sp, t_new)
            t = load(step_new.rearrange("(c p) e -> p c e", p=P), rows_n, c_scr)
            state = {"t": None}

            def columns(source, target, ready):
                for i in range(NK * 2):
                    c, j = i // 2, i % 2
                    bk = 4 + i % 2
                    wait(pe, ready, state.get(bk))
                    tt = pB.mark(pe.transpose(bank[bk][:, 0:P], source(c, j), ident[:, :]))
                    wait(dve, tt)
                    state[bk] = vB.mark(dve.tensor_copy(target[:, c * P:(c + 1) * P, j], bank[bk][:, 0:P]))
                return state[bk]

            t_s = columns(lambda c, j: src_f[:, c, j * P:(j + 1) * P], src_col, t_sf)
            t_d = columns(lambda c, j: rows_d[:, c, 1 + j * P:1 + (j + 1) * P], dst_col, t_sf)
            wait(dve, t)
            for c in range(NK):
                t_l = vB.mark(dve.tensor_tensor(rows_n[:, c, :], rows_d[:, c, 1:EB + 1], rows_d[:, c, 2:EB + 2], ALU.not_equal))
            wait(sp, t_l)
            t_scr = load(step_last.rearrange("(c p) e -> p c e", p=P), rows_n, c_scr)
            t_lc = columns(lambda c, j: rows_n[:, c, j * P:(j + 1) * P], last_col, t_l)
            return t_win, t_scr, t_s, t_lc

        t_win, t_scr, t_srccol, t_cols = b_prep()
        for i in range(NB + 2):
            if i < NB:
                a_load(i)
            if 1 <= i <= NB:
                a_norm(i - 1)
                a_turn(i - 1)
            if i >= 2:
                a_project(i - 2)
        table_written = (c_tab.sem, c_tab.value)
        node_phase_done = [(vA.sem, vA.value), (pA.sem, pA.value), (aA.sem, aA.value), res_free[0], res_free[1]]

        seg_new = [sb(f"seg_new{i}", [HEADS * GS, EB]) for i in range(2)]
        seg_last = [sb(f"seg_last{i}", [HEADS * GS, EB]) for i in range(2)]
        seg_max = sb("seg_max", [HEADS * GS, EB])
        asrc = sb("asrc", [P, 2, GS, HEADS])
        cand = sb("cand", [P, 2, GS, HEADS + 1])
        old = sb("old", [P, GS, 2 * HEADS])
        newm = sb("newm", [P, GS, HEADS])
        nodeval = sb("nodeval", [P, GS, 2 * HEADS])
        shift0 = sb("shift0", [P, GS, HEADS])
        absent = sb("absent", [P, GS])
        scale = [sb(f"scale{i}", [P, GS, HEADS]) for i in range(2)]
        score = sb("score", [P, GT, HEADS])
        wgt = sb("wgt", [P, GT, HEADS])
        c_g = [counter(f"gathered{i}") for i in range(3)]
        c_seg = [counter(f"segments{i}") for i in range(2)]
        gath_free = [None] * 3
        gathered, seg_loaded, seg_free = {}, {}, [None] * 2
        b_asrc, b_cand, b_ms, b_edge = bank[0], bank[0], bank[1], bank[2]
        oh_free, oh_ready, oht_ready, oht_free = [None] * 2, {}, {}, None
        ohp_free, agp_free = [None] * 2, [None] * 3
        msg_ready, scale_ready, scale_free = {}, {}, [None] * 2
        S = {}

        def fetch(g):
            if g == 0:
                wait(pool, table_written, t_srccol, *node_phase_done)
                wait(sp, t_scr)
            wait(pool, gath_free[g % 3])
            for t in range(GT):
                k = g * GS + t // 2
                gathered[g] = c_g[g % 3].mark(pool.indirect_dma_start(
                    gath[g % 3][:, t, :], None, node_table,
                    bass.IndirectOffsetOnAxis(ap=src_col[:, k, t % 2:t % 2 + 1], axis=0)), 16)
            wait(sp, seg_free[g % 2])
            rows = slice(g * GS, (g + 1) * GS)
            c_seg[g % 2].mark(sp.dma_start(seg_new[g % 2][:, :], step_new[rows, :].unsqueeze(1).to_broadcast([GS, HEADS, EB])), 16)
            seg_loaded[g] = c_seg[g % 2].mark(sp.dma_start(seg_last[g % 2][:, :], step_last[rows, :].unsqueeze(1).to_broadcast([GS, HEADS, EB])), 16)

        def one_hots(g):
            if g == 0:
                wait(dve, t_cols, t_scr)
            wait(dve, oh_free[g % 2])
            d = dst_col[:, g * GS:(g + 1) * GS, :].rearrange("p k j -> p (k j)")
            oh_ready[g] = vC.mark(dve.tensor_tensor(
                onehot[g % 2], iota_row[:, :].unsqueeze(1).to_broadcast([P, GT, P]),
                d.unsqueeze(2).to_broadcast([P, GT, P]), ALU.is_equal))

        def turn_one_hots(g):
            nonlocal oht_free
            wait(pe, oh_ready[g])
            wait(act, oht_free)
            for q in range(GT // 4):
                wait(pe, ohp_free[q % 2])
                for j in range(4):
                    ins = pe.transpose(bank[3 + q % 2][:, j * P:(j + 1) * P], onehot[g % 2][:, 4 * q + j, :], ident[:, :])
                t = pC.mark(ins)
                wait(act, t)
                oht_ready[g] = ohp_free[q % 2] = aC.mark(act.copy(
                    onehot_t[:, 4 * q:4 * q + 4, :], bank[3 + q % 2][:, :].rearrange("p (t n) -> p t n", n=P)))

        def seg_scan(g):
            gb = gath[g % 3].rearrange("p (k j) c -> p k j c", j=2)
            wait(act, gathered[g], S.get("asrc_turned"))
            t = aC.mark(act.copy(asrc[:, :, :, :], gb[:, :, :, AGG:ROW].rearrange("p k j h -> p j k h")))
            wait(pe, t, S.get("cand_read"))
            for j in range(2):
                ins = pe.transpose(b_asrc[0:HEADS * GS, j * P:(j + 1) * P], asrc[:, j, :, :].rearrange("p k h -> p (k h)"), ident[:, :])
            S["asrc_turned"] = t = pC.mark(ins)
            wait(dve, t, seg_loaded[g], S.get("cand_turned"))
            t = vC.mark(dve.tensor_tensor_scan(seg_max[:, :], seg_new[g % 2][:, :], b_asrc[0:HEADS * GS, 0:EB], -BIG, ALU.add, ALU.max))
            wait(dve, t)
            S["masked"] = seg_free[g % 2] = vC.mark(dve.tensor_tensor(seg_max[:, :], seg_max[:, :], seg_last[g % 2][:, :], ALU.mult))

        def seg_turn(g):
            wait(pe, S["masked"])
            for j in range(2):
                ins = pe.transpose(b_cand[:, EB + j * 64:EB + (j + 1) * 64], seg_max[:, j * P:(j + 1) * P], ident[0:64, 0:64])
            S["cand_turned"] = t = pC.mark(ins)
            wait(act, t, S.get("ms_done"))
            aC.mark(act.copy(cand[:, :, :, HEADS:HEADS + 1],
                             last_col[:, g * GS:(g + 1) * GS, :].rearrange("p k j -> p j k").unsqueeze(3)))
            S["cand_read"] = aC.mark(act.copy(cand[:, :, :, 0:HEADS], b_cand[:, EB:EB + P].rearrange("p (j k h) -> p j k h", j=2, k=GS)))

        def node_maxima(g):
            wait(pe, S["cand_read"], S.get("ms_read"))
            for k in range(GS):
                for j in range(2):
                    ins = pe.matmul(b_ms[:, k * 9:(k + 1) * 9], onehot[g % 2][:, 2 * k + j, :], cand[:, j, k, :],
                                    start=(j == 0), stop=(j == 1))
            S["ms_done"] = pC.mark(ins)

        def window(k):
            return dve.value_load(win_row[0:1, k:k + 1], min_val=0, max_val=WIN - 1)

        def shifts(g):
            ms = b_ms[:, 0:9 * GS].rearrange("p (k c) -> p k c", c=9)
            wait(dve, S["ms_done"])
            t = vC.mark(dve.tensor_scalar(absent[:, :], ms[:, :, HEADS], BIG, -BIG, ALU.mult, ALU.add))
            wait(dve, t)
            t = S["ms_read"] = vC.mark(dve.tensor_tensor(newm[:, :, :], ms[:, :, 0:HEADS], absent[:, :].unsqueeze(2).to_broadcast([P, GS, HEADS]), ALU.add))
            wait(dve, t)
            for k in range(GS):
                w = window(g * GS + k)
                wait(dve, vC.mark(dve.tensor_copy(old[:, k, :], win[:, w, AGG:WROW])))
                t = vC.mark(dve.tensor_tensor(win[:, w, AGG:ROW], win[:, w, AGG:ROW], newm[:, k, :], ALU.max))
                wait(dve, t)
            t = vC.mark(dve.tensor_tensor(newm[:, :, :], newm[:, :, :], old[:, :, 0:HEADS], ALU.max))
            wait(dve, t, S.get("edge_vals"))
            t = vC.mark(dve.tensor_copy(nodeval[:, :, 0:HEADS], old[:, :, HEADS:2 * HEADS]))
            wait(dve, t)
            for m in (newm[:, :, :], old[:, :, 0:HEADS]):
                t = vC.mark(dve.tensor_tensor(m, m, nodeval[:, :, 0:HEADS], ALU.add))
            wait(dve, t)
            vC.mark(dve.scalar_tensor_tensor(nodeval[:, :, HEADS:2 * HEADS], newm[:, :, :], SLOPE, newm[:, :, :], ALU.mult, ALU.max))
            t = vC.mark(dve.scalar_tensor_tensor(shift0[:, :, :], old[:, :, 0:HEADS], SLOPE, old[:, :, 0:HEADS], ALU.mult, ALU.max))
            wait(dve, t, scale_free[g % 2])
            S["nodeval"] = t = vC.mark(dve.tensor_tensor(scale[g % 2][:, :, :], shift0[:, :, :], nodeval[:, :, HEADS:2 * HEADS], ALU.subtract))
            wait(act, t)
            scale_ready[g] = aC.mark(act.activation(scale[g % 2][:, :, :], scale[g % 2][:, :, :], ACT.Exp))

        def edge_values(g):
            nonlocal oht_free
            wait(pe, S["nodeval"], oht_ready[g], S.get("score_read"))
            for t in range(GT):
                ins = pe.matmul(b_edge[:, t * 16:(t + 1) * 16], onehot_t[:, t, :], nodeval[:, t // 2, :], start=True, stop=True)
            S["edge_vals"] = oht_free = pC.mark(ins)

        def messages(g):
            gb = gath[g % 3]
            ev = b_edge[:, 0:16 * GT].rearrange("p (t c) -> p t c", c=16)
            wait(dve, S["edge_vals"], gathered[g], S.get("exp_done"))
            t = vC.mark(dve.tensor_tensor(score[:, :, :], gb[:, :, AGG:ROW], ev[:, :, 0:HEADS], ALU.add))
            wait(dve, t)
            t = vC.mark(dve.scalar_tensor_tensor(score[:, :, :], score[:, :, :], SLOPE, score[:, :, :], ALU.mult, ALU.max))
            wait(dve, t)
            t = S["score_read"] = vC.mark(dve.tensor_tensor(score[:, :, :], score[:, :, :], ev[:, :, HEADS:16], ALU.subtract))
            wait(act, t, S.get("weighted"))
            S["exp_done"] = t = aC.mark(act.activation(wgt[:, :, :], score[:, :, :], ACT.Exp))
            wait(dve, t)
            for q in range(4):
                r = slice(4 * q, 4 * q + 4)
                rows = gb[:, r, 0:AGG].rearrange("p t (h c) -> p t h c", c=HC)
                msg_ready[g, q] = S["weighted"] = vC.mark(dve.tensor_tensor(
                    rows, rows, wgt[:, r, :].unsqueeze(3).to_broadcast([P, 4, HEADS, HC]), ALU.mult))

        def sum_messages(g, k):
            bk = bank[5 + (g * GS + k) % 3]
            wait(pe, msg_ready[g, k // 2], agp_free[(g * GS + k) % 3])
            for j in range(2):
                ins = pe.matmul(bk[:, 0:AGG], onehot[g % 2][:, 2 * k + j, :], gath[g % 3][:, 2 * k + j, 0:AGG],
                                start=(j == 0), stop=(j == 1))
            S["sum", g, k] = pC.mark(ins)
            if k == GS - 1:
                gath_free[g % 3] = oh_free[g % 2] = S["sum", g, k]

        def add_messages(g, k):
            bk = bank[5 + (g * GS + k) % 3]
            w = window(g * GS + k)
            rows = win[:, w, 0:AGG].rearrange("p (h c) -> p h c", c=HC)
            wait(dve, scale_ready[g], S.get("added"))
            t = vC.mark(dve.tensor_tensor(rows, rows, scale[g % 2][:, k, :].unsqueeze(2).to_broadcast([P, HEADS, HC]), ALU.mult))
            wait(dve, t, S["sum", g, k])
            S["added"] = agp_free[(g * GS + k) % 3] = vC.mark(dve.tensor_tensor(win[:, w, 0:AGG], win[:, w, 0:AGG], bk[:, 0:AGG], ALU.add))
            if k == GS - 1:
                scale_free[g % 2] = S["added"]

        t = c_pool.mark(pool.memset(zero[:, :], 0.0))
        wait(sp, t)
        c_zero = counter("slots_zeroed")
        t_zero = load(slot_rows.rearrange("(p a) d -> p a d", p=P),
                      zero[:, :].unsqueeze(1).to_broadcast([P, slots_total // P, D]), c_zero)
        wait(dve, table_written, t_win, *node_phase_done)
        NGR = NG if not DEBUG_GROUPS else DEBUG_GROUPS
        fetch(0)
        one_hots(0)
        for g in range(NGR + 1):
            if g + 1 < NGR:
                fetch(g + 1)
            half = GS // 2
            if g < NGR:
                turn_one_hots(g)
                seg_scan(g)
            if g > 0:
                for k in range(half):
                    sum_messages(g - 1, k)
                    add_messages(g - 1, k)
            if g < NGR:
                seg_turn(g)
            if g > 0:
                for k in range(half, GS - 1):
                    sum_messages(g - 1, k)
            if g < NGR:
                node_maxima(g)
            if g > 0:
                add_messages(g - 1, half)
                sum_messages(g - 1, GS - 1)
                for k in range(half + 1, GS):
                    add_messages(g - 1, k)
            if g < NGR:
                shifts(g)
                edge_values(g)
            if g + 1 < NGR:
                one_hots(g + 1)
            if g < NGR:
                messages(g)
        edges_done = [(vC.sem, vC.value), (pC.sem, pC.value), (aC.sem, aC.value)]
        if DEBUG:
            dbg = dram("dbg_win", [P, WIN * WROW])
            wait(sp, *edges_done)
            t = c_scr.mark(sp.dma_start(dbg, arena[:, 0:WIN * WROW]), 16)
            wait(sp, t)

        o = GATH
        hidden = [part(o, MC, 512), work_part(0, MC, 512)]
        o += MC * 512
        res_in = [part(o + i * 4 * D, 4, D) for i in range(2)]
        o += 8 * D
        x_in = [part(o + i * 4 * D, 4, D) for i in range(2)]
        o += 8 * D
        rows = [part(o + i * 4 * D, 4, D) for i in range(2)]
        o += 8 * D
        zrow = part(o, 4, D)
        o += 4 * D
        zT = part(o, KC, 512)
        o += KC * 512
        ln2_gb = part(o, 2, D)
        fb2_b = part(o + 2 * D, D)
        o += 3 * D
        assert o <= 33280
        fw1 = work_part(MC * 512, KC, HID)
        fw2 = work_part(MC * 512 + KC * HID, MC, D)
        outT = [work_part(MC * 512 + 2 * KC * HID + i * KC * 512, KC, 512) for i in range(2)]
        rec = sb("rec", [P, 4, HEADS])
        wr_sb = sb("wr_sb", [P, KC, E])
        br_b = sb("br_b", [P, E])
        g2 = sb("g2", [P, 2, KC])
        fb1 = sb("fb1", [P, MC])
        logits = sb("logits", [P, NT, E])
        c_w2 = counter("layer_weights")
        vD, aD, pD = counter("dve_layer"), counter("act_layer"), counter("pe_layer")
        c_in = [counter(f"layer_in{i}") for i in range(2)]
        c_x1 = [counter(f"x1_written{i}") for i in range(2)]

        wait(sp, *edges_done)
        for k in range(KC):
            load(fw1[:, k, :], f_w1[k * P:(k + 1) * P, :], c_w2)
            load(wr_sb[:, k, :], Wr[k * P:(k + 1) * P, :], c_w2)
        load(fw2, f_w2.rearrange("(m p) d -> p m d", p=P), c_w2)
        load(ln2_gb[:, 0, :], ln2_g.unsqueeze(0).to_broadcast([P, D]), c_w2)
        load(ln2_gb[:, 1, :], ln2_b.unsqueeze(0).to_broadcast([P, D]), c_w2)
        load(fb2_b, f_b2.unsqueeze(0).to_broadcast([P, D]), c_w2)
        load(br_b[:, :], br.unsqueeze(0).to_broadcast([P, E]), c_w2)
        with nc.allow_non_contiguous_dma(reason="a few small vectors, one element per partition"):
            load(g2[:, 0, :], ln2_g.rearrange("(k p) -> p k", p=P), c_w2)
            load(g2[:, 1, :], ln2_b.rearrange("(k p) -> p k", p=P), c_w2)
            t_fw = load(fb1[:, :], f_b1.rearrange("(m p) -> p m", p=P), c_w2)
        wait(dve, t_fw, *edges_done)
        t_gb = vD.mark(dve.tensor_tensor(fb2_b, fb2_b, ln2_gb[:, 1, :], ALU.add))
        wait(act, *edges_done)
        wait(pe, *edges_done)
        wait(pool, *edges_done)

        bank_free = [None] * 8
        in_free, hid_free, outT_free, x1_free = [None] * 2, [None] * 2, [None] * 2, [None] * 2
        D_ = {}

        def d_load(b):
            n, i = tiles_of(b), b % 2
            wait(sp, in_free[i])
            r = slice(4 * b * P, (4 * b + n) * P)
            c_in[i].mark(sp.dma_start(res_in[i][:, 0:n, :], residual[r, :].rearrange("(t p) d -> p t d", p=P)), 16)
            if b == NB - 1:
                wait(dve, in_free[i])
                wait(sp, vD.mark(dve.memset(x_in[i][:, n - 1, :], 0.0)))
                if n > 1:
                    c_in[i].mark(sp.dma_start(x_in[i][:, 0:n - 1, :], x[4 * b * P:(NT - 1) * P, :].rearrange("(t p) d -> p t d", p=P)), 16)
                D_["in", b] = c_in[i].mark(sp.dma_start(x_in[i][0:last_rows, n - 1, :], x[(NT - 1) * P:N, :]), 16)
            else:
                D_["in", b] = c_in[i].mark(sp.dma_start(x_in[i][:, 0:n, :], x[r, :].rearrange("(t p) d -> p t d", p=P)), 16)

        def norm_into(dsts, srcs, ready):
            n = len(srcs)
            wait(dve, ready)
            for j, xt in enumerate(srcs):
                t = vD.mark(dve.bn_stats(stats[:, j, :], xt))
            wait(dve, t)
            for j in range(n):
                t = vD.mark(dve.bn_aggr(mv[:, j, :], stats[:, j, :]))
            wait(dve, t)
            t = vD.mark(dve.tensor_scalar(mv[:, 0:n, 1], mv[:, 0:n, 1], EPS, None, ALU.add))
            wait(pool, t)
            t = c_pool.mark(pool.tensor_tensor(rstd[:, 0:n], mv[:, 0:n, 1], neg_half[:, 0:n], ALU.pow))
            wait(dve, t)
            for j, (d, xt) in enumerate(zip(dsts, srcs)):
                t = vD.mark(dve.tensor_scalar(d, xt, mv[:, j, 0:1], rstd[:, j:j + 1], ALU.subtract, ALU.mult))
            return t

        def d_merge(b):
            n, i = tiles_of(b), b % 2
            wv = win[:, 4 * b:4 * b + n, 0:AGG].rearrange("p t (h c) -> p t h c", c=HC)
            rv = rows[i][:, 0:n, :].rearrange("p t (h d) -> p t h d", d=HD)
            wait(dve, D_.get("rec_used"), x1_free[i])
            t = vD.mark(dve.reciprocal(rec[:, 0:n, :].unsqueeze(3), wv[:, :, :, HD:HC]))
            wait(dve, t)
            t = D_["rec_used"] = vD.mark(dve.tensor_tensor(rv, wv[:, :, :, 0:HD], rec[:, 0:n, :].unsqueeze(3).to_broadcast([P, n, HEADS, HD]), ALU.mult))
            wait(dve, t, D_["in", b])
            t = vD.mark(dve.tensor_tensor(rows[i][:, 0:n, :], rows[i][:, 0:n, :], res_in[i][:, 0:n, :], ALU.add))
            tl = [rows[i][:, j, :] for j in range(n)]
            D_["norm", b] = norm_into(tl, tl, t)

        def turn(src, dst, n, b0, ready, dst_free, scaled):
            wait(pe, ready)
            for k in range(KC):
                bk = b0 + k
                wait(pe, bank_free[bk])
                for j in range(n):
                    ins = pe.transpose(bank[bk][:, j * P:(j + 1) * P], src[:, j, k * P:(k + 1) * P], ident[:, :])
                t_pe = pD.mark(ins)
                wait(act, t_pe, dst_free, t_fw)
                if scaled:
                    ins = act.activation(dst[:, k, 0:n * P], bank[bk][:, 0:n * P], ACT.Identity,
                                         scale=g2[:, 0, k:k + 1], bias=g2[:, 1, k:k + 1])
                else:
                    ins = act.copy(dst[:, k, 0:n * P], bank[bk][:, 0:n * P])
                bank_free[bk] = aD.mark(ins)
            return t_pe, bank_free[b0 + KC - 1]

        def d_turn(b):
            n, i = tiles_of(b), b % 2
            t_pe, D_["outT", b] = turn(rows[i], outT[i], n, 0, D_["norm", b], outT_free[i], True)
            wait(pool, t_pe, D_["norm", b], t_gb)
            for op, other in ((ALU.mult, ln2_gb[:, 0, :].unsqueeze(1).to_broadcast([P, n, D])),
                              (ALU.add, fb2_b.unsqueeze(1).to_broadcast([P, n, D])),
                              (ALU.add, x_in[i][:, 0:n, :])):
                t = c_pool.mark(pool.tensor_tensor(rows[i][:, 0:n, :], rows[i][:, 0:n, :], other, op))
                wait(pool, t)
            in_free[i] = D_["base", b] = t

        def d_ffn(b):
            n, i = tiles_of(b), b % 2
            wait(pe, D_["outT", b])
            for m in range(MC):
                bk = 2 + m % 2
                wait(pe, bank_free[bk])
                for k in range(KC):
                    ins = pe.matmul(bank[bk][:, 0:n * P], fw1[:, k, m * P:(m + 1) * P], outT[i][:, k, 0:n * P],
                                    start=(k == 0), stop=(k == KC - 1))
                t = pD.mark(ins)
                wait(act, t, hid_free[i])
                D_["hid", b] = bank_free[bk] = aD.mark(act.activation(
                    hidden[i][:, m, 0:n * P], bank[bk][:, 0:n * P], ACT.Gelu_apprx_tanh, bias=fb1[:, m:m + 1]))
            outT_free[i] = t

        def d_out(b):
            n, i = tiles_of(b), b % 2
            wait(pe, D_["hid", b])
            for j in range(n):
                bk = 4 + j % 2
                wait(pe, bank_free[bk])
                for m in range(MC):
                    ins = pe.matmul(bank[bk][:, 0:D], hidden[i][:, m, j * P:(j + 1) * P], fw2[:, m, :],
                                    start=(m == 0), stop=(m == MC - 1))
                t = pD.mark(ins)
                wait(dve, t, D_["base", b])
                D_["x1", b] = bank_free[bk] = vD.mark(dve.tensor_tensor(rows[i][:, j, :], rows[i][:, j, :], bank[bk][:, 0:D], ALU.add))
            hid_free[i] = t
            wait(sp, D_["x1", b])
            r = slice(4 * b * P, (4 * b + n) * P)
            x1_free[i] = c_x1[i].mark(sp.dma_start(x1_dram[r, :].rearrange("(t p) d -> p t d", p=P), rows[i][:, 0:n, :]), 16)

        def d_route(b):
            n, i = tiles_of(b), b % 2
            zs = [zrow[:, j, :] for j in range(n)]
            wait(dve, D_.get("z_turned"), D_.get("z_used"))
            t = norm_into(zs, [rows[i][:, j, :] for j in range(n)], D_["x1", b])
            D_["z_turned"], t_zT = turn(zrow, zT, n, 6, t, D_.get("zT_used"), False)
            D_["z_used"] = norm_into([win[:, 4 * b + j, 0:D] for j in range(n)], zs, t)
            wait(pe, t_zT, bank_free[5])
            for j in range(n):
                for k in range(KC):
                    ins = pe.matmul(bank[5][:, j * E:(j + 1) * E], zT[:, k, j * P:(j + 1) * P], wr_sb[:, k, :],
                                    start=(k == 0), stop=(k == KC - 1))
            t = D_["zT_used"] = pD.mark(ins)
            wait(dve, t)
            bank_free[5] = vD.mark(dve.tensor_tensor(
                logits[:, 4 * b:4 * b + n, :], bank[5][:, 0:n * E].rearrange("p (t e) -> p t e", e=E),
                br_b[:, :].unsqueeze(1).to_broadcast([P, n, E]), ALU.add))

        for i in range(NB + 2):
            if i < NB:
                d_load(i)
            if 1 <= i <= NB:
                d_ffn(i - 1)
            if i >= 2:
                d_route(i - 2)
            if i < NB:
                d_merge(i)
                d_turn(i)
            if 1 <= i <= NB:
                d_out(i - 1)
        layer_done = [(vD.sem, vD.value), (pD.sem, pD.value), (aD.sem, aD.value), (c_pool.sem, c_pool.value),
                      x1_free[0], x1_free[1]]

        SLOT = 2 * P
        NS = (2 * N + E * (SLOT - 1)) // SLOT
        NWB = 3
        w1_buf = [part(i * (KC * HID + MC * D), KC, HID) for i in range(NWB)]
        w2_buf = [part(i * (KC * HID + MC * D) + KC * HID, MC, D) for i in range(NWB)]
        o = 0
        ehid = [work_part(o + i * MC * SLOT, MC, SLOT) for i in range(2)]
        o += 2 * MC * SLOT
        xin = [work_part(o + i * 2 * D, 2, D) for i in range(2)]
        o += 4 * D
        xinT = [work_part(o + i * KC * SLOT, KC, SLOT) for i in range(2)]
        o += 2 * KC * SLOT
        yout = [work_part(o + i * 2 * D, 2, D) for i in range(2)]
        o += 4 * D
        b2_b = work_part(o, E, D)
        o += E * D
        assert o <= WORK
        epar = sb("epar", [P, E, 2 * KC + MC])
        par = [sb(f"par{i}", [P, 2 * KC + MC]) for i in range(2)]
        c_b2 = counter("expert_b2")
        c_we = [counter(f"expert_weights{i}") for i in range(NWB)]
        vE, aE, pE = counter("dve_experts"), counter("act_experts"), counter("pe_experts")
        c_disp = counter("dispatched")
        c_xin = [counter(f"slot_in{i}") for i in range(2)]
        c_y = [counter(f"slot_out{i}") for i in range(2)]

        for eng in (sp, dve, act, pe, pool):
            wait(eng, *layer_done)
        t_b2 = load(b2_b, b2.rearrange("e d -> (e d)").unsqueeze(0).to_broadcast([P, E * D]).rearrange("p (e d) -> p e d", d=D), c_b2)
        with nc.allow_non_contiguous_dma(reason="small vectors, one element per partition"):
            for e in range(E):
                load(epar[:, e, 0:KC], ln_g[e, :].rearrange("(k p) -> p k", p=P), c_b2)
                load(epar[:, e, KC:2 * KC], ln_b[e, :].rearrange("(k p) -> p k", p=P), c_b2)
                t_epar = load(epar[:, e, 2 * KC:], b1[e, :].rearrange("(m p) -> p m", p=P), c_b2)

        NL = NT * E
        rt = part(GATH, 6, NL)
        prob, sel = logits[:, :, :], [rt[:, i, :].rearrange("p (t e) -> p t e", e=E) for i in range(2)]
        both, top8 = [rt[:, i, :].rearrange("p (t e) -> p t e", e=E) for i in (2, 3)]
        idx8 = rt[:, 4, :].bitcast(U32).rearrange("p (t e) -> p t e", e=E)
        place = rt[:, 5, :].rearrange("p (t e) -> p t e", e=E)
        per_tok = sb("per_tok", [P, 6, NT])
        tmax, wsum, idxf = per_tok[:, 0, :], per_tok[:, 1, :], per_tok[:, 2, :]
        gate = [per_tok[:, 3 + i, :] for i in range(2)]
        valid = per_tok[:, 5, :]
        pos = sb("pos", [P, 2, NT], I32)
        per_exp = sb("per_exp", [P, 8, E])
        slot_e = sb("slot_e", [1, NS, E])
        slot_i = sb("slot_i", [1, NS], I32)
        iota_s = sb("iota_s", [P, NS])
        tri = sb("tri", [P, P])

        def v(ins, *before):
            t = vE.mark(ins)
            wait(dve, t)
            return t

        t = c_pool.mark(pool.memset(tri[:, :], 1.0))
        t2 = c_pool.mark(pool.memset(valid, 1.0))
        wait(pool, t, t2)
        c_pool.mark(pool.affine_select(out=tri[:, :], in_=tri[:, :], compare_op=ALU.is_gt, fill=0.0,
                                       base=0, pattern=[[1, P]], channel_multiplier=-1))
        c_pool.mark(pool.affine_select(out=valid[:, NT - 1:NT], in_=valid[:, NT - 1:NT], compare_op=ALU.is_gt, fill=0.0,
                                       base=last_rows, pattern=[[0, 1]], channel_multiplier=-1))
        t_is = c_pool.mark(pool.iota(iota_s[:, :].bitcast(I32), pattern=[[1, NS]], base=0, channel_multiplier=0))
        wait(dve, t_is)
        t = vE.mark(dve.tensor_copy(slot_e[0:1, :, 0], iota_s[0:1, :].bitcast(I32)))
        wait(dve, t)
        t = vE.mark(dve.tensor_copy(iota_s[0:1, :], slot_e[0:1, :, 0]))
        wait(dve, t)
        v(dve.tensor_reduce(tmax, prob, AX.X, ALU.max))
        t = v(dve.tensor_tensor(prob, prob, tmax.unsqueeze(2).to_broadcast([P, NT, E]), ALU.subtract))
        wait(act, t)
        t = aE.mark(act.activation(prob, prob, ACT.Exp))
        wait(dve, t)
        v(dve.tensor_reduce(wsum, prob, AX.X, ALU.add))
        v(dve.reciprocal(wsum, wsum))
        t = v(dve.tensor_tensor(prob, prob, wsum.unsqueeze(2).to_broadcast([P, NT, E]), ALU.mult))
        for w in range(NT):
            t = vE.mark(dve.max(top8[:, w, :], prob[:, w, :]))
        wait(dve, t)
        for w in range(NT):
            t = vE.mark(dve.max_index(idx8[:, w, :], top8[:, w, :], prob[:, w, :]))
        wait(dve, t)
        v(dve.tensor_tensor(wsum, top8[:, :, 0], top8[:, :, 1], ALU.add))
        v(dve.reciprocal(wsum, wsum))
        for s in range(2):
            v(dve.tensor_tensor(gate[s], top8[:, :, s], wsum, ALU.mult))
        for s in range(2):
            v(dve.tensor_copy(idxf, idx8[:, :, s]))
            v(dve.tensor_tensor(sel[s], iota_row[:, 0:E].unsqueeze(1).to_broadcast([P, NT, E]),
                                idxf.unsqueeze(2).to_broadcast([P, NT, E]), ALU.is_equal))
            v(dve.tensor_tensor(sel[s], sel[s], valid.unsqueeze(2).to_broadcast([P, NT, E]), ALU.mult)) if s or True else None
        t = v(dve.tensor_tensor(both, sel[0], sel[1], ALU.add))
        wait(pe, t, (c_pool.sem, c_pool.value))
        pE.mark(pe.matmul(bank[0][:, 0:NL], tri[:, :], rt[:, 2, :], start=True, stop=True))
        t = pE.mark(pe.matmul(bank[1][:, 0:NL], ones[:, :], rt[:, 2, :], start=True, stop=True))
        wait(dve, t)
        v(dve.tensor_copy(both, bank[1][:, 0:NL].rearrange("p (t e) -> p t e", e=E)))
        for e in range(E):
            t = vE.mark(dve.tensor_tensor_scan(place[:, :, e], both[:, :, e], ones[:, 0:NT], 0.0, ALU.add, ALU.mult))
        wait(dve, t)
        total, slots, upto, start = [per_exp[:, i, :] for i in range(4)]
        total_i = per_exp[:, 4, :].bitcast(I32)
        v(dve.tensor_copy(total, place[:, NT - 1, :]))
        v(dve.tensor_scalar(total_i, total, float(SLOT - 1), None, ALU.add))
        v(dve.tensor_single_scalar(total_i, total_i, 8, ALU.arith_shift_right))
        v(dve.tensor_copy(slots, total_i))
        v(dve.tensor_tensor_scan(upto, slots, ones[:, 0:E], 0.0, ALU.add, ALU.mult))
        v(dve.tensor_tensor(start, upto, slots, ALU.subtract))
        v(dve.tensor_scalar(start, start, float(SLOT), None, ALU.mult))
        v(dve.tensor_tensor(place, place, both, ALU.subtract))
        v(dve.tensor_tensor(place, place, bank[0][:, 0:NL].rearrange("p (t e) -> p t e", e=E), ALU.add))
        v(dve.tensor_tensor(place, place, start.unsqueeze(1).to_broadcast([P, NT, E]), ALU.add))
        for s in range(2):
            v(dve.tensor_tensor(sel[s], sel[s], place, ALU.mult))
            v(dve.tensor_reduce(idxf, sel[s], AX.X, ALU.add))
            t_pos = v(dve.tensor_copy(pos[:, s, :], idxf))
        v(dve.tensor_tensor(slot_e[:, :, :], upto[0:1, :].unsqueeze(1).to_broadcast([1, NS, E]),
                            iota_s[0:1, :].unsqueeze(2).to_broadcast([1, NS, E]), ALU.is_le))
        v(dve.tensor_reduce(iota_s[0:1, :], slot_e[:, :, :], AX.X, ALU.add))
        v(dve.tensor_scalar(iota_s[0:1, :], iota_s[0:1, :], float(E - 1), None, ALU.min))
        t_slot = v(dve.tensor_copy(slot_i[:, :], iota_s[0:1, :]))

        wait(pool, t_pos, t_zero)
        for w in range(NT):
            r = P if w < NT - 1 else last_rows
            for s in range(2):
                t_disp = c_disp.mark(pool.indirect_dma_start(
                    slot_rows, bass.IndirectOffsetOnAxis(ap=pos[0:r, s, w:w + 1], axis=0),
                    win[0:r, w, 0:D], None), 16)
        wait(sp, t_disp, t_slot)

        xin_free, xinT_free, ehid_free, y_free, par_free = [None] * 2, [None] * 2, [None] * 2, [None] * 2, [None] * 2
        bank_free = [None] * 8
        E_ = {}
        wait(dve, t_b2, t_epar)
        w_free = [None] * NWB
        W1_v = W1.rearrange("e (k p) h -> e p k h", p=P)
        W2_v = W2.rearrange("e (m p) d -> e p m d", p=P)

        def e_in(j):
            i = j % 2
            wait(sp, xin_free[i])
            e, wb = sp.value_load(slot_i[0:1, j:j + 1], min_val=0, max_val=E - 1), j % NWB
            wait(sp, w_free[wb])
            load(w1_buf[wb], W1_v[e], c_we[wb])
            E_["w", j] = load(w2_buf[wb], W2_v[e], c_we[wb])
            E_["in", j] = c_xin[i].mark(sp.dma_start(xin[i], slot_rows[j * SLOT:(j + 1) * SLOT, :].rearrange("(t p) d -> p t d", p=P)), 16)

        def e_turn(j):
            i = j % 2
            e = E_["dve_e", j] = dve.value_load(slot_i[0:1, j:j + 1], min_val=0, max_val=E - 1)
            wait(dve, par_free[i])
            t_par = vE.mark(dve.tensor_copy(par[i][:, :], epar[:, e, :]))
            wait(pe, E_["in", j], bank_free[0])
            for k in range(KC):
                for t in range(2):
                    ins = pe.transpose(bank[0][:, k * SLOT + t * P:k * SLOT + (t + 1) * P], xin[i][:, t, k * P:(k + 1) * P], ident[:, :])
            xin_free[i] = t = pE.mark(ins)
            wait(act, t, t_par, xinT_free[i])
            for k in range(KC):
                t = aE.mark(act.activation(xinT[i][:, k, :], bank[0][:, k * SLOT:(k + 1) * SLOT], ACT.Identity,
                                           scale=par[i][:, k:k + 1], bias=par[i][:, KC + k:KC + k + 1]))
            E_["inT", j] = bank_free[0] = t

        def e_first(j):
            i = j % 2
            w1 = w1_buf[j % NWB]
            wait(pe, E_["inT", j], E_["w", j])
            for m in range(MC):
                bk = 1 + m % 4
                wait(pe, bank_free[bk])
                for k in range(KC):
                    ins = pe.matmul(bank[bk][:, 0:SLOT], w1[:, k, m * P:(m + 1) * P], xinT[i][:, k, :],
                                    start=(k == 0), stop=(k == KC - 1))
                t = pE.mark(ins)
                wait(act, t, ehid_free[i])
                E_["hid", j] = bank_free[bk] = aE.mark(act.activation(
                    ehid[i][:, m, :], bank[bk][:, 0:SLOT], ACT.Gelu, bias=par[i][:, 2 * KC + m:2 * KC + m + 1]))
            par_free[i] = E_["hid", j]
            xinT_free[i] = t

        def e_second(j):
            i = j % 2
            w2 = w2_buf[j % NWB]
            wait(pe, E_["hid", j])
            wait(dve, y_free[i])
            for t in range(2):
                bk = 5 + t
                wait(pe, bank_free[bk])
                for m in range(MC):
                    ins = pe.matmul(bank[bk][:, 0:D], ehid[i][:, m, t * P:(t + 1) * P], w2[:, m, :],
                                    start=(m == 0), stop=(m == MC - 1))
                tt = pE.mark(ins)
                wait(dve, tt)
                ty = bank_free[bk] = vE.mark(dve.tensor_tensor(yout[i][:, t, :], bank[bk][:, 0:D], b2_b[:, E_["dve_e", j], :], ALU.add))
            ehid_free[i] = w_free[j % NWB] = tt
            wait(sp, ty)
            y_free[i] = c_y[i].mark(sp.dma_start(slot_out[j * SLOT:(j + 1) * SLOT, :].rearrange("(t p) d -> p t d", p=P), yout[i]), 16)

        for j in range(NS + 2):
            if j < NS:
                e_in(j)
            if 1 <= j <= NS:
                e_turn(j - 1)
                e_first(j - 1)
            if j >= 2:
                e_second(j - 2)

        CR = 4
        experts_done = [(pE.sem, pE.value), y_free[0], y_free[1]]
        ys = [[part((2 * i + s) * D, D) for s in range(2)] for i in range(CR)]
        xo = [part(2 * CR * D + i * D, D) for i in range(CR)]
        c_yg = [counter(f"y_gathered{i}") for i in range(CR)]
        c_xo = [counter(f"x1_loaded{i}") for i in range(CR)]
        c_out = [counter(f"out_written{i}") for i in range(CR)]
        out_done, ys_free = [None] * CR, [None] * CR
        wait(pool, *experts_done)
        wait(sp, *experts_done)
        for w in range(NT):
            i, r = w % CR, (P if w < NT - 1 else last_rows)
            wait(pool, ys_free[i])
            for s in range(2):
                ty = c_yg[i].mark(pool.indirect_dma_start(ys[i][s][0:r, :], None, slot_out,
                                                          bass.IndirectOffsetOnAxis(ap=pos[0:r, s, w:w + 1], axis=0)), 16)
            wait(sp, out_done[i])
            tx = c_xo[i].mark(sp.dma_start(xo[i][0:r, :], x1_dram[w * P:w * P + r, :]), 16)
            wait(dve, ty, tx)
            t = vE.mark(dve.scalar_tensor_tensor(xo[i][0:r, :], ys[i][0][0:r, :], gate[0][0:r, w:w + 1], xo[i][0:r, :], ALU.mult, ALU.add))
            wait(dve, t)
            t = ys_free[i] = vE.mark(dve.scalar_tensor_tensor(xo[i][0:r, :], ys[i][1][0:r, :], gate[1][0:r, w:w + 1], xo[i][0:r, :], ALU.mult, ALU.add))
            wait(act, t)
            out_done[i] = c_out[i].mark(act.dma_start(out[w * P:w * P + r, :], xo[i][0:r, :]), 16)
        wait(sp, *out_done)


DEBUG = 0
DEBUG_GROUPS = 0


_INS = ["x", "src", "dst", "L0_gnn_W", "L0_gnn_att_src", "L0_gnn_att_dst", "L0_gnn_bias", "L0_gnn_W_res",
        "L0_gnn_ln1_g", "L0_gnn_ln1_b", "L0_gnn_ln2_g", "L0_gnn_ln2_b", "L0_gnn_ffn_w1", "L0_gnn_ffn_b1",
        "L0_gnn_ffn_w2", "L0_gnn_ffn_b2", "L0_ffn_Wr", "L0_ffn_br", "L0_ffn_ln_g", "L0_ffn_ln_b", "L0_ffn_W1",
        "L0_ffn_b1", "L0_ffn_W2", "L0_ffn_b2"]


def kernel(**inputs):
    import numpy as np
    import concourse.bacc as bacc
    from concourse.bass_utils import run_bass_kernel_spmd

    nc = bacc.Bacc("TRN2", target_bir_lowering=False, num_devices=1)
    arrays, args = {}, []
    for name in _INS:
        a = np.ascontiguousarray(inputs[name])
        if name in ("src", "dst"):
            a = np.pad(a, (0, -len(a) % 256), constant_values=(1 << 20) if name == "dst" else 0)
        arrays[f"in_{name}"] = a
        args.append(nc.dram_tensor(f"in_{name}", a.shape, mybir.dt.from_np(a.dtype), kind="ExternalInput").ap())
    shape = inputs["x"].shape
    args.append(nc.dram_tensor("out", shape, F32, kind="ExternalOutput").ap())
    build(nc, *args)
    result = run_bass_kernel_spmd(nc, [arrays], core_ids=[0])
    return result.results[0]["out"]
```

```python
from contextlib import ExitStack

import concourse.bass as bass
from concourse import mybir

F32 = mybir.dt.float32
I32 = mybir.dt.int32
BF16 = mybir.dt.bfloat16
U32 = mybir.dt.uint32
ALU = mybir.AluOpType
ACT = mybir.ActivationFunctionType
AX = mybir.AxisListType

P = 128
BIG = 1.0e30
EPS = 1e-5
SLOPE = 0.2


class Counter:

    def __init__(self, nc, ctx, name):
        self.sem, self.value = ctx.enter_context(nc.semaphore(name)), 0

    def mark(self, instruction, by=1):
        instruction.then_inc(self.sem, by)
        self.value += by
        return self.sem, self.value


def wait(engine, *tokens):
    for token in tokens:
        if token is not None:
            engine.wait_ge(*token)


def build(nc, x, src, dst, gW, att_src, att_dst, g_bias, gW_res, ln1_g, ln1_b, ln2_g, ln2_b,
          f_w1, f_b1, f_w2, f_b2, Wr, br, ln_g, ln_b, W1, b1, W2, b2, out):
    N, D = x.shape
    HEADS, HD = att_src.shape
    HID = f_w1.shape[1]
    E = Wr.shape[1]
    KC = D // P
    MC = HID // P
    NT = -(-N // P)
    NB = -(-NT // 4)
    EB = 256
    NEB = dst.shape[0] // EB
    WIN = NT + 1
    GS = 8
    NG = -(-(NEB + NT - 1) // GS)
    NSTEP = NG * GS
    NK = -(-NSTEP // P)
    GT = 2 * GS
    HC = HD + 1
    AGG = HEADS * HC
    ROW = AGG + HEADS
    WROW = ROW + HEADS
    last_rows = N - (NT - 1) * P
    ARENA = 43520
    WORK = 10240

    ctx = ExitStack()
    with ctx:
        def sb(name, shape, dt=F32):
            return ctx.enter_context(nc.sbuf_tensor(name, shape, dt))

        def counter(name):
            return Counter(nc, ctx, name)

        def dram(name, shape, dt=F32):
            return nc.dram_tensor(name, shape, dt, kind="Internal").ap()

        pe, dve, act, pool, sp = nc.tensor, nc.vector, nc.scalar, nc.gpsimd, nc.sync

        node_table = dram("node_table", [NT * P, ROW])
        residual = dram("residual", [NT * P, D])
        step_new = dram("step_new", [NK * P, EB])
        step_last = dram("step_last", [NK * P, EB])
        x1_dram = dram("x1", [NT * P, D])
        slots_total = (2 * N + E * 255) // 256 * 256
        slot_rows = dram("slot_rows", [slots_total, D])
        slot_out = dram("slot_out", [slots_total, D])
        step_win = dram("step_win", [NK * P, 1], I32)

        c_ld = counter("const_loads")
        c_pool = counter("pool_done")
        vA, aA, pA = counter("dve_nodes"), counter("act_nodes"), counter("pe_nodes")
        vB, pB = counter("dve_prep"), counter("pe_prep")
        vC, aC, pC = counter("dve_edges"), counter("act_edges"), counter("pe_edges")
        c_x = [counter(f"x_loaded{i}") for i in range(3)]
        c_tab, c_res = counter("table_written"), counter("residual_written")
        c_prep = counter("prep_dma")

        bank = [ctx.enter_context(nc.psum_tensor(f"bank{i}", [P, 512], F32)) for i in range(8)]

        ident = sb("ident", [P, P])
        iota_row = sb("iota_row", [P, P])
        iota16 = sb("iota16", [P, P], BF16)
        ident16 = sb("ident16", [P, P], BF16)
        ones = sb("ones", [P, P])
        zero = sb("zero", [P, D])
        neg_half = sb("neg_half", [P, 8])
        arena = sb("arena", [P, ARENA])

        def part(offset, *shape):
            size = 1
            for s in shape:
                size *= s
            flat = arena[:, offset:offset + size]
            if len(shape) == 1:
                return flat
            names = "abcd"[:len(shape)]
            return flat.rearrange(f"p ({' '.join(names)}) -> p {' '.join(names)}",
                                  **{n: s for n, s in zip(names, shape)})

        win = part(0, WIN, WROW)
        GATH = WIN * WROW
        NGB = 4
        gath = [part(GATH + i * GT * ROW, GT, ROW) for i in range(NGB)]
        OH0 = GATH + NGB * GT * ROW
        onehot = [part(OH0 + i * GT * P, GT, P) for i in range(2)]
        OT0 = OH0 + 2 * GT * P

        def half_part(offset):
            return part(offset, GT * P // 2).bitcast(BF16).rearrange("p (t n) -> p t n", n=P)

        onehot16 = [half_part(OT0 + i * GT * P // 2) for i in range(2)]
        onehot_t = [half_part(OT0 + (2 + i) * GT * P // 2) for i in range(2)]
        assert OT0 + 2 * GT * P <= ARENA, OT0 + 2 * GT * P

        work = arena[:, ARENA - WORK:ARENA]

        def work_part(offset, *shape):
            size = 1
            for d in shape:
                size *= d
            names = "abcd"[:len(shape)]
            return work[:, offset:offset + size].rearrange(
                f"p ({' '.join(names)}) -> p {' '.join(names)}", **{n: d for n, d in zip(names, shape)})

        xs = [part(GATH + i * 4 * D, 4, D) for i in range(3)]
        o = GATH + 12 * D
        xnT = [part(o + i * KC * 512, KC, 512) for i in range(2)]
        o += 2 * KC * 512
        res_st = [part(o + i * 4 * D, 4, D) for i in range(2)]
        o += 8 * D
        Wc = part(o, KC, D + 2 * HEADS)
        o += KC * (D + 2 * HEADS)
        Wres = part(o, KC, D)
        o += KC * D
        att = part(o, 2, D)
        att_tmp = part(o + 2 * D, D)
        bias_b = part(o + 3 * D, D)

        src_col = sb("src_col", [P, NK * P, 2], I32)
        dst_col = sb("dst_col", [P, NK * P, 2], BF16)
        last_col = sb("last_col", [P, NK * P, 2])
        win_row = sb("win_row", [1, NSTEP], I32)
        win_delta = sb("win_delta", [1, NG, GS], I32)
        win_word = sb("win_word", [1, NG], I32)

        t_c0 = c_pool.mark(pool.memset(ident[:, :], 0.0))
        c_pool.mark(pool.memset(ones[:, :], 1.0))
        c_pool.mark(pool.memset(neg_half[:, :], -0.5))
        wait(pool, t_c0)
        c_pool.mark(pool.affine_select(out=ident[:, :], in_=ident[:, :], compare_op=ALU.not_equal,
                                       fill=1.0, base=0, pattern=[[-1, P]], channel_multiplier=1))
        iota_i = part(OT0 + 2 * GT * P - P, P).bitcast(I32)
        t_i = c_pool.mark(pool.iota(iota_i, pattern=[[1, P]], base=0, channel_multiplier=0))
        wait(dve, t_i)
        vB.mark(dve.tensor_copy(iota_row[:, :], iota_i))
        vB.mark(dve.tensor_copy(iota16[:, :], iota_i))
        wait(dve, (c_pool.sem, c_pool.value))
        t_const = vB.mark(dve.tensor_copy(ident16[:, :], ident[:, :]))
        ident_ready = (c_pool.sem, c_pool.value)

        def load(dst_ap, src_ap, c=None):
            return (c or c_ld).mark(sp.dma_start(dst_ap, src_ap), 16)

        g1 = sb("g1", [P, 2, KC])
        for k in range(KC):
            load(Wc[:, k, 0:D], gW[k * P:(k + 1) * P, :])
            load(Wres[:, k, :], gW_res[k * P:(k + 1) * P, :])
        with nc.allow_non_contiguous_dma(reason="a few small vectors, one element per partition"):
            load(g1[:, 0, :], ln1_g.rearrange("(k p) -> p k", p=P))
            load(g1[:, 1, :], ln1_b.rearrange("(k p) -> p k", p=P))
        load(att[:, 0, :], att_src.rearrange("h d -> (h d)").unsqueeze(0).to_broadcast([P, D]))
        load(att[:, 1, :], att_dst.rearrange("h d -> (h d)").unsqueeze(0).to_broadcast([P, D]))
        weights_loaded = load(bias_b, g_bias.unsqueeze(0).to_broadcast([P, D]))

        wait(dve, weights_loaded)
        for k in range(KC):
            for s in range(2):
                t = vA.mark(dve.tensor_tensor(att_tmp, Wc[:, k, 0:D], att[:, s, :], ALU.mult))
                wait(dve, t)
                t_att = vA.mark(dve.tensor_reduce(Wc[:, k, D + s * HEADS:D + (s + 1) * HEADS],
                                                  att_tmp.rearrange("p (h d) -> p h d", d=HD),
                                                  AX.X, ALU.add))
                wait(dve, t_att)
        t_wc = t_att
        t_ones = vA.mark(dve.memset(win[:, :, 0:AGG].rearrange("p w (h c) -> p w h c", c=HC)[:, :, :, HD:HC], 1.0))
        wait(dve, t_ones)
        t_padw = vA.mark(dve.memset(win[:, NT, :], 0.0))
        t_xpad = None
        stats = sb("stats", [P, 4, 6])
        mv = sb("mv", [P, 4, 2])
        rstd = sb("rstd", [P, 4])

        def norm_steps(dsts, srcs, c, ready, done):
            n = len(srcs)
            wait(dve, ready)
            for j, xt in enumerate(srcs):
                t = c.mark(dve.bn_stats(stats[:, j, :], xt))
            wait(dve, t)
            for j in range(n):
                t = c.mark(dve.bn_aggr(mv[:, j, :], stats[:, j, :]))
            wait(dve, t)
            t = c.mark(dve.tensor_scalar(mv[:, 0:n, 1], mv[:, 0:n, 1], EPS, None, ALU.add))
            wait(pool, t)
            t_pow = c_pool.mark(pool.tensor_tensor(rstd[:, 0:n], mv[:, 0:n, 1], neg_half[:, 0:n], ALU.pow))
            yield
            wait(dve, t_pow)
            for j, (d, xt) in enumerate(zip(dsts, srcs)):
                t = c.mark(dve.tensor_scalar(d, xt, mv[:, j, 0:1], rstd[:, j:j + 1], ALU.subtract, ALU.mult))
            done.append(t)

        def tiles_of(b):
            return min(4, NT - 4 * b)

        x_free, xnT_free, res_free = [None] * 3, [None] * 2, [None] * 2
        loadedA, normedA = {}, {}

        def a_load(b):
            n, buf = tiles_of(b), xs[b % 3]
            wait(sp, x_free[b % 3])
            if b == NB - 1:
                wait(dve, x_free[b % 3])
                t = vA.mark(dve.memset(buf[:, n - 1, :], 0.0))
                wait(sp, t)
                if n > 1:
                    c_x[b % 3].mark(sp.dma_start(buf[:, 0:n - 1, :], x[4 * b * P:(NT - 1) * P, :].rearrange("(t p) d -> p t d", p=P)), 16)
                loadedA[b] = c_x[b % 3].mark(sp.dma_start(buf[0:last_rows, n - 1, :], x[(NT - 1) * P:N, :]), 16)
            else:
                loadedA[b] = c_x[b % 3].mark(sp.dma_start(buf[:, 0:n, :], x[4 * b * P:(4 * b + n) * P, :].rearrange("(t p) d -> p t d", p=P)), 16)

        def a_norm(b):
            tiles, done = [xs[b % 3][:, j, :] for j in range(tiles_of(b))], [loadedA[b]]
            yield from norm_steps(tiles, tiles, vA, done[-1], done)
            yield from norm_steps(tiles, tiles, vA, done[-1], done)
            normedA[b] = done[-1]

        bank_free = [None] * 8
        xnT_ready = {}

        def a_turn(b):
            n, buf = tiles_of(b), xs[b % 3]
            wait(pe, normedA[b], ident_ready)
            for k in range(KC):
                bk = k
                wait(pe, bank_free[bk])
                for j in range(n):
                    ins = pe.transpose(bank[bk][:, j * P:(j + 1) * P], buf[:, j, k * P:(k + 1) * P], ident[:, :])
                t = pA.mark(ins)
                wait(act, t, weights_loaded, xnT_free[b % 2])
                xnT_ready[b] = bank_free[bk] = aA.mark(act.activation(
                    xnT[b % 2][:, k, 0:n * P], bank[bk][:, 0:n * P], ACT.Identity,
                    scale=g1[:, 0, k:k + 1], bias=g1[:, 1, k:k + 1]))
            x_free[b % 3] = t

        def a_project(b, between):
            n = tiles_of(b)
            wait(pe, xnT_ready[b], t_wc)
            wait(act, t_ones)
            for j in range(n):
                w = 4 * b + j
                bh, br_ = 2 + (w % 3), 5 + (w % 3)
                wait(pe, bank_free[bh])
                for k in range(KC):
                    ins = pe.matmul(bank[bh][:, 0:D + 2 * HEADS], xnT[b % 2][:, k, j * P:(j + 1) * P],
                                    Wc[:, k, :], start=(k == 0), stop=(k == KC - 1))
                t_h = pA.mark(ins)
                wait(pe, bank_free[br_])
                for k in range(KC):
                    ins = pe.matmul(bank[br_][:, 0:D], xnT[b % 2][:, k, j * P:(j + 1) * P],
                                    Wres[:, k, :], start=(k == 0), stop=(k == KC - 1))
                t_r = pA.mark(ins)
                wait(act, t_h)
                aA.mark(act.copy(win[:, w, 0:AGG].rearrange("p (h c) -> p h c", c=HC)[:, :, 0:HD],
                                 bank[bh][:, 0:D].rearrange("p (h d) -> p h d", d=HD)))
                t_w = bank_free[bh] = aA.mark(act.copy(win[:, w, AGG:WROW], bank[bh][:, D:D + 2 * HEADS]))
                wait(dve, t_r, res_free[b % 2] if j == 0 else None)
                t_rs = bank_free[br_] = vA.mark(dve.tensor_tensor(res_st[b % 2][:, j, :], bank[br_][:, 0:D], bias_b, ALU.add))
                next(between, None)
            xnT_free[b % 2] = t_r
            wait(sp, t_w, t_ones)
            rows = slice(4 * b * P, (4 * b + n) * P)
            c_tab.mark(sp.dma_start(node_table[rows, :].rearrange("(t p) c -> p t c", p=P),
                                    win[:, 4 * b:4 * b + n, 0:ROW]), 16)
            wait(sp, t_rs)
            c_r = c_resb[b % 2]
            res_free[b % 2] = c_r.mark(sp.dma_start(residual[rows, :].rearrange("(t p) c -> p t c", p=P),
                                                    res_st[b % 2][:, 0:n, :]), 16)

        c_resb = [counter(f"residual_written{i}") for i in range(2)]

        dst_rows = dst.rearrange("(b e) -> b e", e=EB)
        src_rows = src.rearrange("(b e) -> b e", e=EB)
        PB0 = OH0
        first = part(PB0, NEB).bitcast(I32)
        first_w = part(PB0 + 400, NEB)
        iota_b = part(PB0 + 800, 400).bitcast(I32)
        le = part(PB0 + 1200, NEB)
        count = sb("count", [P, 4 * 5])
        kcol = sb("kcol", [P, NK], I32)
        tk_i = sb("tk_i", [P, NK], I32)
        wk_i = sb("wk_i", [P, NK], I32)
        rows_i = part(PB0 + 1600, NK, EB).bitcast(I32)
        rows_s = part(PB0 + 1600 + NK * EB, NK, EB)
        rows_d = part(PB0 + 1600 + 2 * NK * EB, NK, EB + 2)
        rows_n = part(PB0 + 1600 + 3 * NK * EB + 16, NK, EB)
        assert PB0 + 1600 + 4 * NK * EB + 16 <= OT0 + 2 * GT * P
        c_rows = counter("step_rows")
        c_scr = counter("step_scratch")

        def b_prep():
            with nc.allow_non_contiguous_dma(reason="one element per edge block"):
                t_f = load(first[0:1, :], dst_rows[:, 0:1].rearrange("b o -> o b"), c_prep)
            t_i1 = c_pool.mark(pool.iota(iota_b[0:1, 0:NEB], pattern=[[1, NEB]], base=0, channel_multiplier=0))
            t_i2 = c_pool.mark(pool.iota(kcol[:, :], pattern=[[P, NK]], base=0, channel_multiplier=1))
            wait(dve, t_f, t_i1, t_i2)
            t = vB.mark(dve.tensor_single_scalar(first[0:1, :], first[0:1, :], 7, ALU.arith_shift_right))
            wait(dve, t)
            t = vB.mark(dve.tensor_scalar(first_w[0:1, :], first[0:1, :], float(NT - 1), None, ALU.min))
            wait(dve, t)
            t = vB.mark(dve.memset(first_w[0:1, 0:1], 0.0))
            wait(dve, t)
            t = vB.mark(dve.tensor_tensor(first_w[0:1, :], first_w[0:1, :], iota_b[0:1, 0:NEB], ALU.add))
            wait(pe, t, ident_ready, bank_free[7])
            t = pB.mark(pe.matmul(bank[7][:, 0:NEB], ones[0:1, :], first_w[0:1, :], start=True, stop=True))
            wait(dve, t)
            yield
            kf, tf, wf = count[:, 0:NK], count[:, NK:2 * NK], count[:, 2 * NK:3 * NK]
            t = vB.mark(dve.tensor_copy(kf, kcol[:, :]))
            wait(dve, t)
            for c in range(NK):
                t = vB.mark(dve.tensor_scalar(le, bank[7][:, 0:NEB], kf[:, c:c + 1], None, ALU.is_le))
                wait(dve, t)
                t = vB.mark(dve.tensor_reduce(tf[:, c:c + 1], le, AX.X, ALU.add))
                wait(dve, t)
            bank_free[7] = t
            yield
            t = vB.mark(dve.tensor_scalar(tf, tf, -1.0, None, ALU.add))
            wait(dve, t)
            t_tk = vB.mark(dve.tensor_copy(tk_i[:, :], tf))
            t = vB.mark(dve.tensor_tensor(wf, kf, tf, ALU.subtract))
            wait(dve, t)
            t_wk = vB.mark(dve.tensor_copy(wk_i[:, :], wf))
            t_w128 = vB.mark(dve.tensor_scalar(kf, wf, float(P), None, ALU.mult))
            wait(sp, t_wk)
            with nc.allow_non_contiguous_dma(reason="one element per step"):
                t = load(step_win.rearrange("(c p) o -> p (c o)", p=P), wk_i[:, :], c_prep)
                wait(sp, t)
                t_win = load(win_row[:, :], step_win[0:NSTEP, :].rearrange("k o -> o k"), c_prep)
            yield
            wr = win_row[:, :].rearrange("o (g k) -> o g k", k=GS)
            wait(dve, t_win)
            t = vB.mark(dve.tensor_tensor(win_delta[:, :, 1:GS], wr[:, :, 1:GS], wr[:, :, 0:1].to_broadcast([1, NG, GS - 1]), ALU.subtract))
            t = vB.mark(dve.tensor_copy(win_word[:, :], wr[:, :, 0]))
            wait(dve, t)
            for k in range(1, GS):
                t = vB.mark(dve.tensor_single_scalar(win_delta[:, :, k], win_delta[:, :, k], 3 + 3 * k, ALU.logical_shift_left))
                wait(dve, t)
                t = vB.mark(dve.tensor_tensor(win_word[:, :], win_word[:, :], win_delta[:, :, k], ALU.bitwise_or))
                wait(dve, t)
            t_win = t
            yield
            wait(pool, t_tk)
            for c in range(NK):
                c_rows.mark(pool.indirect_dma_start(rows_i[:, c, :], None, dst_rows, bass.IndirectOffsetOnAxis(ap=tk_i[:, c:c + 1], axis=0)), 16)
                t = c_rows.mark(pool.indirect_dma_start(rows_s[:, c, :].bitcast(I32), None, src_rows, bass.IndirectOffsetOnAxis(ap=tk_i[:, c:c + 1], axis=0)), 16)
            yield
            wait(dve, t, t_w128)
            t = vB.mark(dve.memset(rows_d[:, :, :], -1.0e6))
            wait(dve, t)
            for c in range(NK):
                t = vB.mark(dve.tensor_scalar(rows_d[:, c, 1:EB + 1], rows_i[:, c, :], kf[:, c:c + 1], None, ALU.subtract))
            wait(dve, t)
            src_f = rows_i[:, :, :].bitcast(F32)
            t_sf = vB.mark(dve.tensor_copy(src_f, rows_s.bitcast(I32)))
            for c in range(NK):
                t = vB.mark(dve.tensor_tensor(rows_n[:, c, :], rows_d[:, c, 1:EB + 1], rows_d[:, c, 0:EB], ALU.not_equal))
            wait(dve, t)
            t_new = vB.mark(dve.tensor_scalar(rows_n, rows_n, -BIG, None, ALU.mult))
            wait(sp, t_new)
            t = load(step_new.rearrange("(c p) e -> p c e", p=P), rows_n, c_scr)
            yield
            def columns(source, target, ready):
                for i in range(NK * 2):
                    c, j = i // 2, i % 2
                    bk = i % 2
                    wait(pe, ready, bank_free[bk])
                    tt = pB.mark(pe.transpose(bank[bk][:, 0:P], source(c, j), ident[:, :]))
                    wait(dve, tt)
                    bank_free[bk] = vB.mark(dve.tensor_copy(target[:, c * P:(c + 1) * P, j], bank[bk][:, 0:P]))
                return bank_free[bk]

            t_s = columns(lambda c, j: src_f[:, c, j * P:(j + 1) * P], src_col, t_sf)
            yield
            t_d = columns(lambda c, j: rows_d[:, c, 1 + j * P:1 + (j + 1) * P], dst_col, t_sf)
            yield
            wait(dve, t)
            for c in range(NK):
                t_l = vB.mark(dve.tensor_tensor(rows_n[:, c, :], rows_d[:, c, 1:EB + 1], rows_d[:, c, 2:EB + 2], ALU.not_equal))
            wait(sp, t_l)
            t_scr = load(step_last.rearrange("(c p) e -> p c e", p=P), rows_n, c_scr)
            yield
            t_lc = columns(lambda c, j: rows_n[:, c, j * P:(j + 1) * P], last_col, t_l)
            prepared.update(win=t_win, scratch=t_scr, src=t_s, cols=t_lc)

        prepared, prep = {}, b_prep()
        for i in range(NB + 2):
            if i < NB:
                a_load(i)
            norm = a_norm(i - 1) if 1 <= i <= NB else iter(())
            next(norm, None)
            if i >= 2:
                a_project(i - 2, norm)
            for _ in norm:
                pass
            if 1 <= i <= NB:
                a_turn(i - 1)
            next(prep, None)
        for _ in prep:
            pass
        t_win, t_scr, t_srccol, t_cols = (prepared[k] for k in ("win", "scratch", "src", "cols"))
        table_written = (c_tab.sem, c_tab.value)
        node_phase_done = [(vA.sem, vA.value), (pA.sem, pA.value), (aA.sem, aA.value), res_free[0], res_free[1]]

        seg_new = [sb(f"seg_new{i}", [HEADS * GS, EB]) for i in range(2)]
        seg_last = [sb(f"seg_last{i}", [HEADS * GS, EB]) for i in range(2)]
        seg_max = sb("seg_max", [HEADS * GS, EB])
        asrc = sb("asrc", [P, 2, GS, HEADS])
        cand = sb("cand", [P, 3, 2, GS, HEADS + 1], BF16)
        cand_rest = sb("cand_rest", [P, 2, GS, HEADS])
        old = sb("old", [P, GS, 2 * HEADS])
        newm = sb("newm", [P, GS, HEADS])
        nodeval = sb("nodeval", [P, GS, 2 * HEADS])
        parts = sb("parts", [P, 3, GS, 2 * HEADS], BF16)
        rest = sb("rest", [P, GS, 2 * HEADS])
        shift0 = sb("shift0", [P, GS, HEADS])
        absent = sb("absent", [P, GS])
        scale = [sb(f"scale{i}", [P, GS, HEADS]) for i in range(2)]
        score = sb("score", [P, GT, HEADS])
        wgt = sb("wgt", [P, GT, HEADS])
        c_g = [counter(f"gathered{i}") for i in range(NGB)]
        c_seg = [counter(f"segments{i}") for i in range(2)]
        gath_free, oh_free, oh16_free, oh32_ready = [None] * NGB, [None] * 2, [None] * 2, {}
        gathered, seg_loaded, seg_free = {}, {}, [None] * 2
        b_asrc, b_cand, b_ms, b_edge = bank[0], bank[0], bank[1], bank[2]
        oh_ready, oht_ready, oht_free = {}, {}, [None] * 2
        ohp_free, agp_free = [None] * 2, [None] * 3
        msg_ready, scale_ready, scale_free, words = {}, {}, [None] * 2, {}
        S = {}

        def fetch(g):
            if g == 0:
                wait(pool, table_written, t_srccol, *node_phase_done)
                wait(sp, t_scr)
            wait(pool, gath_free[g % NGB])
            for t in range(GT):
                k = g * GS + t // 2
                gathered[g] = c_g[g % NGB].mark(pool.indirect_dma_start(
                    gath[g % NGB][:, t, :], None, node_table,
                    bass.IndirectOffsetOnAxis(ap=src_col[:, k, t % 2:t % 2 + 1], axis=0)), 16)
            wait(sp, seg_free[g % 2])
            rows = slice(g * GS, (g + 1) * GS)
            c_seg[g % 2].mark(sp.dma_start(seg_new[g % 2][:, :], step_new[rows, :].unsqueeze(1).to_broadcast([GS, HEADS, EB])), 16)
            seg_loaded[g] = c_seg[g % 2].mark(sp.dma_start(seg_last[g % 2][:, :], step_last[rows, :].unsqueeze(1).to_broadcast([GS, HEADS, EB])), 16)

        def one_hots(g):
            wait(dve, oh16_free[g % 2])
            d = dst_col[:, g * GS:(g + 1) * GS, :].rearrange("p k j -> p (k j)")
            oh_ready[g] = vC.mark(dve.tensor_tensor(
                onehot16[g % 2], iota16[:, :].unsqueeze(1).to_broadcast([P, GT, P]),
                d.unsqueeze(2).to_broadcast([P, GT, P]), ALU.is_equal))

        def turn_one_hots(g):
            wait(pe, oh_ready[g])
            wait(act, oht_free[g % 2])
            for q in range(2):
                wait(pe, ohp_free[q])
                turned = bank[3 + q][:, :].bitcast(BF16)
                for j in range(GT // 2):
                    ins = pe.transpose(turned[:, j * P:(j + 1) * P], onehot16[g % 2][:, q * GT // 2 + j, :], ident16[:, :])
                t = pC.mark(ins)
                wait(act, t)
                oht_ready[g] = ohp_free[q] = aC.mark(act.copy(
                    onehot_t[g % 2][:, q * GT // 2:(q + 1) * GT // 2, :], turned.rearrange("p (t n) -> p t n", n=P)))

        def widen_one_hots(g):
            wait(act, oh_ready[g], oh_free[g % 2])
            oh16_free[g % 2] = oh32_ready[g] = aC.mark(act.copy(onehot[g % 2], onehot16[g % 2]))

        def take_asrc(g):
            gb = gath[g % NGB].rearrange("p (k j) c -> p k j c", j=2)
            wait(act, gathered[g], S.get("asrc_turned"))
            t = aC.mark(act.copy(asrc[:, :, :, :], gb[:, :, :, AGG:ROW].rearrange("p k j h -> p j k h")))
            wait(pe, t, S.get("cand_read"))
            for j in range(2):
                ins = pe.transpose(b_asrc[0:HEADS * GS, j * P:(j + 1) * P], asrc[:, j, :, :].rearrange("p k h -> p (k h)"), ident[:, :])
            S["asrc_turned"] = pC.mark(ins)

        def seg_scan(g):
            wait(dve, S["asrc_turned"], seg_loaded[g], S.get("cand_turned"))
            S["scanned"] = vC.mark(dve.tensor_tensor_scan(seg_max[:, :], seg_new[g % 2][:, :], b_asrc[0:HEADS * GS, 0:EB], -BIG, ALU.add, ALU.max))

        def seg_mask(g):
            wait(dve, S["scanned"])
            S["masked"] = seg_free[g % 2] = vC.mark(dve.tensor_tensor(seg_max[:, :], seg_max[:, :], seg_last[g % 2][:, :], ALU.mult))

        def seg_turn(g):
            wait(pe, S["masked"])
            for j in range(2):
                ins = pe.transpose(b_cand[:, EB + j * 64:EB + (j + 1) * 64], seg_max[:, j * P:(j + 1) * P], ident[0:64, 0:64])
            S["cand_turned"] = t = pC.mark(ins)
            wait(act, S.get("ms_done"))
            aC.mark(act.copy(cand[:, 0, :, :, HEADS:HEADS + 1],
                             last_col[:, g * GS:(g + 1) * GS, :].rearrange("p k j -> p j k").unsqueeze(3)))
            values = b_cand[:, EB:EB + P].rearrange("p (j k h) -> p j k h", j=2, k=GS)
            wait(act, t)
            t = aC.mark(act.copy(cand[:, 0, :, :, 0:HEADS], values))
            wait(dve, t)
            t = S["cand_read"] = vC.mark(dve.tensor_tensor(cand_rest[:, :, :, :], values, cand[:, 0, :, :, 0:HEADS], ALU.subtract))
            wait(act, t)
            t = aC.mark(act.copy(cand[:, 1, :, :, 0:HEADS], cand_rest[:, :, :, :]))
            wait(dve, t)
            S["cand_split"] = vC.mark(dve.tensor_tensor(cand[:, 2, :, :, 0:HEADS], cand_rest[:, :, :, :], cand[:, 1, :, :, 0:HEADS], ALU.subtract))

        def node_maxima(g):
            wait(pe, S["cand_split"], S.get("ms_read"))
            for k in range(GS):
                for j in range(2):
                    for i in range(3):
                        ins = pe.matmul(b_ms[:, k * 9:(k + 1) * 9], onehot16[g % 2][:, 2 * k + j, :], cand[:, i, j, k, :],
                                        start=(i == j == 0), stop=(j == 1 and i == 2))
            S["ms_done"] = pC.mark(ins)

        def window(g, k):
            if g not in words:
                words[g] = dve.value_load(win_word[0:1, g:g + 1], min_val=0, max_val=(1 << 27) - 1)
            w = words[g] & 63
            if k:
                w = w + ((words[g] >> (3 + 3 * k)) & 7)
            return nc.s_assert_within(w, 0, WIN - 1, skip_runtime_bounds_check_because="a step's window is at most WIN - 1")

        def shifts(g):
            ms = b_ms[:, 0:9 * GS].rearrange("p (k c) -> p k c", c=9)
            if g < NGR:
                wait(dve, S["ms_done"])
                t = vC.mark(dve.tensor_scalar(absent[:, :], ms[:, :, HEADS], BIG, -BIG, ALU.mult, ALU.add))
                wait(dve, t)
                t = S["ms_read"] = vC.mark(dve.tensor_tensor(newm[:, :, :], ms[:, :, 0:HEADS], absent[:, :].unsqueeze(2).to_broadcast([P, GS, HEADS]), ALU.add))
                t_max = t
            for k in range(GS):
                if g < NGR:
                    w = window(g, k)
                    wait(dve, t_max)
                    t_copy = vC.mark(dve.tensor_copy(old[:, k, :], win[:, w, AGG:WROW]))
                if g > 0:
                    scale_sums(g - 1, k)
                if g < NGR:
                    wait(dve, t_copy)
                    t_max = vC.mark(dve.tensor_tensor(win[:, w, AGG:ROW], win[:, w, AGG:ROW], newm[:, k, :], ALU.max))
                if g > 0:
                    add_sums(g - 1, k)
            if g == NGR:
                return
            wait(dve, t_max, S.get("edge_vals"))
            t = vC.mark(dve.tensor_tensor(newm[:, :, :], newm[:, :, :], old[:, :, 0:HEADS], ALU.max))
            t2 = vC.mark(dve.tensor_copy(nodeval[:, :, 0:HEADS], old[:, :, HEADS:2 * HEADS]))
            wait(dve, t2)
            for m in (newm[:, :, :], old[:, :, 0:HEADS]):
                t = vC.mark(dve.tensor_tensor(m, m, nodeval[:, :, 0:HEADS], ALU.add))
            wait(dve, t)
            t_nv = vC.mark(dve.scalar_tensor_tensor(nodeval[:, :, HEADS:2 * HEADS], newm[:, :, :], SLOPE, newm[:, :, :], ALU.mult, ALU.max))
            t = vC.mark(dve.scalar_tensor_tensor(shift0[:, :, :], old[:, :, 0:HEADS], SLOPE, old[:, :, 0:HEADS], ALU.mult, ALU.max))
            wait(dve, t_nv)
            t = vC.mark(dve.tensor_copy(parts[:, 0, :, :], nodeval[:, :, :]))
            wait(dve, t, scale_free[g % 2])
            t = vC.mark(dve.tensor_tensor(rest[:, :, :], nodeval[:, :, :], parts[:, 0, :, :], ALU.subtract))
            t_sc = vC.mark(dve.tensor_tensor(scale[g % 2][:, :, :], shift0[:, :, :], nodeval[:, :, HEADS:2 * HEADS], ALU.subtract))
            wait(dve, t)
            t = vC.mark(dve.tensor_copy(parts[:, 1, :, :], rest[:, :, :]))
            wait(dve, t)
            S["parts"] = vC.mark(dve.tensor_tensor(parts[:, 2, :, :], rest[:, :, :], parts[:, 1, :, :], ALU.subtract))
            wait(act, t_sc)
            scale_ready[g] = aC.mark(act.activation(scale[g % 2][:, :, :], scale[g % 2][:, :, :], ACT.Exp))

        def edge_values(g):
            wait(pe, S["parts"], oht_ready[g], S.get("score_read"))
            for t in range(GT):
                for i in range(3):
                    ins = pe.matmul(b_edge[:, t * 16:(t + 1) * 16], onehot_t[g % 2][:, t, :], parts[:, i, t // 2, :],
                                    start=(i == 0), stop=(i == 2))
            S["edge_vals"] = oht_free[g % 2] = pC.mark(ins)

        def scores(g):
            gb = gath[g % NGB]
            ev = b_edge[:, 0:16 * GT].rearrange("p (t c) -> p t c", c=16)
            wait(dve, S["edge_vals"], gathered[g], S.get("exp_done"))
            t = vC.mark(dve.tensor_tensor(score[:, :, :], gb[:, :, AGG:ROW], ev[:, :, 0:HEADS], ALU.add))
            wait(dve, t)
            t = vC.mark(dve.scalar_tensor_tensor(score[:, :, :], score[:, :, :], SLOPE, score[:, :, :], ALU.mult, ALU.max))
            wait(dve, t)
            t = S["score_read"] = vC.mark(dve.tensor_tensor(score[:, :, :], score[:, :, :], ev[:, :, HEADS:16], ALU.subtract))
            wait(act, t, S.get("weighted"))
            S["exp_done"] = aC.mark(act.activation(wgt[:, :, :], score[:, :, :], ACT.Exp))

        def messages(g, q):
            wait(dve, S["exp_done"])
            r = slice(4 * q, 4 * q + 4)
            rows = gath[g % NGB][:, r, 0:AGG].rearrange("p t (h c) -> p t h c", c=HC)
            msg_ready[g, q] = S["weighted"] = vC.mark(dve.tensor_tensor(
                rows, rows, wgt[:, r, :].unsqueeze(3).to_broadcast([P, 4, HEADS, HC]), ALU.mult))

        def sum_messages(g, k):
            bk = bank[5 + (g * GS + k) % 3]
            wait(pe, msg_ready[g, k // 2], oh32_ready[g], agp_free[(g * GS + k) % 3])
            for j in range(2):
                ins = pe.matmul(bk[:, 0:AGG], onehot[g % 2][:, 2 * k + j, :], gath[g % NGB][:, 2 * k + j, 0:AGG],
                                start=(j == 0), stop=(j == 1))
            S["sum", g, k] = pC.mark(ins)
            if k == GS - 1:
                gath_free[g % NGB] = oh_free[g % 2] = S["sum", g, k]

        def scale_sums(g, k):
            rows = win[:, window(g, k), 0:AGG].rearrange("p (h c) -> p h c", c=HC)
            wait(dve, scale_ready[g], S.get("added"))
            S["scaled"] = vC.mark(dve.tensor_tensor(rows, rows, scale[g % 2][:, k, :].unsqueeze(2).to_broadcast([P, HEADS, HC]), ALU.mult))

        def add_sums(g, k):
            bk = bank[5 + (g * GS + k) % 3]
            sum_messages(g, k)
            row = win[:, window(g, k), 0:AGG]
            wait(dve, S["scaled"], S["sum", g, k])
            S["added"] = agp_free[(g * GS + k) % 3] = vC.mark(dve.tensor_tensor(row, row, bk[:, 0:AGG], ALU.add))
            if k == GS - 1:
                scale_free[g % 2] = S["added"]

        t = vC.mark(dve.memset(cand[:, 1:3, :, :, HEADS:HEADS + 1], 0.0))
        wait(pe, t)
        t = c_pool.mark(pool.memset(zero[:, :], 0.0))
        wait(sp, t)
        c_zero = counter("slots_zeroed")
        t_zero = load(slot_rows.rearrange("(p a) d -> p a d", p=P),
                      zero[:, :].unsqueeze(1).to_broadcast([P, slots_total // P, D]), c_zero)
        wait(dve, table_written, t_win, t_cols, t_scr, *node_phase_done)
        wait(act, t_cols)
        NGR = NG if not DEBUG_GROUPS else DEBUG_GROUPS
        for g in range(-1, NGR + 1):
            if g == -1:
                fetch(0)
            if g + 2 < NGR:
                fetch(g + 2)
            if g >= 0:
                shifts(g)
            if 0 <= g < NGR:
                edge_values(g)
            if g + 1 < NGR:
                take_asrc(g + 1)
                one_hots(g + 1)
            if 0 <= g < NGR:
                scores(g)
            if g + 1 < NGR:
                seg_scan(g + 1)
                seg_mask(g + 1)
                turn_one_hots(g + 1)
            for q in range(4):
                if 0 <= g < NGR:
                    messages(g, q)
                if q == 0 and g + 1 < NGR:
                    seg_turn(g + 1)
            if g + 1 < NGR:
                node_maxima(g + 1)
            if 0 <= g < NGR:
                widen_one_hots(g)
        edges_done = [(vC.sem, vC.value), (pC.sem, pC.value), (aC.sem, aC.value)]
        if DEBUG:
            dbg = dram("dbg_win", [P, WIN * WROW])
            wait(sp, *edges_done)
            t = c_scr.mark(sp.dma_start(dbg, arena[:, 0:WIN * WROW]), 16)
            wait(sp, t)

        o = GATH
        hidden = [part(o, MC, 512), work_part(0, MC, 512)]
        o += MC * 512
        res_in = [part(o + i * 4 * D, 4, D) for i in range(2)]
        o += 8 * D
        x_in = [part(o + i * 4 * D, 4, D) for i in range(2)]
        o += 8 * D
        rows = [part(o + i * 4 * D, 4, D) for i in range(2)]
        o += 8 * D
        zrow = part(o, 4, D)
        o += 4 * D
        zT = part(o, KC, 512)
        o += KC * 512
        ln2_gb = part(o, 2, D)
        fb2_b = part(o + 2 * D, D)
        o += 3 * D
        assert o <= ARENA - WORK
        fw1 = work_part(MC * 512, KC, HID)
        fw2 = work_part(MC * 512 + KC * HID, MC, D)
        outT = [work_part(MC * 512 + 2 * KC * HID + i * KC * 512, KC, 512) for i in range(2)]
        rec = sb("rec", [P, 4, HEADS])
        wr_sb = sb("wr_sb", [P, KC, E])
        br_b = sb("br_b", [P, E])
        g2 = sb("g2", [P, 2, KC])
        fb1 = sb("fb1", [P, MC])
        logits = sb("logits", [P, NT, E])
        c_w2 = counter("layer_weights")
        vD, aD, pD = counter("dve_layer"), counter("act_layer"), counter("pe_layer")
        c_in = [counter(f"layer_in{i}") for i in range(2)]
        c_x1 = [counter(f"x1_written{i}") for i in range(2)]

        wait(sp, *edges_done)
        for k in range(KC):
            load(fw1[:, k, :], f_w1[k * P:(k + 1) * P, :], c_w2)
            load(wr_sb[:, k, :], Wr[k * P:(k + 1) * P, :], c_w2)
        load(fw2, f_w2.rearrange("(m p) d -> p m d", p=P), c_w2)
        load(ln2_gb[:, 0, :], ln2_g.unsqueeze(0).to_broadcast([P, D]), c_w2)
        load(ln2_gb[:, 1, :], ln2_b.unsqueeze(0).to_broadcast([P, D]), c_w2)
        load(fb2_b, f_b2.unsqueeze(0).to_broadcast([P, D]), c_w2)
        load(br_b[:, :], br.unsqueeze(0).to_broadcast([P, E]), c_w2)
        with nc.allow_non_contiguous_dma(reason="a few small vectors, one element per partition"):
            load(g2[:, 0, :], ln2_g.rearrange("(k p) -> p k", p=P), c_w2)
            load(g2[:, 1, :], ln2_b.rearrange("(k p) -> p k", p=P), c_w2)
            t_fw = load(fb1[:, :], f_b1.rearrange("(m p) -> p m", p=P), c_w2)
        wait(dve, t_fw, *edges_done)
        t_gb = vD.mark(dve.tensor_tensor(fb2_b, fb2_b, ln2_gb[:, 1, :], ALU.add))
        wait(act, *edges_done)
        wait(pe, *edges_done)
        wait(pool, *edges_done)

        bank_free = [None] * 8
        in_free, hid_free, outT_free, x1_free = [None] * 2, [None] * 2, [None] * 2, [None] * 2
        D_ = {}

        def d_load(b):
            n, i = tiles_of(b), b % 2
            wait(sp, in_free[i])
            r = slice(4 * b * P, (4 * b + n) * P)
            c_in[i].mark(sp.dma_start(res_in[i][:, 0:n, :], residual[r, :].rearrange("(t p) d -> p t d", p=P)), 16)
            if b == NB - 1:
                wait(dve, in_free[i])
                wait(sp, vD.mark(dve.memset(x_in[i][:, n - 1, :], 0.0)))
                if n > 1:
                    c_in[i].mark(sp.dma_start(x_in[i][:, 0:n - 1, :], x[4 * b * P:(NT - 1) * P, :].rearrange("(t p) d -> p t d", p=P)), 16)
                D_["in", b] = c_in[i].mark(sp.dma_start(x_in[i][0:last_rows, n - 1, :], x[(NT - 1) * P:N, :]), 16)
            else:
                D_["in", b] = c_in[i].mark(sp.dma_start(x_in[i][:, 0:n, :], x[r, :].rearrange("(t p) d -> p t d", p=P)), 16)

        def norm_into(dsts, srcs, ready):
            done = []
            for _ in norm_steps(dsts, srcs, vD, ready, done):
                pass
            return done[-1]

        def d_merge(b):
            n, i = tiles_of(b), b % 2
            wv = win[:, 4 * b:4 * b + n, 0:AGG].rearrange("p t (h c) -> p t h c", c=HC)
            rv = rows[i][:, 0:n, :].rearrange("p t (h d) -> p t h d", d=HD)
            wait(dve, D_.get("rec_used"), x1_free[i])
            t = vD.mark(dve.reciprocal(rec[:, 0:n, :].unsqueeze(3), wv[:, :, :, HD:HC]))
            wait(dve, t)
            t = D_["rec_used"] = vD.mark(dve.tensor_tensor(rv, wv[:, :, :, 0:HD], rec[:, 0:n, :].unsqueeze(3).to_broadcast([P, n, HEADS, HD]), ALU.mult))
            wait(dve, t, D_["in", b])
            t = vD.mark(dve.tensor_tensor(rows[i][:, 0:n, :], rows[i][:, 0:n, :], res_in[i][:, 0:n, :], ALU.add))
            tl = [rows[i][:, j, :] for j in range(n)]
            D_["norm", b] = norm_into(tl, tl, t)

        def turn(src, dst, n, b0, ready, dst_free, scaled):
            wait(pe, ready)
            for k in range(KC):
                bk = b0 + k
                wait(pe, bank_free[bk])
                for j in range(n):
                    ins = pe.transpose(bank[bk][:, j * P:(j + 1) * P], src[:, j, k * P:(k + 1) * P], ident[:, :])
                t_pe = pD.mark(ins)
                wait(act, t_pe, dst_free, t_fw)
                if scaled:
                    ins = act.activation(dst[:, k, 0:n * P], bank[bk][:, 0:n * P], ACT.Identity,
                                         scale=g2[:, 0, k:k + 1], bias=g2[:, 1, k:k + 1])
                else:
                    ins = act.copy(dst[:, k, 0:n * P], bank[bk][:, 0:n * P])
                bank_free[bk] = aD.mark(ins)
            return t_pe, bank_free[b0 + KC - 1]

        def d_turn(b):
            n, i = tiles_of(b), b % 2
            t_pe, D_["outT", b] = turn(rows[i], outT[i], n, 0, D_["norm", b], outT_free[i], True)
            wait(pool, t_pe, D_["norm", b], t_gb)
            for op, other in ((ALU.mult, ln2_gb[:, 0, :].unsqueeze(1).to_broadcast([P, n, D])),
                              (ALU.add, fb2_b.unsqueeze(1).to_broadcast([P, n, D])),
                              (ALU.add, x_in[i][:, 0:n, :])):
                t = c_pool.mark(pool.tensor_tensor(rows[i][:, 0:n, :], rows[i][:, 0:n, :], other, op))
                wait(pool, t)
            in_free[i] = D_["base", b] = t

        def d_ffn(b):
            n, i = tiles_of(b), b % 2
            wait(pe, D_["outT", b])
            for m in range(MC):
                bk = 2 + m % 2
                wait(pe, bank_free[bk])
                for k in range(KC):
                    ins = pe.matmul(bank[bk][:, 0:n * P], fw1[:, k, m * P:(m + 1) * P], outT[i][:, k, 0:n * P],
                                    start=(k == 0), stop=(k == KC - 1))
                t = pD.mark(ins)
                wait(act, t, hid_free[i])
                D_["hid", b] = bank_free[bk] = aD.mark(act.activation(
                    hidden[i][:, m, 0:n * P], bank[bk][:, 0:n * P], ACT.Gelu_apprx_tanh, bias=fb1[:, m:m + 1]))
            outT_free[i] = t

        def d_out(b):
            n, i = tiles_of(b), b % 2
            wait(pe, D_["hid", b])
            for j in range(n):
                bk = 4 + j % 2
                wait(pe, bank_free[bk])
                for m in range(MC):
                    ins = pe.matmul(bank[bk][:, 0:D], hidden[i][:, m, j * P:(j + 1) * P], fw2[:, m, :],
                                    start=(m == 0), stop=(m == MC - 1))
                t = pD.mark(ins)
                wait(dve, t, D_["base", b])
                D_["x1", b] = bank_free[bk] = vD.mark(dve.tensor_tensor(rows[i][:, j, :], rows[i][:, j, :], bank[bk][:, 0:D], ALU.add))
            hid_free[i] = t
            wait(sp, D_["x1", b])
            r = slice(4 * b * P, (4 * b + n) * P)
            x1_free[i] = c_x1[i].mark(sp.dma_start(x1_dram[r, :].rearrange("(t p) d -> p t d", p=P), rows[i][:, 0:n, :]), 16)

        def d_route(b):
            n, i = tiles_of(b), b % 2
            zs = [zrow[:, j, :] for j in range(n)]
            wait(dve, D_.get("z_turned"), D_.get("z_used"))
            t = norm_into(zs, [rows[i][:, j, :] for j in range(n)], D_["x1", b])
            D_["z_turned"], t_zT = turn(zrow, zT, n, 6, t, D_.get("zT_used"), False)
            D_["z_used"] = norm_into([win[:, 4 * b + j, 0:D] for j in range(n)], zs, t)
            D_["zT"] = t_zT

        def d_logits(b):
            n = tiles_of(b)
            wait(pe, D_["zT"], bank_free[5])
            for j in range(n):
                for k in range(KC):
                    ins = pe.matmul(bank[5][:, j * E:(j + 1) * E], zT[:, k, j * P:(j + 1) * P], wr_sb[:, k, :],
                                    start=(k == 0), stop=(k == KC - 1))
            t = D_["zT_used"] = pD.mark(ins)
            wait(dve, t)
            bank_free[5] = vD.mark(dve.tensor_tensor(
                logits[:, 4 * b:4 * b + n, :], bank[5][:, 0:n * E].rearrange("p (t e) -> p t e", e=E),
                br_b[:, :].unsqueeze(1).to_broadcast([P, n, E]), ALU.add))

        for i in range(NB + 2):
            if i < NB:
                d_load(i)
            if 1 <= i <= NB:
                d_ffn(i - 1)
            if i >= 2:
                d_route(i - 2)
            if i < NB:
                d_merge(i)
                d_turn(i)
            if i >= 2:
                d_logits(i - 2)
            if 1 <= i <= NB:
                d_out(i - 1)
        layer_done = [(vD.sem, vD.value), (pD.sem, pD.value), (aD.sem, aD.value), (c_pool.sem, c_pool.value),
                      x1_free[0], x1_free[1]]

        SLOT = 2 * P
        NS = (2 * N + E * (SLOT - 1)) // SLOT
        NWB = 4
        w1_buf = [part(i * (KC * HID + MC * D), KC, HID) for i in range(NWB)]
        w2_buf = [part(i * (KC * HID + MC * D) + KC * HID, MC, D) for i in range(NWB)]
        o = 0
        ehid = [work_part(o + i * MC * SLOT, MC, SLOT) for i in range(2)]
        o += 2 * MC * SLOT
        xin = [work_part(o + i * 2 * D, 2, D) for i in range(2)]
        o += 4 * D
        xinT = [work_part(o + i * KC * SLOT, KC, SLOT) for i in range(2)]
        o += 2 * KC * SLOT
        yout = [work_part(o + i * 2 * D, 2, D) for i in range(2)]
        o += 4 * D
        b2_b = work_part(o, E, D)
        o += E * D
        assert o <= WORK
        epar = sb("epar", [P, E, 2 * KC + MC])
        par = [sb(f"par{i}", [P, 2 * KC + MC]) for i in range(3)]
        c_b2 = counter("expert_b2")
        c_we = [counter(f"expert_weights{i}") for i in range(NWB)]
        vE, aE, pE = counter("dve_experts"), counter("act_experts"), counter("pe_experts")
        c_disp = counter("dispatched")
        c_xin = [counter(f"slot_in{i}") for i in range(2)]
        c_y = [counter(f"slot_out{i}") for i in range(2)]

        for eng in (sp, dve, act, pe, pool):
            wait(eng, *layer_done)
        t_b2 = load(b2_b, b2.rearrange("e d -> (e d)").unsqueeze(0).to_broadcast([P, E * D]).rearrange("p (e d) -> p e d", d=D), c_b2)
        with nc.allow_non_contiguous_dma(reason="small vectors, one element per partition"):
            for e in range(E):
                load(epar[:, e, 0:KC], ln_g[e, :].rearrange("(k p) -> p k", p=P), c_b2)
                load(epar[:, e, KC:2 * KC], ln_b[e, :].rearrange("(k p) -> p k", p=P), c_b2)
                t_epar = load(epar[:, e, 2 * KC:], b1[e, :].rearrange("(m p) -> p m", p=P), c_b2)

        NL = NT * E
        rt = part(GATH, 6, NL)
        prob, sel = logits[:, :, :], [rt[:, i, :].rearrange("p (t e) -> p t e", e=E) for i in range(2)]
        both, top8 = [rt[:, i, :].rearrange("p (t e) -> p t e", e=E) for i in (2, 3)]
        idx8 = rt[:, 4, :].bitcast(U32).rearrange("p (t e) -> p t e", e=E)
        place = rt[:, 5, :].rearrange("p (t e) -> p t e", e=E)
        per_tok = sb("per_tok", [P, 6, NT])
        tmax, wsum, idxf = per_tok[:, 0, :], per_tok[:, 1, :], per_tok[:, 2, :]
        gate = [per_tok[:, 3 + i, :] for i in range(2)]
        valid = per_tok[:, 5, :]
        pos = sb("pos", [P, 2, NT], I32)
        per_exp = sb("per_exp", [P, 8, E])
        slot_e = sb("slot_e", [1, NS, E])
        slot_i = sb("slot_i", [1, NS], I32)
        iota_s = sb("iota_s", [P, NS])
        tri = sb("tri", [P, P])

        def v(ins, *before):
            t = vE.mark(ins)
            wait(dve, t)
            return t

        t = c_pool.mark(pool.memset(tri[:, :], 1.0))
        t2 = c_pool.mark(pool.memset(valid, 1.0))
        wait(pool, t, t2)
        c_pool.mark(pool.affine_select(out=tri[:, :], in_=tri[:, :], compare_op=ALU.is_gt, fill=0.0,
                                       base=0, pattern=[[1, P]], channel_multiplier=-1))
        c_pool.mark(pool.affine_select(out=valid[:, NT - 1:NT], in_=valid[:, NT - 1:NT], compare_op=ALU.is_gt, fill=0.0,
                                       base=last_rows, pattern=[[0, 1]], channel_multiplier=-1))
        t_is = c_pool.mark(pool.iota(iota_s[:, :].bitcast(I32), pattern=[[1, NS]], base=0, channel_multiplier=0))
        wait(dve, t_is)
        t = vE.mark(dve.tensor_copy(slot_e[0:1, :, 0], iota_s[0:1, :].bitcast(I32)))
        wait(dve, t)
        t = vE.mark(dve.tensor_copy(iota_s[0:1, :], slot_e[0:1, :, 0]))
        wait(dve, t)
        v(dve.tensor_reduce(tmax, prob, AX.X, ALU.max))
        t = v(dve.tensor_tensor(prob, prob, tmax.unsqueeze(2).to_broadcast([P, NT, E]), ALU.subtract))
        wait(act, t)
        t = aE.mark(act.activation(prob, prob, ACT.Exp))
        wait(dve, t)
        v(dve.tensor_reduce(wsum, prob, AX.X, ALU.add))
        v(dve.reciprocal(wsum, wsum))
        t = v(dve.tensor_tensor(prob, prob, wsum.unsqueeze(2).to_broadcast([P, NT, E]), ALU.mult))
        for w in range(NT):
            t = vE.mark(dve.max(top8[:, w, :], prob[:, w, :]))
        wait(dve, t)
        for w in range(NT):
            t = vE.mark(dve.max_index(idx8[:, w, :], top8[:, w, :], prob[:, w, :]))
        wait(dve, t)
        v(dve.tensor_tensor(wsum, top8[:, :, 0], top8[:, :, 1], ALU.add))
        v(dve.reciprocal(wsum, wsum))
        for s in range(2):
            v(dve.tensor_tensor(gate[s], top8[:, :, s], wsum, ALU.mult))
        for s in range(2):
            v(dve.tensor_copy(idxf, idx8[:, :, s]))
            v(dve.tensor_tensor(sel[s], iota_row[:, 0:E].unsqueeze(1).to_broadcast([P, NT, E]),
                                idxf.unsqueeze(2).to_broadcast([P, NT, E]), ALU.is_equal))
            v(dve.tensor_tensor(sel[s], sel[s], valid.unsqueeze(2).to_broadcast([P, NT, E]), ALU.mult)) if s or True else None
        t = v(dve.tensor_tensor(both, sel[0], sel[1], ALU.add))
        wait(pe, t, (c_pool.sem, c_pool.value))
        pE.mark(pe.matmul(bank[0][:, 0:NL], tri[:, :], rt[:, 2, :], start=True, stop=True))
        t = pE.mark(pe.matmul(bank[1][:, 0:NL], ones[:, :], rt[:, 2, :], start=True, stop=True))
        wait(dve, t)
        v(dve.tensor_copy(both, bank[1][:, 0:NL].rearrange("p (t e) -> p t e", e=E)))
        for e in range(E):
            t = vE.mark(dve.tensor_tensor_scan(place[:, :, e], both[:, :, e], ones[:, 0:NT], 0.0, ALU.add, ALU.mult))
        wait(dve, t)
        total, slots, upto, start = [per_exp[:, i, :] for i in range(4)]
        total_i = per_exp[:, 4, :].bitcast(I32)
        v(dve.tensor_copy(total, place[:, NT - 1, :]))
        v(dve.tensor_scalar(total_i, total, float(SLOT - 1), None, ALU.add))
        v(dve.tensor_single_scalar(total_i, total_i, 8, ALU.arith_shift_right))
        v(dve.tensor_copy(slots, total_i))
        v(dve.tensor_tensor_scan(upto, slots, ones[:, 0:E], 0.0, ALU.add, ALU.mult))
        v(dve.tensor_tensor(start, upto, slots, ALU.subtract))
        v(dve.tensor_scalar(start, start, float(SLOT), None, ALU.mult))
        v(dve.tensor_tensor(place, place, both, ALU.subtract))
        v(dve.tensor_tensor(place, place, bank[0][:, 0:NL].rearrange("p (t e) -> p t e", e=E), ALU.add))
        v(dve.tensor_tensor(place, place, start.unsqueeze(1).to_broadcast([P, NT, E]), ALU.add))
        for s in range(2):
            v(dve.tensor_tensor(sel[s], sel[s], place, ALU.mult))
            v(dve.tensor_reduce(idxf, sel[s], AX.X, ALU.add))
            t_pos = v(dve.tensor_copy(pos[:, s, :], idxf))
        v(dve.tensor_tensor(slot_e[:, :, :], upto[0:1, :].unsqueeze(1).to_broadcast([1, NS, E]),
                            iota_s[0:1, :].unsqueeze(2).to_broadcast([1, NS, E]), ALU.is_le))
        v(dve.tensor_reduce(iota_s[0:1, :], slot_e[:, :, :], AX.X, ALU.add))
        v(dve.tensor_scalar(iota_s[0:1, :], iota_s[0:1, :], float(E - 1), None, ALU.min))
        t_slot = v(dve.tensor_copy(slot_i[:, :], iota_s[0:1, :]))

        wait(pool, t_pos, t_zero)
        for w in range(NT):
            r = P if w < NT - 1 else last_rows
            for s in range(2):
                t_disp = c_disp.mark(pool.indirect_dma_start(
                    slot_rows, bass.IndirectOffsetOnAxis(ap=pos[0:r, s, w:w + 1], axis=0),
                    win[0:r, w, 0:D], None), 16)
        wait(sp, t_disp, t_slot)

        xin_free, xinT_free, ehid_free, y_free, par_free = [None] * 2, [None] * 2, [None] * 2, [None] * 2, [None] * 3
        bank_free = [None] * 8
        E_ = {}
        wait(dve, t_b2, t_epar)
        w_free = [None] * NWB
        W1_v = W1.rearrange("e (k p) h -> e p k h", p=P)
        W2_v = W2.rearrange("e (m p) d -> e p m d", p=P)

        def e_in(j):
            i = j % 2
            e, wb = sp.value_load(slot_i[0:1, j:j + 1], min_val=0, max_val=E - 1), j % NWB
            wait(sp, w_free[wb])
            load(w1_buf[wb], W1_v[e], c_we[wb])
            E_["w", j] = load(w2_buf[wb], W2_v[e], c_we[wb])
            wait(sp, xin_free[i])
            E_["in", j] = c_xin[i].mark(sp.dma_start(xin[i], slot_rows[j * SLOT:(j + 1) * SLOT, :].rearrange("(t p) d -> p t d", p=P)), 16)

        def e_turn(j):
            i = j % 2
            e = E_["dve_e", j] = dve.value_load(slot_i[0:1, j:j + 1], min_val=0, max_val=E - 1)
            wait(dve, par_free[j % 3])
            t_par = vE.mark(dve.tensor_copy(par[j % 3][:, :], epar[:, e, :]))
            wait(pe, E_["in", j], bank_free[0])
            for k in range(KC):
                for t in range(2):
                    ins = pe.transpose(bank[0][:, k * SLOT + t * P:k * SLOT + (t + 1) * P], xin[i][:, t, k * P:(k + 1) * P], ident[:, :])
            xin_free[i] = t = pE.mark(ins)
            wait(act, t, t_par, xinT_free[i])
            for k in range(KC):
                t = aE.mark(act.activation(xinT[i][:, k, :], bank[0][:, k * SLOT:(k + 1) * SLOT], ACT.Identity,
                                           scale=par[j % 3][:, k:k + 1], bias=par[j % 3][:, KC + k:KC + k + 1]))
            E_["inT", j] = bank_free[0] = t

        def e_first(j):
            i = j % 2
            w1 = w1_buf[j % NWB]
            wait(pe, E_["inT", j], E_["w", j])
            for m in range(MC):
                bk = 1 + m % 4
                wait(pe, bank_free[bk])
                for k in range(KC):
                    ins = pe.matmul(bank[bk][:, 0:SLOT], w1[:, k, m * P:(m + 1) * P], xinT[i][:, k, :],
                                    start=(k == 0), stop=(k == KC - 1))
                t = pE.mark(ins)
                wait(act, t, ehid_free[i])
                E_["hid", j] = bank_free[bk] = aE.mark(act.activation(
                    ehid[i][:, m, :], bank[bk][:, 0:SLOT], ACT.Gelu, bias=par[j % 3][:, 2 * KC + m:2 * KC + m + 1]))
            par_free[j % 3] = E_["hid", j]
            xinT_free[i] = t

        def e_second(j):
            i = j % 2
            w2 = w2_buf[j % NWB]
            wait(pe, E_["hid", j])
            wait(dve, y_free[i])
            for t in range(2):
                bk = 5 + t
                wait(pe, bank_free[bk])
                for m in range(MC):
                    ins = pe.matmul(bank[bk][:, 0:D], ehid[i][:, m, t * P:(t + 1) * P], w2[:, m, :],
                                    start=(m == 0), stop=(m == MC - 1))
                tt = pE.mark(ins)
                wait(dve, tt)
                ty = bank_free[bk] = vE.mark(dve.tensor_tensor(yout[i][:, t, :], bank[bk][:, 0:D], b2_b[:, E_["dve_e", j], :], ALU.add))
            ehid_free[i] = w_free[j % NWB] = tt
            wait(sp, ty)
            y_free[i] = c_y[i].mark(sp.dma_start(slot_out[j * SLOT:(j + 1) * SLOT, :].rearrange("(t p) d -> p t d", p=P), yout[i]), 16)

        for j in range(NS + 3):
            if j < NS:
                e_in(j)
            if 1 <= j <= NS:
                e_turn(j - 1)
            if 2 <= j <= NS + 1:
                e_first(j - 2)
            if j >= 3:
                e_second(j - 3)

        CR = 4
        experts_done = [(pE.sem, pE.value), y_free[0], y_free[1]]
        ys = [[part((2 * i + s) * D, D) for s in range(2)] for i in range(CR)]
        xo = [part(2 * CR * D + i * D, D) for i in range(CR)]
        c_yg = [counter(f"y_gathered{i}") for i in range(CR)]
        c_xo = [counter(f"x1_loaded{i}") for i in range(CR)]
        c_out = [counter(f"out_written{i}") for i in range(CR)]
        out_done, ys_free = [None] * CR, [None] * CR
        wait(pool, *experts_done)
        wait(sp, *experts_done)
        for w in range(NT):
            i, r = w % CR, (P if w < NT - 1 else last_rows)
            wait(pool, ys_free[i])
            for s in range(2):
                ty = c_yg[i].mark(pool.indirect_dma_start(ys[i][s][0:r, :], None, slot_out,
                                                          bass.IndirectOffsetOnAxis(ap=pos[0:r, s, w:w + 1], axis=0)), 16)
            wait(sp, out_done[i])
            tx = c_xo[i].mark(sp.dma_start(xo[i][0:r, :], x1_dram[w * P:w * P + r, :]), 16)
            wait(dve, ty, tx)
            t = vE.mark(dve.scalar_tensor_tensor(xo[i][0:r, :], ys[i][0][0:r, :], gate[0][0:r, w:w + 1], xo[i][0:r, :], ALU.mult, ALU.add))
            wait(dve, t)
            t = ys_free[i] = vE.mark(dve.scalar_tensor_tensor(xo[i][0:r, :], ys[i][1][0:r, :], gate[1][0:r, w:w + 1], xo[i][0:r, :], ALU.mult, ALU.add))
            wait(act, t)
            out_done[i] = c_out[i].mark(act.dma_start(out[w * P:w * P + r, :], xo[i][0:r, :]), 16)
        wait(sp, *out_done)


DEBUG = 0
DEBUG_GROUPS = 0


_INS = ["x", "src", "dst", "L0_gnn_W", "L0_gnn_att_src", "L0_gnn_att_dst", "L0_gnn_bias", "L0_gnn_W_res",
        "L0_gnn_ln1_g", "L0_gnn_ln1_b", "L0_gnn_ln2_g", "L0_gnn_ln2_b", "L0_gnn_ffn_w1", "L0_gnn_ffn_b1",
        "L0_gnn_ffn_w2", "L0_gnn_ffn_b2", "L0_ffn_Wr", "L0_ffn_br", "L0_ffn_ln_g", "L0_ffn_ln_b", "L0_ffn_W1",
        "L0_ffn_b1", "L0_ffn_W2", "L0_ffn_b2"]


def kernel(**inputs):
    import numpy as np
    import concourse.bacc as bacc
    from concourse.bass_utils import run_bass_kernel_spmd

    nc = bacc.Bacc("TRN2", target_bir_lowering=False, num_devices=1)
    arrays, args = {}, []
    for name in _INS:
        a = np.ascontiguousarray(inputs[name])
        if name in ("src", "dst"):
            a = np.pad(a, (0, -len(a) % 256), constant_values=(1 << 20) if name == "dst" else 0)
        arrays[f"in_{name}"] = a
        args.append(nc.dram_tensor(f"in_{name}", a.shape, mybir.dt.from_np(a.dtype), kind="ExternalInput").ap())
    shape = inputs["x"].shape
    args.append(nc.dram_tensor("out", shape, F32, kind="ExternalOutput").ap())
    build(nc, *args)
    result = run_bass_kernel_spmd(nc, [arrays], core_ids=[0])
    return result.results[0]["out"]
```

```python
from contextlib import ExitStack

import concourse.bass as bass
from concourse import mybir

F32 = mybir.dt.float32
I32 = mybir.dt.int32
BF16 = mybir.dt.bfloat16
U32 = mybir.dt.uint32
F32R = mybir.dt.float32r
ALU = mybir.AluOpType
ACT = mybir.ActivationFunctionType
AX = mybir.AxisListType

P = 128
BIG = 1.0e30
EPS = 1e-5
SLOPE = 0.2


class Counter:

    def __init__(self, nc, ctx, name):
        self.sem, self.value = ctx.enter_context(nc.semaphore(name)), 0

    def mark(self, instruction, by=1):
        instruction.then_inc(self.sem, by)
        self.value += by
        return self.sem, self.value


def wait(engine, *tokens):
    for token in tokens:
        if token is not None:
            engine.wait_ge(*token)


def build(nc, x, src, dst, gW, att_src, att_dst, g_bias, gW_res, ln1_g, ln1_b, ln2_g, ln2_b,
          f_w1, f_b1, f_w2, f_b2, Wr, br, ln_g, ln_b, W1, b1, W2, b2, out):
    N, D = x.shape
    HEADS, HD = att_src.shape
    HID = f_w1.shape[1]
    E = Wr.shape[1]
    KC = D // P
    MC = HID // P
    NT = -(-N // P)
    NB = -(-NT // 4)
    EB = 256
    NEB = dst.shape[0] // EB
    WIN = NT + 1
    GS = 8
    NG = -(-(NEB + NT - 1) // GS)
    NSTEP = NG * GS
    NK = -(-NSTEP // P)
    GT = 2 * GS
    HC = HD + 1
    AGG = HEADS * HC
    ROW = AGG + HEADS
    WROW = ROW + HEADS
    last_rows = N - (NT - 1) * P

    ctx = ExitStack()
    with ctx:
        memory = [ctx]

        def sb(name, shape, dt=F32):
            return memory[-1].enter_context(nc.sbuf_tensor(name, shape, dt))

        def phase_memory():
            if len(memory) > 1:
                memory.pop().close()
            memory.append(ctx.enter_context(ExitStack()))

        def counter(name):
            return Counter(nc, ctx, name)

        def dram(name, shape, dt=F32):
            return nc.dram_tensor(name, shape, dt, kind="Internal").ap()

        pe, dve, act, pool, sp = nc.tensor, nc.vector, nc.scalar, nc.gpsimd, nc.sync

        node_table = dram("node_table", [NT * P, ROW])
        residual = dram("residual", [NT * P, D])
        step_new = dram("step_new", [NK * P, EB])
        step_last = dram("step_last", [NK * P, EB])
        SLOT = 2 * P
        NS = (2 * N + E * (SLOT - 1)) // SLOT
        CAP = -(-N // SLOT) * SLOT + SLOT
        XROW = D + 1 + E
        sums = dram("sums", [NT * P + SLOT, D])
        expert_rows = dram("expert_rows", [E * CAP + SLOT, XROW])
        step_win = dram("step_win", [NK * P, 1], I32)

        c_ld = counter("const_loads")
        c_pool = counter("pool_done")
        vA, aA, pA = counter("dve_nodes"), counter("act_nodes"), counter("pe_nodes")
        vB, pB = counter("dve_prep"), counter("pe_prep")
        vC, aC, pC = counter("dve_edges"), counter("act_edges"), counter("pe_edges")
        c_x = [counter(f"x_loaded{i}") for i in range(3)]
        c_tab = counter("table_written")
        c_prep = counter("prep_dma")

        bank = [ctx.enter_context(nc.psum_tensor(f"bank{i}", [P, 512], F32)) for i in range(8)]

        ident = sb("ident", [P, P])
        iota_row = sb("iota_row", [P, P])
        iota16 = sb("iota16", [P, P], BF16)
        ident16 = sb("ident16", [P, P], BF16)
        ones = sb("ones", [P, P])
        neg_half = sb("neg_half", [P, 8])
        norm_bufs = [[sb(f"{name}{i}", shape) for name, shape in (("stats", [P, 4, 6]), ("mv", [P, 4, 2]), ("rstd", [P, 4]))]
                     for i in range(2)]
        filled = sb("filled", [P, E])
        wr_sb = sb("wr_sb", [P, KC, E])
        br_b = sb("br_b", [P, E])
        g2 = sb("g2", [P, 2, KC])
        fb1 = sb("fb1", [P, MC])
        epar = sb("epar", [P, E, 2 * KC + MC])
        pos = sb("pos", [P, 2, 4, 2], I32)
        slot_number = sb("slot_number", [1, NS], I32)
        fill_id = sb("fill_id", [P, 2], I32)
        win_mem = sb("win_mem", [P, WIN * WROW])

        def cut(tensor, offset, *shape):
            size = 1
            for d in shape:
                size *= d
            names = "abcd"[:len(shape)]
            return tensor[:, offset:offset + size].rearrange(
                f"p ({' '.join(names)}) -> p {' '.join(names)}", **{n: d for n, d in zip(names, shape)})

        win = cut(win_mem, 0, WIN, WROW)

        phase_memory()
        NGB = 4
        OH0 = NGB * GT * ROW
        OT0 = OH0 + 2 * GT * P
        edge_mem = sb("edge_mem", [P, OT0 + 2 * GT * P])

        def part(offset, *shape):
            return cut(edge_mem, offset, *shape)

        def half_part(offset):
            return part(offset, GT * P // 2).bitcast(BF16).rearrange("p (t n) -> p t n", n=P)

        gath = [part(i * GT * ROW, GT, ROW) for i in range(NGB)]
        onehot = [part(OH0 + i * GT * P, GT, P) for i in range(2)]
        onehot16 = [half_part(OT0 + i * GT * P // 2) for i in range(2)]
        onehot_t = [half_part(OT0 + (2 + i) * GT * P // 2) for i in range(2)]

        xs = [part(i * 4 * D, 4, D) for i in range(3)]
        o = 12 * D
        xnT = [part(o + i * KC * 512, KC, 512) for i in range(2)]
        o += 2 * KC * 512
        res_st = [part(o + i * 4 * D, 4, D) for i in range(2)]
        o += 8 * D
        Wc = part(o, KC, D + 2 * HEADS)
        o += KC * (D + 2 * HEADS)
        Wres = part(o, KC, D)
        o += KC * D
        att = part(o, 2, D)
        att_tmp = part(o + 2 * D, D)
        bias_b = part(o + 3 * D, D)

        src_col = sb("src_col", [P, NK * P, 2], I32)
        dst_col = sb("dst_col", [P, NK * P, 2])
        last_col = sb("last_col", [P, NK * P, 2])
        win_row = sb("win_row", [1, NSTEP], I32)
        win_delta = sb("win_delta", [1, NG, GS], I32)
        win_word = sb("win_word", [1, NG], I32)

        t_c0 = c_pool.mark(pool.memset(ident[:, :], 0.0))
        c_pool.mark(pool.memset(ones[:, :], 1.0))
        c_pool.mark(pool.memset(neg_half[:, :], -0.5))
        wait(pool, t_c0)
        c_pool.mark(pool.affine_select(out=ident[:, :], in_=ident[:, :], compare_op=ALU.not_equal,
                                       fill=1.0, base=0, pattern=[[-1, P]], channel_multiplier=1))
        iota_i = part(OT0 + 2 * GT * P - P, P).bitcast(I32)
        t_i = c_pool.mark(pool.iota(iota_i, pattern=[[1, P]], base=0, channel_multiplier=0))
        wait(dve, t_i)
        vB.mark(dve.tensor_copy(iota_row[:, :], iota_i))
        vB.mark(dve.tensor_copy(iota16[:, :], iota_i))
        wait(dve, (c_pool.sem, c_pool.value))
        vB.mark(dve.tensor_copy(ident16[:, :], ident[:, :]))
        c_pool.mark(pool.iota(fill_id[:, :], pattern=[[1, 2]], base=NT * P, channel_multiplier=2))
        c_pool.mark(pool.iota(slot_number[:, :], pattern=[[1, NS]], base=0, channel_multiplier=0))
        ident_ready = (c_pool.sem, c_pool.value)

        def load(dst_ap, src_ap, c=None):
            return (c or c_ld).mark(sp.dma_start(dst_ap, src_ap), 16)

        g1 = sb("g1", [P, 2, KC])
        for k in range(KC):
            load(Wc[:, k, 0:D], gW[k * P:(k + 1) * P, :])
            load(Wres[:, k, :], gW_res[k * P:(k + 1) * P, :])
        with nc.allow_non_contiguous_dma(reason="a few small vectors, one element per partition"):
            load(g1[:, 0, :], ln1_g.rearrange("(k p) -> p k", p=P))
            load(g1[:, 1, :], ln1_b.rearrange("(k p) -> p k", p=P))
        load(att[:, 0, :], att_src.rearrange("h d -> (h d)").unsqueeze(0).to_broadcast([P, D]))
        load(att[:, 1, :], att_dst.rearrange("h d -> (h d)").unsqueeze(0).to_broadcast([P, D]))
        weights_loaded = load(bias_b, g_bias.unsqueeze(0).to_broadcast([P, D]))

        wait(dve, weights_loaded)
        for k in range(KC):
            for s in range(2):
                t = vA.mark(dve.tensor_tensor(att_tmp, Wc[:, k, 0:D], att[:, s, :], ALU.mult))
                wait(dve, t)
                t_att = vA.mark(dve.tensor_reduce(Wc[:, k, D + s * HEADS:D + (s + 1) * HEADS],
                                                  att_tmp.rearrange("p (h d) -> p h d", d=HD),
                                                  AX.X, ALU.add))
                wait(dve, t_att)
        t_wc = t_att
        t_ones = vA.mark(dve.memset(win[:, :, 0:AGG].rearrange("p w (h c) -> p w h c", c=HC)[:, :, :, HD:HC], 1.0))
        wait(dve, t_ones)
        vA.mark(dve.memset(win[:, NT, :], 0.0))
        def norm_steps(dsts, srcs, c, ready, done, which=0):
            n = len(srcs)
            stats, mv, rstd = norm_bufs[which]
            wait(dve, ready)
            for j, xt in enumerate(srcs):
                t = c.mark(dve.bn_stats(stats[:, j, :], xt))
            wait(dve, t)
            for j in range(n):
                t = c.mark(dve.bn_aggr(mv[:, j, :], stats[:, j, :]))
            wait(dve, t)
            t = c.mark(dve.tensor_scalar(mv[:, 0:n, 1], mv[:, 0:n, 1], EPS, None, ALU.add))
            wait(pool, t)
            t_pow = c_pool.mark(pool.tensor_tensor(rstd[:, 0:n], mv[:, 0:n, 1], neg_half[:, 0:n], ALU.pow))
            yield
            wait(dve, t_pow)
            for j, (d, xt) in enumerate(zip(dsts, srcs)):
                t = c.mark(dve.tensor_scalar(d, xt, mv[:, j, 0:1], rstd[:, j:j + 1], ALU.subtract, ALU.mult))
            done.append(t)

        def tiles_of(b):
            return min(4, NT - 4 * b)

        x_free, xnT_free, res_free = [None] * 3, [None] * 2, [None] * 2
        loadedA, normedA = {}, {}

        def a_load(b):
            n, buf = tiles_of(b), xs[b % 3]
            wait(sp, x_free[b % 3])
            if b == NB - 1:
                wait(dve, x_free[b % 3])
                t = vA.mark(dve.memset(buf[:, n - 1, :], 0.0))
                wait(sp, t)
                if n > 1:
                    c_x[b % 3].mark(sp.dma_start(buf[:, 0:n - 1, :], x[4 * b * P:(NT - 1) * P, :].rearrange("(t p) d -> p t d", p=P)), 16)
                loadedA[b] = c_x[b % 3].mark(sp.dma_start(buf[0:last_rows, n - 1, :], x[(NT - 1) * P:N, :]), 16)
            else:
                loadedA[b] = c_x[b % 3].mark(sp.dma_start(buf[:, 0:n, :], x[4 * b * P:(4 * b + n) * P, :].rearrange("(t p) d -> p t d", p=P)), 16)

        def a_norm(b):
            tiles, done = [xs[b % 3][:, j, :] for j in range(tiles_of(b))], [loadedA[b]]
            yield from norm_steps(tiles, tiles, vA, done[-1], done)
            yield from norm_steps(tiles, tiles, vA, done[-1], done)
            normedA[b] = done[-1]

        bank_free = [None] * 8
        xnT_ready = {}

        def a_turn(b):
            n, buf = tiles_of(b), xs[b % 3]
            wait(pe, normedA[b], ident_ready)
            for k in range(KC):
                bk = k
                wait(pe, bank_free[bk])
                for j in range(n):
                    ins = pe.transpose(bank[bk][:, j * P:(j + 1) * P], buf[:, j, k * P:(k + 1) * P], ident[:, :])
                t = pA.mark(ins)
                wait(act, t, weights_loaded, xnT_free[b % 2])
                xnT_ready[b] = bank_free[bk] = aA.mark(act.activation(
                    xnT[b % 2][:, k, 0:n * P], bank[bk][:, 0:n * P], ACT.Identity,
                    scale=g1[:, 0, k:k + 1], bias=g1[:, 1, k:k + 1]))
            x_free[b % 3] = t

        def a_project(b, between):
            n = tiles_of(b)
            wait(pe, xnT_ready[b], t_wc)
            wait(act, t_ones)
            for j in range(n):
                w = 4 * b + j
                bh, br_ = 2 + (w % 3), 5 + (w % 3)
                wait(pe, bank_free[bh])
                for k in range(KC):
                    ins = pe.matmul(bank[bh][:, 0:D + 2 * HEADS], xnT[b % 2][:, k, j * P:(j + 1) * P],
                                    Wc[:, k, :], start=(k == 0), stop=(k == KC - 1))
                t_h = pA.mark(ins)
                wait(pe, bank_free[br_])
                for k in range(KC):
                    ins = pe.matmul(bank[br_][:, 0:D], xnT[b % 2][:, k, j * P:(j + 1) * P],
                                    Wres[:, k, :], start=(k == 0), stop=(k == KC - 1))
                t_r = pA.mark(ins)
                wait(act, t_h)
                aA.mark(act.copy(win[:, w, 0:AGG].rearrange("p (h c) -> p h c", c=HC)[:, :, 0:HD],
                                 bank[bh][:, 0:D].rearrange("p (h d) -> p h d", d=HD)))
                t_w = bank_free[bh] = aA.mark(act.copy(win[:, w, AGG:WROW], bank[bh][:, D:D + 2 * HEADS]))
                wait(dve, t_r, res_free[b % 2] if j == 0 else None)
                t_rs = bank_free[br_] = vA.mark(dve.tensor_tensor(res_st[b % 2][:, j, :], bank[br_][:, 0:D], bias_b, ALU.add))
                next(between, None)
            xnT_free[b % 2] = t_r
            wait(sp, t_w, t_ones)
            rows = slice(4 * b * P, (4 * b + n) * P)
            c_tab.mark(sp.dma_start(node_table[rows, :].rearrange("(t p) c -> p t c", p=P),
                                    win[:, 4 * b:4 * b + n, 0:ROW]), 16)
            wait(sp, t_rs)
            c_r = c_resb[b % 2]
            res_free[b % 2] = c_r.mark(sp.dma_start(residual[rows, :].rearrange("(t p) c -> p t c", p=P),
                                                    res_st[b % 2][:, 0:n, :]), 16)

        c_resb = [counter(f"residual_written{i}") for i in range(2)]

        dst_rows = dst.rearrange("(b e) -> b e", e=EB)
        src_rows = src.rearrange("(b e) -> b e", e=EB)
        PB0 = OH0
        first = part(PB0, NEB).bitcast(I32)
        first_w = part(PB0 + 400, NEB)
        iota_b = part(PB0 + 800, 400).bitcast(I32)
        le = part(PB0 + 1200, NEB)
        count = sb("count", [P, 4 * 5])
        kcol = sb("kcol", [P, NK], I32)
        tk_i = sb("tk_i", [P, NK], I32)
        wk_i = sb("wk_i", [P, NK], I32)
        rows_i = part(PB0 + 1600, NK, EB).bitcast(I32)
        rows_s = part(PB0 + 1600 + NK * EB, NK, EB)
        rows_d = part(PB0 + 1600 + 2 * NK * EB, NK, EB + 2)
        rows_n = part(PB0 + 1600 + 3 * NK * EB + 16, NK, EB)
        assert PB0 + 1600 + 4 * NK * EB + 16 <= OT0 + 2 * GT * P
        c_rows = counter("step_rows")
        c_scr = counter("step_scratch")

        def b_prep():
            with nc.allow_non_contiguous_dma(reason="one element per edge block"):
                t_f = load(first[0:1, :], dst_rows[:, 0:1].rearrange("b o -> o b"), c_prep)
            t_i1 = c_pool.mark(pool.iota(iota_b[0:1, 0:NEB], pattern=[[1, NEB]], base=0, channel_multiplier=0))
            t_i2 = c_pool.mark(pool.iota(kcol[:, :], pattern=[[P, NK]], base=0, channel_multiplier=1))
            wait(dve, t_f, t_i1, t_i2)
            t = vB.mark(dve.tensor_single_scalar(first[0:1, :], first[0:1, :], 7, ALU.arith_shift_right))
            wait(dve, t)
            t = vB.mark(dve.tensor_scalar(first_w[0:1, :], first[0:1, :], float(NT - 1), None, ALU.min))
            wait(dve, t)
            t = vB.mark(dve.memset(first_w[0:1, 0:1], 0.0))
            wait(dve, t)
            t = vB.mark(dve.tensor_tensor(first_w[0:1, :], first_w[0:1, :], iota_b[0:1, 0:NEB], ALU.add))
            wait(pe, t, ident_ready, bank_free[7])
            t = pB.mark(pe.matmul(bank[7][:, 0:NEB], ones[0:1, :], first_w[0:1, :], start=True, stop=True))
            wait(dve, t)
            yield
            kf, tf, wf = count[:, 0:NK], count[:, NK:2 * NK], count[:, 2 * NK:3 * NK]
            t = vB.mark(dve.tensor_copy(kf, kcol[:, :]))
            wait(dve, t)
            for c in range(NK):
                t = vB.mark(dve.tensor_scalar(le, bank[7][:, 0:NEB], kf[:, c:c + 1], None, ALU.is_le))
                wait(dve, t)
                t = vB.mark(dve.tensor_reduce(tf[:, c:c + 1], le, AX.X, ALU.add))
                wait(dve, t)
            bank_free[7] = t
            yield
            t = vB.mark(dve.tensor_scalar(tf, tf, -1.0, None, ALU.add))
            wait(dve, t)
            t_tk = vB.mark(dve.tensor_copy(tk_i[:, :], tf))
            t = vB.mark(dve.tensor_tensor(wf, kf, tf, ALU.subtract))
            wait(dve, t)
            t_wk = vB.mark(dve.tensor_copy(wk_i[:, :], wf))
            t_w128 = vB.mark(dve.tensor_scalar(kf, wf, float(P), None, ALU.mult))
            wait(sp, t_wk)
            with nc.allow_non_contiguous_dma(reason="one element per step"):
                t = load(step_win.rearrange("(c p) o -> p (c o)", p=P), wk_i[:, :], c_prep)
                wait(sp, t)
                t_win = load(win_row[:, :], step_win[0:NSTEP, :].rearrange("k o -> o k"), c_prep)
            yield
            wr = win_row[:, :].rearrange("o (g k) -> o g k", k=GS)
            wait(dve, t_win)
            t = vB.mark(dve.tensor_tensor(win_delta[:, :, 1:GS], wr[:, :, 1:GS], wr[:, :, 0:1].to_broadcast([1, NG, GS - 1]), ALU.subtract))
            t = vB.mark(dve.tensor_copy(win_word[:, :], wr[:, :, 0]))
            wait(dve, t)
            for k in range(1, GS):
                t = vB.mark(dve.tensor_single_scalar(win_delta[:, :, k], win_delta[:, :, k], 3 + 3 * k, ALU.logical_shift_left))
                wait(dve, t)
                t = vB.mark(dve.tensor_tensor(win_word[:, :], win_word[:, :], win_delta[:, :, k], ALU.bitwise_or))
                wait(dve, t)
            t_win = t
            yield
            wait(pool, t_tk)
            for c in range(NK):
                c_rows.mark(pool.indirect_dma_start(rows_i[:, c, :], None, dst_rows, bass.IndirectOffsetOnAxis(ap=tk_i[:, c:c + 1], axis=0)), 16)
                t = c_rows.mark(pool.indirect_dma_start(rows_s[:, c, :].bitcast(I32), None, src_rows, bass.IndirectOffsetOnAxis(ap=tk_i[:, c:c + 1], axis=0)), 16)
            yield
            wait(dve, t, t_w128)
            t = vB.mark(dve.memset(rows_d[:, :, :], -1.0e6))
            wait(dve, t)
            for c in range(NK):
                t = vB.mark(dve.tensor_scalar(rows_d[:, c, 1:EB + 1], rows_i[:, c, :], kf[:, c:c + 1], None, ALU.subtract))
            wait(dve, t)
            src_f = rows_i[:, :, :].bitcast(F32)
            t_sf = vB.mark(dve.tensor_copy(src_f, rows_s.bitcast(I32)))
            for c in range(NK):
                t = vB.mark(dve.tensor_tensor(rows_n[:, c, :], rows_d[:, c, 1:EB + 1], rows_d[:, c, 0:EB], ALU.not_equal))
            wait(dve, t)
            t_new = vB.mark(dve.tensor_scalar(rows_n, rows_n, -BIG, None, ALU.mult))
            wait(sp, t_new)
            t = load(step_new.rearrange("(c p) e -> p c e", p=P), rows_n, c_scr)
            yield
            def columns(source, target, ready):
                for i in range(NK * 2):
                    c, j = i // 2, i % 2
                    bk = i % 2
                    wait(pe, ready, bank_free[bk])
                    tt = pB.mark(pe.transpose(bank[bk][:, 0:P], source(c, j), ident[:, :]))
                    wait(dve, tt)
                    bank_free[bk] = vB.mark(dve.tensor_copy(target[:, c * P:(c + 1) * P, j], bank[bk][:, 0:P]))
                return bank_free[bk]

            t_s = columns(lambda c, j: src_f[:, c, j * P:(j + 1) * P], src_col, t_sf)
            yield
            columns(lambda c, j: rows_d[:, c, 1 + j * P:1 + (j + 1) * P], dst_col, t_sf)
            yield
            wait(dve, t)
            for c in range(NK):
                t_l = vB.mark(dve.tensor_tensor(rows_n[:, c, :], rows_d[:, c, 1:EB + 1], rows_d[:, c, 2:EB + 2], ALU.not_equal))
            wait(sp, t_l)
            t_scr = load(step_last.rearrange("(c p) e -> p c e", p=P), rows_n, c_scr)
            yield
            t_lc = columns(lambda c, j: rows_n[:, c, j * P:(j + 1) * P], last_col, t_l)
            prepared.update(win=t_win, scratch=t_scr, src=t_s, cols=t_lc)

        prepared, prep = {}, b_prep()
        for i in range(NB + 2):
            if i < NB:
                a_load(i)
            norm = a_norm(i - 1) if 1 <= i <= NB else iter(())
            next(norm, None)
            if i >= 2:
                a_project(i - 2, norm)
            for _ in norm:
                pass
            if 1 <= i <= NB:
                a_turn(i - 1)
            next(prep, None)
        for _ in prep:
            pass
        t_win, t_scr, t_srccol, t_cols = (prepared[k] for k in ("win", "scratch", "src", "cols"))
        table_written = (c_tab.sem, c_tab.value)
        node_phase_done = [(vA.sem, vA.value), (pA.sem, pA.value), (aA.sem, aA.value), res_free[0], res_free[1]]

        seg_new = [sb(f"seg_new{i}", [HEADS * GS, EB]) for i in range(2)]
        seg_last = [sb(f"seg_last{i}", [HEADS * GS, EB]) for i in range(2)]
        seg_max = sb("seg_max", [HEADS * GS, EB])
        asrc = sb("asrc", [P, 2, GS, HEADS])
        cand = sb("cand", [P, 3, 2, GS, HEADS + 1], BF16)
        cand_rest = sb("cand_rest", [P, 2, GS, HEADS])
        old = sb("old", [P, GS, 2 * HEADS])
        newm = sb("newm", [P, GS, HEADS])
        nodeval = sb("nodeval", [P, GS, 2 * HEADS])
        parts = sb("parts", [P, 3, GS, 2 * HEADS], BF16)
        rest = sb("rest", [P, GS, 2 * HEADS])
        shift0 = sb("shift0", [P, GS, HEADS])
        absent = sb("absent", [P, GS])
        scale = [sb(f"scale{i}", [P, GS, HEADS]) for i in range(2)]
        score = sb("score", [P, GT, HEADS])
        wgt = sb("wgt", [P, GT, HEADS])
        c_g = [counter(f"gathered{i}") for i in range(NGB)]
        c_seg = [counter(f"segments{i}") for i in range(2)]
        gath_free, oh_free, oh16_free, oh32_ready = [None] * NGB, [None] * 2, [None] * 2, {}
        gathered, seg_loaded, seg_free = {}, {}, [None] * 2
        b_asrc, b_cand, b_ms, b_edge = bank[0], bank[0], bank[1], bank[2]
        oh_ready, oht_ready, oht_free = {}, {}, [None] * 2
        ohp_free, agp_free = [None] * 2, [None] * 3
        msg_ready, scale_ready, scale_free, words = {}, {}, [None] * 2, {}
        S = {}

        def fetch(g):
            if g == 0:
                wait(pool, table_written, t_srccol, *node_phase_done)
                wait(sp, t_scr)
            wait(pool, gath_free[g % NGB])
            for t in range(GT):
                k = g * GS + t // 2
                gathered[g] = c_g[g % NGB].mark(pool.indirect_dma_start(
                    gath[g % NGB][:, t, :], None, node_table,
                    bass.IndirectOffsetOnAxis(ap=src_col[:, k, t % 2:t % 2 + 1], axis=0)), 16)
            wait(sp, seg_free[g % 2])
            rows = slice(g * GS, (g + 1) * GS)
            c_seg[g % 2].mark(sp.dma_start(seg_new[g % 2][:, :], step_new[rows, :].unsqueeze(1).to_broadcast([GS, HEADS, EB])), 16)
            seg_loaded[g] = c_seg[g % 2].mark(sp.dma_start(seg_last[g % 2][:, :], step_last[rows, :].unsqueeze(1).to_broadcast([GS, HEADS, EB])), 16)

        def one_hots(g):
            wait(act, oh16_free[g % 2], oh32_ready.get(g - 2))
            for t in range(GT):
                k = g * GS + t // 2
                ins = act.activation(onehot16[g % 2][:, t, :], iota16[:, :], ACT.Abs, scale=-1.0,
                                     bias=dst_col[:, k, t % 2:t % 2 + 1])
            wait(act, aC.mark(ins))
            oh_ready[g] = aC.mark(act.activation(onehot16[g % 2], onehot16[g % 2], ACT.Relu, scale=-1.0, bias=ones[:, 0:1]))

        def turn_one_hots(g):
            wait(pe, oh_ready[g])
            wait(act, oht_free[g % 2])
            for q in range(2):
                wait(pe, ohp_free[q])
                turned = bank[3 + q][:, :].bitcast(BF16)
                for j in range(GT // 2):
                    ins = pe.transpose(turned[:, j * P:(j + 1) * P], onehot16[g % 2][:, q * GT // 2 + j, :], ident16[:, :])
                t = pC.mark(ins)
                wait(act, t)
                oht_ready[g] = ohp_free[q] = aC.mark(act.copy(
                    onehot_t[g % 2][:, q * GT // 2:(q + 1) * GT // 2, :], turned.rearrange("p (t n) -> p t n", n=P)))

        def widen_one_hots(g):
            wait(act, oh_ready[g], oh_free[g % 2])
            oh32_ready[g] = aC.mark(act.copy(onehot[g % 2], onehot16[g % 2]))

        def take_asrc(g):
            gb = gath[g % NGB].rearrange("p (k j) c -> p k j c", j=2)
            wait(act, gathered[g], S.get("asrc_turned"))
            t = aC.mark(act.copy(asrc[:, :, :, :], gb[:, :, :, AGG:ROW].rearrange("p k j h -> p j k h")))
            wait(pe, t, S.get("cand_read"))
            for j in range(2):
                ins = pe.transpose(b_asrc[0:HEADS * GS, j * P:(j + 1) * P], asrc[:, j, :, :].rearrange("p k h -> p (k h)"), ident[:, :])
            S["asrc_turned"] = pC.mark(ins)

        def seg_scan(g):
            wait(dve, S["asrc_turned"], seg_loaded[g], S.get("cand_turned"))
            S["scanned"] = vC.mark(dve.tensor_tensor_scan(seg_max[:, :], seg_new[g % 2][:, :], b_asrc[0:HEADS * GS, 0:EB], -BIG, ALU.add, ALU.max))

        def seg_mask(g):
            wait(dve, S["scanned"])
            S["masked"] = seg_free[g % 2] = vC.mark(dve.tensor_tensor(seg_max[:, :], seg_max[:, :], seg_last[g % 2][:, :], ALU.mult))

        def seg_turn(g):
            wait(pe, S["masked"])
            for j in range(2):
                ins = pe.transpose(b_cand[:, EB + j * 64:EB + (j + 1) * 64], seg_max[:, j * P:(j + 1) * P], ident[0:64, 0:64])
            S["cand_turned"] = t = pC.mark(ins)
            wait(act, S.get("ms_done"))
            aC.mark(act.copy(cand[:, 0, :, :, HEADS:HEADS + 1],
                             last_col[:, g * GS:(g + 1) * GS, :].rearrange("p k j -> p j k").unsqueeze(3)))
            values = b_cand[:, EB:EB + P].rearrange("p (j k h) -> p j k h", j=2, k=GS)
            wait(act, t)
            t = aC.mark(act.copy(cand[:, 0, :, :, 0:HEADS], values))
            S["cand_high"] = t

        def cand_middle(g):
            values = b_cand[:, EB:EB + P].rearrange("p (j k h) -> p j k h", j=2, k=GS)
            wait(dve, S["cand_high"])
            t = S["cand_read"] = vC.mark(dve.tensor_tensor(cand_rest[:, :, :, :], values, cand[:, 0, :, :, 0:HEADS], ALU.subtract))
            wait(act, t)
            S["cand_middle"] = aC.mark(act.copy(cand[:, 1, :, :, 0:HEADS], cand_rest[:, :, :, :]))

        def cand_low(g):
            wait(dve, S["cand_middle"])
            S["cand_split"] = vC.mark(dve.tensor_tensor(cand[:, 2, :, :, 0:HEADS], cand_rest[:, :, :, :], cand[:, 1, :, :, 0:HEADS], ALU.subtract))

        def node_maxima(g):
            wait(pe, S["cand_split"], S.get("ms_read"))
            for k in range(GS):
                for j in range(2):
                    for i in range(3):
                        ins = pe.matmul(b_ms[:, k * 9:(k + 1) * 9], onehot16[g % 2][:, 2 * k + j, :], cand[:, i, j, k, :],
                                        start=(i == j == 0), stop=(j == 1 and i == 2))
            S["ms_done"] = pC.mark(ins)
            oh16_free[g % 2] = S["ms_done"]

        def window(g, k):
            if g not in words:
                words[g] = dve.value_load(win_word[0:1, g:g + 1], min_val=0, max_val=(1 << 27) - 1)
            w = words[g] & 63
            if k:
                w = w + ((words[g] >> (3 + 3 * k)) & 7)
            return nc.s_assert_within(w, 0, WIN - 1, skip_runtime_bounds_check_because="a step's window is at most WIN - 1")

        late_tiles = {k: (3 * GT // 4 + k, 3 * GT // 4 + k + 1) for k in range(GT // 4)}

        def node_maximum(g):
            ms = b_ms[:, 0:9 * GS].rearrange("p (k c) -> p k c", c=9)
            window(g, 0)
            wait(dve, S["ms_done"])
            t = vC.mark(dve.tensor_scalar(absent[:, :], ms[:, :, HEADS], BIG, -BIG, ALU.mult, ALU.add))
            wait(dve, t)
            t = S["ms_read"] = vC.mark(dve.tensor_tensor(newm[:, :, :], ms[:, :, 0:HEADS], absent[:, :].unsqueeze(2).to_broadcast([P, GS, HEADS]), ALU.add))
            for k in range(GS):
                w = window(g, k)
                values, maxima = win[:, w, AGG:WROW], win[:, w, AGG:ROW]
                wait(dve, t)
                t_copy = vC.mark(dve.tensor_copy(old[:, k, :], values))
                yield
                wait(dve, t_copy)
                t = S["max_done"] = vC.mark(dve.tensor_tensor(maxima, maxima, newm[:, k, :], ALU.max))
                yield

        def node_shifts(g):
            wait(dve, S["max_done"], S.get("edge_vals"))
            t = vC.mark(dve.tensor_tensor(newm[:, :, :], newm[:, :, :], old[:, :, 0:HEADS], ALU.max))
            t2 = vC.mark(dve.tensor_copy(nodeval[:, :, 0:HEADS], old[:, :, HEADS:2 * HEADS]))
            yield
            wait(dve, t2)
            for m in (newm[:, :, :], old[:, :, 0:HEADS]):
                t = vC.mark(dve.tensor_tensor(m, m, nodeval[:, :, 0:HEADS], ALU.add))
            yield
            wait(dve, t)
            vC.mark(dve.scalar_tensor_tensor(nodeval[:, :, HEADS:2 * HEADS], newm[:, :, :], SLOPE, newm[:, :, :], ALU.mult, ALU.max))
            t_s0 = vC.mark(dve.scalar_tensor_tensor(shift0[:, :, :], old[:, :, 0:HEADS], SLOPE, old[:, :, 0:HEADS], ALU.mult, ALU.max))
            yield
            wait(dve, t_s0)
            t = vC.mark(dve.tensor_copy(parts[:, 0, :, :], nodeval[:, :, :]))
            wait(dve, scale_free[g % 2])
            S["scale_taken"] = vC.mark(dve.tensor_tensor(scale[g % 2][:, :, :], shift0[:, :, :], nodeval[:, :, HEADS:2 * HEADS], ALU.subtract))
            yield
            wait(dve, t)
            t = vC.mark(dve.tensor_tensor(rest[:, :, :], nodeval[:, :, :], parts[:, 0, :, :], ALU.subtract))
            yield
            wait(dve, t)
            t = vC.mark(dve.tensor_copy(parts[:, 1, :, :], rest[:, :, :]))
            yield
            wait(dve, t)
            S["parts"] = vC.mark(dve.tensor_tensor(parts[:, 2, :, :], rest[:, :, :], parts[:, 1, :, :], ALU.subtract))

        def shifts(g):
            def chain():
                if g < NG:
                    yield from node_maximum(g)
                    yield from node_shifts(g)

            small = chain()
            next(small, None)
            for k in range(GS if g > 0 else 0):
                if k in late_tiles:
                    messages(g - 1, *late_tiles[k])
                    next(small, None)
                scale_sums(g - 1, k)
                next(small, None)
                add_sums(g - 1, k)
                next(small, None)
            for _ in small:
                pass

        def scales(g):
            wait(act, S["scale_taken"])
            scale_ready[g] = aC.mark(act.activation(scale[g % 2][:, :, :], scale[g % 2][:, :, :], ACT.Exp))

        def edge_values(g):
            wait(pe, S["parts"], oht_ready[g], S.get("score_read"))
            for t in range(GT):
                for i in range(3):
                    ins = pe.matmul(b_edge[:, t * 16:(t + 1) * 16], onehot_t[g % 2][:, t, :], parts[:, i, t // 2, :],
                                    start=(i == 0), stop=(i == 2))
            S["edge_vals"] = oht_free[g % 2] = pC.mark(ins)

        def scores(g):
            gb = gath[g % NGB]
            ev = b_edge[:, 0:16 * GT].rearrange("p (t c) -> p t c", c=16)
            wait(dve, S["edge_vals"], gathered[g], S.get("exp_done"))
            t = vC.mark(dve.tensor_tensor(score[:, :, :], gb[:, :, AGG:ROW], ev[:, :, 0:HEADS], ALU.add))
            wait(dve, t)
            t = vC.mark(dve.scalar_tensor_tensor(score[:, :, :], score[:, :, :], SLOPE, score[:, :, :], ALU.mult, ALU.max))
            wait(dve, t)
            t = S["score_read"] = vC.mark(dve.tensor_tensor(score[:, :, :], score[:, :, :], ev[:, :, HEADS:16], ALU.subtract))
            wait(act, t, S.get("weighted"))
            S["exp_done"] = aC.mark(act.activation(wgt[:, :, :], score[:, :, :], ACT.Exp))

        def messages(g, first, end):
            wait(dve, S["exp_done"])
            r = slice(first, end)
            rows = gath[g % NGB][:, r, 0:AGG].rearrange("p t (h c) -> p t h c", c=HC)
            S["weighted"] = vC.mark(dve.tensor_tensor(
                rows, rows, wgt[:, r, :].unsqueeze(3).to_broadcast([P, end - first, HEADS, HC]), ALU.mult))
            for t in range(first, end):
                msg_ready[g, t] = S["weighted"]

        def sum_messages(g, k):
            bk = bank[5 + (g * GS + k) % 3]
            wait(pe, msg_ready[g, 2 * k + 1], oh32_ready[g], agp_free[(g * GS + k) % 3])
            for j in range(2):
                ins = pe.matmul(bk[:, 0:AGG], onehot[g % 2][:, 2 * k + j, :], gath[g % NGB][:, 2 * k + j, 0:AGG],
                                start=(j == 0), stop=(j == 1))
            S["sum", g, k] = pC.mark(ins)
            if k == GS - 1:
                gath_free[g % NGB] = oh_free[g % 2] = S["sum", g, k]

        def scale_sums(g, k):
            S["window"] = window(g, k)
            rows = win[:, S["window"], 0:AGG].rearrange("p (h c) -> p h c", c=HC)
            wait(dve, scale_ready[g], S.get("added"))
            S["scaled"] = vC.mark(dve.tensor_tensor(rows, rows, scale[g % 2][:, k, :].unsqueeze(2).to_broadcast([P, HEADS, HC]), ALU.mult))

        def add_sums(g, k):
            bk = bank[5 + (g * GS + k) % 3]
            sum_messages(g, k)
            row = win[:, S["window"], 0:AGG]
            wait(dve, S["scaled"], S["sum", g, k])
            S["added"] = agp_free[(g * GS + k) % 3] = vC.mark(dve.tensor_tensor(row, row, bk[:, 0:AGG], ALU.add))
            if k == GS - 1:
                scale_free[g % 2] = S["added"]

        t = vC.mark(dve.memset(cand[:, 1:3, :, :, HEADS:HEADS + 1], 0.0))
        wait(pe, t)
        wait(dve, table_written, t_win, t_cols, t_scr, *node_phase_done)
        wait(act, t_cols)
        c_small = counter("small_weights")
        load(br_b[:, :], br.unsqueeze(0).to_broadcast([P, E]), c_small)
        for k in range(KC):
            load(wr_sb[:, k, :], Wr[k * P:(k + 1) * P, :], c_small)
        with nc.allow_non_contiguous_dma(reason="small vectors, one element per partition"):
            load(g2[:, 0, :], ln2_g.rearrange("(k p) -> p k", p=P), c_small)
            load(g2[:, 1, :], ln2_b.rearrange("(k p) -> p k", p=P), c_small)
            load(fb1[:, :], f_b1.rearrange("(m p) -> p m", p=P), c_small)
            for e in range(E):
                load(epar[:, e, 0:KC], ln_g[e, :].rearrange("(k p) -> p k", p=P), c_small)
                load(epar[:, e, KC:2 * KC], ln_b[e, :].rearrange("(k p) -> p k", p=P), c_small)
                t_small = load(epar[:, e, 2 * KC:], b1[e, :].rearrange("(m p) -> p m", p=P), c_small)
        for g in range(-1, NG + 1):
            if g == -1:
                fetch(0)
            if g + 2 < NG:
                fetch(g + 2)
            if g + 1 < NG:
                one_hots(g + 1)
            if g >= 0:
                shifts(g)
            if g + 1 < NG:
                turn_one_hots(g + 1)
                take_asrc(g + 1)
            if 0 <= g < NG:
                scales(g)
                edge_values(g)
            if g + 1 < NG:
                seg_scan(g + 1)
                seg_mask(g + 1)
                seg_turn(g + 1)
            if 0 <= g < NG:
                scores(g)
            if g + 1 < NG:
                cand_middle(g + 1)
            if 0 <= g < NG:
                messages(g, 0, GT // 4)
            if g + 1 < NG:
                cand_low(g + 1)
            if 0 <= g < NG:
                messages(g, GT // 4, GT // 2)
                messages(g, GT // 2, 3 * GT // 4)
            if g + 1 < NG:
                node_maxima(g + 1)
            if 0 <= g < NG:
                widen_one_hots(g)
        edges_done = [(vC.sem, vC.value), (pC.sem, pC.value), (aC.sem, aC.value)]

        def split_product(out_ap, stationary, moving, first, last):
            (s_hi, s_lo), (m_hi, m_lo) = stationary, moving
            for a, b, start, stop in ((s_hi, m_lo, first, False), (s_lo, m_hi, False, False), (s_hi, m_hi, False, last)):
                ins = pe.matmul(out_ap, a, b, start=start, stop=stop)
            return ins

        def low(eng, lo, full, hi):
            return eng.tensor_tensor(lo, full, hi.bitcast(F32), ALU.subtract)

        phase_memory()
        layer_mem = sb("layer_mem", [P, 32 * D + KC * 512 + 4 * 512 + 3 * D])
        rows = [cut(layer_mem, 4 * i * D, 4, D) for i in range(2)]
        zrow = cut(layer_mem, 8 * D, 4, D)
        outT_full = cut(layer_mem, 12 * D, KC, 512)
        fw1_full, fw2_full = cut(layer_mem, 0, KC, HID), cut(layer_mem, KC * HID, MC, D)
        res_in, x_in = [[cut(layer_mem, 16 * D + (8 * s_ + 4 * i) * D, 4, D) for i in range(2)] for s_ in range(2)]
        o = 32 * D
        zT = cut(layer_mem, o, KC, 512)
        o += KC * 512
        hid_full = [cut(layer_mem, o + i * 512, 512) for i in range(4)]
        o += 4 * 512
        ln2_gb = cut(layer_mem, o, 2, D)
        fb2_b = cut(layer_mem, o + 2 * D, D)
        rounded = sb("layer_rounded", [P, 4 * MC * 512 + 2 * KC * 512], F32R)
        hid_hi, hid_lo = [cut(rounded, i * MC * 512, MC, 512) for i in range(2)]
        o = 2 * MC * 512
        fw1_hi, fw1_lo = [cut(rounded, o + i * KC * HID, KC, HID) for i in range(2)]
        o += 2 * KC * HID
        fw2_hi, fw2_lo = [cut(rounded, o + i * MC * D, MC, D) for i in range(2)]
        o += 2 * MC * D
        out_hi, out_lo = [cut(rounded, o + i * KC * 512, KC, 512) for i in range(2)]
        rec = sb("rec", [P, 4, HEADS])
        prob, top8, place = (sb(name, [P, 4, E]) for name in ("prob", "top8", "place"))
        idx8 = sb("idx8", [P, 4, E], U32)
        sel = sb("sel", [P, 4, 2, E])
        both = sb("both", [P, 4, E], BF16)
        tok = sb("tok", [P, 4, 4])
        ids = sb("ids", [P, NT], I32)
        valid = sb("valid", [P, 1])
        tri = sb("tri", [P, P])
        tri16, ones16 = sb("tri16", [P, P], BF16), sb("ones16", [P, P], BF16)
        c_disp = [counter(f"dispatched{i}") for i in range(2)]
        pos_free = [None] * 2
        c_w2 = counter("layer_weights")
        vD, aD, pD = counter("dve_layer"), counter("act_layer"), counter("pe_layer")
        c_in = [counter(f"layer_in{i}") for i in range(2)]
        c_x1 = [counter(f"x1_written{i}") for i in range(2)]

        POOL_HID = (0, 5)
        in_free, x1_free = [None] * 2, [None] * 2
        D_ = {}

        def d_load(b):
            n, i = tiles_of(b), b % 2
            wait(sp, in_free[i])
            r = slice(4 * b * P, (4 * b + n) * P)
            c_in[i].mark(sp.dma_start(res_in[i][:, 0:n, :], residual[r, :].rearrange("(t p) d -> p t d", p=P)), 16)
            if b == NB - 1:
                wait(dve, in_free[i])
                wait(sp, vD.mark(dve.memset(x_in[i][:, n - 1, :], 0.0)))
                if n > 1:
                    c_in[i].mark(sp.dma_start(x_in[i][:, 0:n - 1, :], x[4 * b * P:(NT - 1) * P, :].rearrange("(t p) d -> p t d", p=P)), 16)
                D_["in", b] = c_in[i].mark(sp.dma_start(x_in[i][0:last_rows, n - 1, :], x[(NT - 1) * P:N, :]), 16)
            else:
                D_["in", b] = c_in[i].mark(sp.dma_start(x_in[i][:, 0:n, :], x[r, :].rearrange("(t p) d -> p t d", p=P)), 16)

        assert 16 * D <= GT * ROW and 32 * D <= 2 * GT * ROW
        wait(sp, gath_free[0])
        for k in range(KC):
            load(fw1_full[:, k, :], f_w1[k * P:(k + 1) * P, :], c_w2)
        t_fw = load(fw2_full, f_w2.rearrange("(m p) d -> p m d", p=P), c_w2)
        wait(sp, gath_free[1])
        d_load(0)
        wait(sp, *edges_done)
        c_gb = counter("layer_vectors")
        load(ln2_gb[:, 0, :], ln2_g.unsqueeze(0).to_broadcast([P, D]), c_gb)
        load(ln2_gb[:, 1, :], ln2_b.unsqueeze(0).to_broadcast([P, D]), c_gb)
        t_gb = load(fb2_b, f_b2.unsqueeze(0).to_broadcast([P, D]), c_gb)
        wait(dve, t_small, *edges_done)
        wait(act, t_fw, t_small, *edges_done)
        wait(pe, t_small, *edges_done)
        for full, hi, lo in ((fw1_full, fw1_hi, fw1_lo), (fw2_full, fw2_hi, fw2_lo)):
            t = aD.mark(act.copy(hi, full))
            wait(dve, t)
            t_split = vD.mark(low(dve, lo, full, hi))
        wait(pe, t_split)
        wait(dve, t_gb, t_split)
        t_gb = vD.mark(dve.tensor_tensor(fb2_b, fb2_b, ln2_gb[:, 1, :], ALU.add))
        wait(pool, *edges_done)

        t = c_pool.mark(pool.memset(tri[:, :], 1.0))
        t2 = c_pool.mark(pool.memset(valid[:, :], 1.0))
        c_pool.mark(pool.iota(ids[:, :], pattern=[[P, NT]], base=0, channel_multiplier=1))
        wait(pool, t, t2)
        c_pool.mark(pool.affine_select(out=tri[:, :], in_=tri[:, :], compare_op=ALU.is_gt, fill=0.0,
                                       base=0, pattern=[[1, P]], channel_multiplier=-1))
        t = c_pool.mark(pool.affine_select(out=valid[:, :], in_=valid[:, :], compare_op=ALU.is_gt, fill=0.0,
                                           base=last_rows, pattern=[[0, 1]], channel_multiplier=-1))
        wait(dve, t)
        vD.mark(dve.tensor_copy(tri16[:, :], tri[:, :]))
        vD.mark(dve.tensor_copy(ones16[:, :], ones[:, :]))
        wait(pe, vD.mark(dve.tensor_scalar(filled[:, :], iota_row[:, 0:E], float(CAP), None, ALU.mult)))

        bank_free = [None] * 8
        def d_merge(b):
            n, i = tiles_of(b), b % 2
            wv = win[:, 4 * b:4 * b + n, 0:AGG].rearrange("p t (h c) -> p t h c", c=HC)
            rv = rows[i][:, 0:n, :].rearrange("p t (h d) -> p t h d", d=HD)
            wait(dve, D_.get("rec_used"), x1_free[i])
            t = vD.mark(dve.reciprocal(rec[:, 0:n, :].unsqueeze(3), wv[:, :, :, HD:HC]))
            wait(dve, t)
            t = D_["rec_used"] = vD.mark(dve.tensor_tensor(rv, wv[:, :, :, 0:HD], rec[:, 0:n, :].unsqueeze(3).to_broadcast([P, n, HEADS, HD]), ALU.mult))
            yield
            wait(dve, t, D_["in", b])
            t = vD.mark(dve.tensor_tensor(rows[i][:, 0:n, :], rows[i][:, 0:n, :], res_in[i][:, 0:n, :], ALU.add))
            yield
            tl, done = [rows[i][:, j, :] for j in range(n)], []
            yield from norm_steps(tl, tl, vD, t, done, 1)
            D_["norm", b] = done[-1]

        def turn(src, dst, n, b0, ready, dst_free, full=None):
            wait(pe, ready)
            for k in range(KC):
                bk = b0 + k
                wait(pe, bank_free[bk])
                for j in range(n):
                    ins = pe.transpose(bank[bk][:, j * P:(j + 1) * P], src[:, j, k * P:(k + 1) * P], ident[:, :])
                t_pe = pD.mark(ins)
                wait(act, t_pe, *dst_free)
                if full is not None:
                    for d in (full[:, k, 0:n * P], dst[:, k, 0:n * P]):
                        ins = act.activation(d, bank[bk][:, 0:n * P], ACT.Identity,
                                             scale=g2[:, 0, k:k + 1], bias=g2[:, 1, k:k + 1])
                else:
                    ins = act.copy(dst[:, k, 0:n * P], bank[bk][:, 0:n * P])
                bank_free[bk] = aD.mark(ins)
            return t_pe, bank_free[b0 + KC - 1]

        def d_turn(b):
            n, i = tiles_of(b), b % 2
            t_pe, D_["outT", b] = turn(rows[i], out_hi, n, 0, D_["norm", b],
                                           [D_.get("outT_used"), D_.get("low_taken")], outT_full)
            wait(pool, t_pe, D_["norm", b], t_gb)
            for op, other in ((ALU.mult, ln2_gb[:, 0, :].unsqueeze(1).to_broadcast([P, n, D])),
                              (ALU.add, fb2_b.unsqueeze(1).to_broadcast([P, n, D])),
                              (ALU.add, x_in[i][:, 0:n, :])):
                t = c_pool.mark(pool.tensor_tensor(rows[i][:, 0:n, :], rows[i][:, 0:n, :], other, op))
                wait(pool, t)
            in_free[i] = D_["base", b] = t

        def d_out_low(b):
            n, i = tiles_of(b), b % 2
            wait(dve, D_["outT", b])
            D_["outT", b] = D_["low_taken"] = vD.mark(low(dve, *[a[:, :, 0:n * P] for a in (out_lo, outT_full, out_hi)]))

        def d_ffn(b, between):
            n, i = tiles_of(b), b % 2
            wait(pe, D_["outT", b])
            for m in range(MC):
                bk = (2, 3, 7)[m % 3]
                wait(pe, bank_free[bk])
                for k in range(KC):
                    ins = split_product(bank[bk][:, 0:n * P], [w[:, k, m * P:(m + 1) * P] for w in (fw1_hi, fw1_lo)],
                                        [a[:, k, 0:n * P] for a in (out_hi, out_lo)], k == 0, k == KC - 1)
                t = pD.mark(ins)
                hi, lo, full = hid_hi[:, m, 0:n * P], hid_lo[:, m, 0:n * P], hid_full[m % 4][:, 0:n * P]
                wait(act, t, D_.get("hid_used"), D_.get(("hid_full_used", m % 4)))
                for d in (full, hi):
                    ins = act.activation(d, bank[bk][:, 0:n * P], ACT.Gelu_apprx_tanh, bias=fb1[:, m:m + 1])
                bank_free[bk] = aD.mark(ins)
                eng, c = (pool, c_pool) if m in POOL_HID else (dve, vD)
                wait(eng, bank_free[bk])
                D_["hid", b, m in POOL_HID] = D_["hid_full_used", m % 4] = c.mark(low(eng, lo, full, hi))
                next(between, None)
            D_["outT_used"] = t

        def d_out(b, between):
            n, i = tiles_of(b), b % 2
            wait(pe, D_["hid", b, False], D_["hid", b, True])
            for j in range(n):
                bk = 4 + j % 2
                wait(pe, bank_free[bk])
                for m in range(MC):
                    ins = split_product(bank[bk][:, 0:D], [h[:, m, j * P:(j + 1) * P] for h in (hid_hi, hid_lo)],
                                        [w[:, m, :] for w in (fw2_hi, fw2_lo)], m == 0, m == MC - 1)
                t = pD.mark(ins)
                wait(dve, t, D_["base", b])
                D_["x1", b] = bank_free[bk] = vD.mark(dve.tensor_tensor(rows[i][:, j, :], rows[i][:, j, :], bank[bk][:, 0:D], ALU.add))
                next(between, None)
            D_["hid_used"] = t
            wait(sp, D_["x1", b])
            r = slice(4 * b * P, (4 * b + n) * P)
            x1_free[i] = c_x1[i].mark(sp.dma_start(sums[r, :].rearrange("(t p) d -> p t d", p=P), rows[i][:, 0:n, :]), 16)

        def route_input(b):
            n, i = tiles_of(b), b % 2
            done = []
            wait(dve, D_.get("z_turned"), D_.get("z_used"))
            yield from norm_steps([zrow[:, j, :] for j in range(n)], [rows[i][:, j, :] for j in range(n)], vD, D_["x1", b], done)
            D_["z", b] = done[-1]

        def route_rows(b):
            n, done = tiles_of(b), []
            yield from norm_steps([win[:, 4 * b + j, 0:D] for j in range(n)], [zrow[:, j, :] for j in range(n)],
                                  vD, D_["z", b], done)
            D_["z_used"] = D_["z_used", b] = done[-1]

        def d_logits(b):
            n = tiles_of(b)
            D_["z_turned"], D_["zT"] = turn(zrow, zT, n, 0, D_["z", b], [D_.get("zT_used")])
            wait(pe, D_["zT"], bank_free[6])
            for j in range(n):
                for k in range(KC):
                    ins = pe.matmul(bank[6][:, j * E:(j + 1) * E], zT[:, k, j * P:(j + 1) * P], wr_sb[:, k, :],
                                    start=(k == 0), stop=(k == KC - 1))
            t = D_["zT_used"] = pD.mark(ins)
            wait(dve, t)
            D_["logits"] = t

        def v(ins):
            t = vD.mark(ins)
            wait(dve, t)
            return t

        def gates(b):
            n, w0 = tiles_of(b), 4 * b
            p, idx, s2 = prob[:, 0:n, :], idx8[:, 0:n, :], sel[:, 0:n, :, :]
            wait(dve, D_["logits"])
            bank_free[6] = v(dve.tensor_tensor(p, bank[6][:, 0:n * E].rearrange("p (t e) -> p t e", e=E),
                                               br_b[:, :].unsqueeze(1).to_broadcast([P, n, E]), ALU.add))
            v(dve.tensor_reduce(tok[:, 0, 0:n], p, AX.X, ALU.max))
            t = v(dve.tensor_tensor(p, p, tok[:, 0, 0:n].unsqueeze(2).to_broadcast([P, n, E]), ALU.subtract))
            wait(act, t)
            t_exp = aD.mark(act.activation(p, p, ACT.Exp))
            yield
            wait(dve, t_exp)
            v(dve.tensor_reduce(tok[:, 0, 0:n], p, AX.X, ALU.add))
            v(dve.reciprocal(tok[:, 0, 0:n], tok[:, 0, 0:n]))
            v(dve.tensor_tensor(p, p, tok[:, 0, 0:n].unsqueeze(2).to_broadcast([P, n, E]), ALU.mult))
            for j in range(n):
                t = vD.mark(dve.max(top8[:, j, :], prob[:, j, :]))
            wait(dve, t)
            for j in range(n):
                t = vD.mark(dve.max_index(idx8[:, j, :], top8[:, j, :], prob[:, j, :]))
            wait(dve, t)
            yield
            v(dve.tensor_copy(tok[:, 2:4, 0:n].rearrange("p s t -> p t s"), idx[:, :, 0:2]))
            v(dve.tensor_tensor(s2, iota_row[:, 0:E].unsqueeze(1).unsqueeze(1).to_broadcast([P, n, 2, E]),
                                tok[:, 2:4, 0:n].rearrange("p s t -> p t s").unsqueeze(3).to_broadcast([P, n, 2, E]), ALU.is_equal))
            if b == NB - 1:
                v(dve.tensor_scalar(sel[:, n - 1, :, :], sel[:, n - 1, :, :], valid[:, :], None, ALU.mult))
            v(dve.tensor_tensor(tok[:, 1, 0:n], top8[:, 0:n, 0], top8[:, 0:n, 1], ALU.add))
            v(dve.reciprocal(tok[:, 1, 0:n], tok[:, 1, 0:n]))
            wait(dve, D_.get("counted"))
            D_["both"] = v(dve.tensor_tensor(both[:, 0:n, :], s2[:, :, 0, :], s2[:, :, 1, :], ALU.add))
            v(dve.tensor_tensor(p, p, both[:, 0:n, :], ALU.mult))
            v(dve.tensor_tensor(win[:, w0:w0 + n, D + 1:XROW], p, tok[:, 1, 0:n].unsqueeze(2).to_broadcast([P, n, E]), ALU.mult))
            D_["gated", b] = v(dve.tensor_copy(win[:, w0:w0 + n, D:D + 1].bitcast(I32), ids[:, w0:w0 + n].unsqueeze(2)))

        def d_count(b):
            n = tiles_of(b)
            wait(pe, D_["both"], bank_free[6])
            for j in range(n):
                for i in range(j + 1):
                    pe.matmul(bank[6][:, j * E:(j + 1) * E], (tri16 if i == j else ones16)[:, :], both[:, i, :],
                              start=(i == 0), stop=(i == j))
            for i in range(n):
                ins = pe.matmul(bank[6][:, 4 * E:5 * E], ones16[:, :], both[:, i, :], start=(i == 0), stop=(i == n - 1))
            D_["counted"] = pD.mark(ins)

        def d_dispatch(b):
            n = tiles_of(b)
            pl, s2 = place[:, 0:n, :], sel[:, 0:n, :, :]
            wait(dve, D_["counted"])
            v(dve.tensor_tensor(pl, bank[6][:, 0:n * E].rearrange("p (t e) -> p t e", e=E),
                                filled[:, :].unsqueeze(1).to_broadcast([P, n, E]), ALU.add))
            bank_free[6] = v(dve.tensor_tensor(filled[:, :], filled[:, :], bank[6][:, 4 * E:5 * E], ALU.add))
            v(dve.tensor_tensor(s2, s2, pl.unsqueeze(2).to_broadcast([P, n, 2, E]), ALU.mult))
            v(dve.tensor_reduce(tok[:, 0:2, 0:n].rearrange("p s t -> p t s"), s2, AX.X, ALU.add))
            wait(dve, pos_free[b % 2])
            t = v(dve.tensor_copy(pos[:, b % 2, 0:n, :], tok[:, 0:2, 0:n].rearrange("p s t -> p t s")))
            D_["places", b] = t

        def d_scatter(b):
            n = tiles_of(b)
            wait(pool, D_["places", b], D_["z_used", b], D_["gated", b])
            for j in range(n):
                r = P if 4 * b + j < NT - 1 else last_rows
                for s_ in range(2):
                    pos_free[b % 2] = c_disp[b % 2].mark(pool.indirect_dma_start(
                        expert_rows, bass.IndirectOffsetOnAxis(ap=pos[0:r, b % 2, j, s_:s_ + 1], axis=0),
                        win[0:r, 4 * b + j, 0:XROW], None), 16)

        def beside_ffn(i):
            route, merge, rows2 = iter(()), iter(()), iter(())
            if 2 <= i <= NB + 1:
                route, rows2 = route_input(i - 2), route_rows(i - 2)
                next(route)
            if 3 <= i:
                d_count(i - 3)
            yield
            for _ in route:
                pass
            yield
            if 3 <= i:
                d_dispatch(i - 3)
            yield
            if i < NB:
                merge = d_merge(i)
                for _ in range(3):
                    next(merge)
                    yield
            yield
            yield
            next(rows2, None)
            if 3 <= i:
                d_scatter(i - 3)
            for _ in merge:
                pass
            if 2 <= i <= NB + 1:
                d_logits(i - 2)
            for _ in rows2:
                pass

        def beside_out(i):
            steps = gates(i - 2) if 2 <= i <= NB + 1 else iter(())
            next(steps, None)
            yield
            if i < NB:
                d_turn(i)
            yield
            next(steps, None)
            if i < NB:
                d_out_low(i)
            yield
            for _ in steps:
                pass

        for i in range(NB + 3):
            if 1 <= i < NB:
                d_load(i)
            beside = beside_ffn(i)
            if 1 <= i <= NB:
                d_ffn(i - 1, beside)
            for _ in beside:
                pass
            beside = beside_out(i)
            if 1 <= i <= NB:
                d_out(i - 1, beside)
            for _ in beside:
                pass
        layer_done = [(vD.sem, vD.value), (pD.sem, pD.value), (aD.sem, aD.value), (c_pool.sem, c_pool.value),
                      x1_free[0], x1_free[1]]
        dispatched = [t for t in pos_free if t]

        for eng in (sp, dve, act, pe, pool):
            wait(eng, *layer_done)
        phase_memory()
        PIECES = (1, 3, 5, 7)
        POOL_W1 = 1
        NTB = 6
        WSZ = KC * HID
        rounded = sb("expert_rounded", [P, 8 * WSZ + 4 * MC * SLOT + 4 * KC * SLOT], F32R)
        w1_hi, w1_lo = [[cut(rounded, (2 * s_ + i) * WSZ, KC, HID) for i in range(2)] for s_ in range(2)]
        w2_hi, w2_lo = [[cut(rounded, (4 + 2 * s_ + i) * WSZ, MC, D) for i in range(2)] for s_ in range(2)]
        o = 8 * WSZ
        ehid_hi, ehid_lo = [[cut(rounded, o + (2 * s_ + i) * MC * SLOT, MC, SLOT) for i in range(2)] for s_ in range(2)]
        o += 4 * MC * SLOT
        xin_hi, xin_lo = [[cut(rounded, o + (2 * s_ + i) * KC * SLOT, KC, SLOT) for i in range(2)] for s_ in range(2)]
        w1_full = [cut(win_mem, i * WSZ, KC, HID) for i in range(2)]
        w2_full = [cut(win_mem, (2 + i) * WSZ, MC, D) for i in range(2)]
        b2_b = cut(win_mem, 4 * WSZ, E, D)
        expert_mem = sb("expert_mem", [P, 6 * XROW + 6 * D + 4 * SLOT + KC * SLOT])
        xin = [cut(expert_mem, i * 2 * XROW, 2, XROW) for i in range(3)]
        o = 6 * XROW
        yout = [cut(expert_mem, o + i * 2 * D, 2, D) for i in range(3)]
        o += 6 * D
        ehid_full = [cut(expert_mem, o + i * 2 * SLOT, 2, SLOT) for i in range(2)]
        o += 4 * SLOT
        xin_full = cut(expert_mem, o, KC, SLOT)
        slot_tok, slot_gate = sb("slot_tok", [P, NTB, 2], I32), sb("slot_gate", [P, NTB, 2])
        par = [sb(f"par{i}", [P, 2 * KC + MC]) for i in range(3)]
        c_w1e, c_w2e = [[counter(f"expert_w{s_}_{i}") for i in range(2)] for s_ in (1, 2)]
        vE, aE, pE = counter("dve_experts"), counter("act_experts"), counter("pe_experts")
        c_xin = [counter(f"slot_in{i}") for i in range(3)]
        c_y = counter("slot_added")

        per_exp = sb("per_exp", [P, 4, E])
        slot_e = sb("slot_e", [1, NS, E])
        slot_f = sb("slot_f", [1, 5, NS])
        slot_i = sb("slot_i", [1, 2, NS], I32)
        fill_at = sb("fill_at", [1, E], I32)
        filling = cut(expert_mem, 6 * XROW, 2, XROW)

        def v(ins):
            t = vE.mark(ins)
            wait(dve, t)
            return t

        v(dve.memset(filling, 0.0))
        t_fill = v(dve.tensor_copy(filling[:, :, D].bitcast(I32), fill_id[:, :]))
        count, slots, upto = [per_exp[:, i, :] for i in range(3)]
        slots_i = per_exp[:, 3, :].bitcast(I32)
        sj, se, ss, su, sr = [slot_f[:, i, :] for i in range(5)]
        v(dve.tensor_copy(fill_at[:, :], filled[0:1, :]))
        v(dve.tensor_scalar(count, iota_row[:, 0:E], float(CAP), None, ALU.mult))
        v(dve.tensor_tensor(count, filled[:, :], count, ALU.subtract))
        v(dve.tensor_scalar(slots_i, count, float(SLOT - 1), None, ALU.add))
        v(dve.tensor_single_scalar(slots_i, slots_i, 8, ALU.arith_shift_right))
        v(dve.tensor_copy(slots, slots_i))
        v(dve.tensor_tensor_scan(upto, slots, ones[:, 0:E], 0.0, ALU.add, ALU.mult))
        v(dve.tensor_copy(sj, slot_number[:, :]))
        v(dve.tensor_tensor(slot_e[:, :, :], upto[0:1, :].unsqueeze(1).to_broadcast([1, NS, E]),
                            sj.unsqueeze(2).to_broadcast([1, NS, E]), ALU.is_le))
        v(dve.tensor_reduce(se, slot_e[:, :, :], AX.X, ALU.add))
        v(dve.tensor_tensor(slot_e[:, :, :], slot_e[:, :, :], slots[0:1, :].unsqueeze(1).to_broadcast([1, NS, E]), ALU.mult))
        v(dve.tensor_reduce(ss, slot_e[:, :, :], AX.X, ALU.add))
        v(dve.tensor_scalar(su, se, float(E), None, ALU.is_equal))
        v(dve.tensor_tensor(sr, sj, ss, ALU.subtract))
        v(dve.tensor_scalar(sr, sr, float(SLOT), None, ALU.mult))
        v(dve.scalar_tensor_tensor(sr, se, float(CAP), sr, ALU.mult, ALU.add))
        v(dve.tensor_scalar(ss, su, -1.0, 1.0, ALU.mult, ALU.add))
        v(dve.tensor_tensor(sr, sr, ss, ALU.mult))
        v(dve.scalar_tensor_tensor(sr, su, float(E * CAP), sr, ALU.mult, ALU.add))
        v(dve.tensor_copy(slot_i[:, 1, :], sr))
        v(dve.tensor_scalar(se, se, float(E - 1), None, ALU.min))
        t_slot = v(dve.tensor_copy(slot_i[:, 0, :], se))
        xin_free, xinT_free, ehid_free, y_free, par_free = [None] * 3, [None] * 2, [None] * 2, [None] * 3, [None] * 3
        bank_free = [None] * 8
        E_ = {}
        w1_free, w2_free, full_free = [None] * 2, [None] * 2, [[None] * 2, [None] * 2]
        W1_v = W1.rearrange("e (k p) h -> e p k h", p=P)
        W2_v = W2.rearrange("e (m p) d -> e p m d", p=P)

        def e_pick(j):
            E_["sp_e", j] = sp.value_load(slot_i[0:1, 0, j:j + 1], min_val=0, max_val=E - 1)
            E_["sp_row", j] = sp.value_load(slot_i[0:1, 1, j:j + 1], min_val=0, max_val=E * CAP)

        def e_w2(j):
            i = j % 2
            wait(sp, *(full_free[1][i] or ()))
            E_["w2", j] = load(w2_full[i], W2_v[E_["sp_e", j]], c_w2e[i])

        def e_in(j):
            i = j % 3
            wait(sp, *(xin_free[i] or ()))
            E_["in", j] = c_xin[i].mark(sp.dma_start(xin[i], expert_rows[bass.ds(E_["sp_row", j], SLOT), :].rearrange("(t p) d -> p t d", p=P)), 16)

        def e_w1(j):
            i = j % 2
            wait(sp, *(full_free[0][i] or ()))
            E_["w1", j] = load(w1_full[i], W1_v[E_["sp_e", j]], c_w1e[i])

        def e_turn(j):
            i = j % 2
            e = E_["dve_e", j] = dve.value_load(slot_i[0:1, 0, j:j + 1], min_val=0, max_val=E - 1)
            wait(dve, par_free[j % 3])
            t_par = vE.mark(dve.tensor_copy(par[j % 3][:, :], epar[:, e, :]))
            wait(dve, E_["in", j], E_.get(("added", j - NTB)))
            vE.mark(dve.tensor_copy(slot_tok[:, j % NTB, :], xin[j % 3][:, :, D].bitcast(I32)))
            t_tok = vE.mark(dve.tensor_copy(slot_gate[:, j % NTB, :].unsqueeze(2), xin[j % 3][:, :, bass.ds(e + (D + 1), 1)]))
            wait(pe, E_["in", j], bank_free[0])
            for k in range(KC):
                for t in range(2):
                    ins = pe.transpose(bank[0][:, k * SLOT + t * P:k * SLOT + (t + 1) * P], xin[j % 3][:, t, k * P:(k + 1) * P], ident[:, :])
            t = pE.mark(ins)
            xin_free[j % 3] = [t, t_tok]
            E_["transposed", j] = [t, t_par]

        def e_scale(j):
            i = j % 2
            wait(act, *E_["transposed", j], xinT_free[i], E_.get(("inT", j - 1)))
            for k in range(KC):
                for d in (xin_full[:, k, :], xin_hi[i][:, k, :]):
                    t = aE.mark(act.activation(d, bank[0][:, k * SLOT:(k + 1) * SLOT], ACT.Identity,
                                               scale=par[j % 3][:, k:k + 1], bias=par[j % 3][:, KC + k:KC + k + 1]))
            E_["turned", j] = bank_free[0] = t

        def e_low(j):
            i = j % 2
            wait(dve, E_["turned", j])
            E_["inT", j] = vE.mark(low(dve, xin_lo[i], xin_full, xin_hi[i]))

        def split_weights(j1, j2):
            if 0 <= j1 < NS:
                e_scale(j1)
            yield
            for q in range(4):
                if 0 <= j1 < NS:
                    i = j1 % 2
                    full, hi, lo = [w[i].rearrange("p k h -> p (k h)")[:, q * 512:(q + 1) * 512] for w in (w1_full, w1_hi, w1_lo)]
                    wait(act, E_["w1", j1], w1_free[i])
                    t = aE.mark(act.copy(hi, full))
                    eng, c = (pool, c_pool) if q < POOL_W1 else (dve, vE)
                    wait(eng, t)
                    t = E_["w1s", j1, q < POOL_W1] = c.mark(low(eng, lo, full, hi))
                    full_free[0][i] = [E_.get(("w1s", j1, True)), t]
                yield
                if 0 <= j2 < NS:
                    i = j2 % 2
                    full, hi, lo = [w[i].rearrange("p m d -> p (m d)")[:, q * 512:(q + 1) * 512] for w in (w2_full, w2_hi, w2_lo)]
                    wait(act, E_["w2", j2], w2_free[i])
                    t = aE.mark(act.copy(hi, full))
                    wait(pool, t)
                    t = E_["w2s", j2] = c_pool.mark(low(pool, lo, full, hi))
                    full_free[1][i] = [t]
                yield

        def e_first(j, between):
            i = j % 2
            wait(pe, E_["inT", j], E_["w1s", j, False], E_.get(("w1s", j, True)))
            for m in range(MC):
                bk = 1 + m % 4
                wait(pe, bank_free[bk])
                for k in range(KC):
                    ins = split_product(bank[bk][:, 0:SLOT], [w[i][:, k, m * P:(m + 1) * P] for w in (w1_hi, w1_lo)],
                                        [a[i][:, k, :] for a in (xin_hi, xin_lo)], k == 0, k == KC - 1)
                t = pE.mark(ins)
                full = ehid_full[m // 2 % 2]
                wait(act, t, E_.get(("hid_full_used", m // 2 % 2)))
                bank_free[bk] = aE.mark(act.activation(
                    full[:, m % 2, :], bank[bk][:, 0:SLOT], ACT.Gelu, bias=par[j % 3][:, 2 * KC + m:2 * KC + m + 1]))
                if m % 2:
                    hi, lo = ehid_hi[i][:, m - 1:m + 1, :], ehid_lo[i][:, m - 1:m + 1, :]
                    wait(dve, bank_free[bk], ehid_free[i])
                    th = vE.mark(dve.tensor_copy(hi, full))
                if m in PIECES:
                    next(between, None)
                if m % 2:
                    wait(dve, th)
                    E_["hid", j] = E_["hid_full_used", m // 2 % 2] = vE.mark(low(dve, lo, full, hi))
            par_free[j % 3] = bank_free[bk]
            xinT_free[i] = w1_free[i] = t

        def e_second(j):
            i = j % 2
            wait(pe, E_["hid", j], E_["w2s", j])
            wait(dve, y_free[j % 3])
            for t in range(2):
                bk = 5 + t
                wait(pe, bank_free[bk])
                for m in range(MC):
                    ins = split_product(bank[bk][:, 0:D], [h[i][:, m, t * P:(t + 1) * P] for h in (ehid_hi, ehid_lo)],
                                        [w[i][:, m, :] for w in (w2_hi, w2_lo)], m == 0, m == MC - 1)
                E_["y", j, t] = pE.mark(ins)
            ehid_free[i] = w2_free[i] = E_["y", j, 1]

        def e_add(j):
            for t in range(2):
                bk = 5 + t
                wait(dve, E_["y", j, t])
                y = yout[j % 3][:, t, :]
                bank_free[bk] = vE.mark(dve.tensor_tensor(y, bank[bk][:, 0:D], b2_b[:, E_["dve_e", j], :], ALU.add))
                wait(dve, bank_free[bk])
                ty = vE.mark(dve.tensor_scalar(y, y, slot_gate[:, j % NTB, t:t + 1], None, ALU.mult))
            wait(pool, ty, E_.get("added"))
            for t in range(2):
                E_["added"] = E_["added", j] = y_free[j % 3] = c_y.mark(pool.indirect_dma_start(
                    sums, bass.IndirectOffsetOnAxis(ap=slot_tok[:, j % NTB, t:t + 1], axis=0), yout[j % 3][:, t, :], None,
                    compute_op=ALU.add), 16)

        wait(sp, t_slot, *dispatched)
        c_fill = counter("filled_up")
        c_fill2 = counter("filled_up_too")
        wait(act, t_fill, t_slot)
        wait(sp, t_fill)
        load(sums[NT * P:, :].rearrange("(p i) c -> p i c", i=2), filling[:, :, 0:D], c_fill)
        load(expert_rows[E * CAP:, :].rearrange("(p i) c -> p i c", i=2), filling, c_fill)
        for e in range(E):
            eng, c = (sp, c_fill) if e % 2 else (act, c_fill2)
            at = eng.value_load(fill_at[0:1, e:e + 1], min_val=0, max_val=E * CAP)
            c.mark(eng.dma_start(expert_rows[bass.ds(at, SLOT), :].rearrange("(p i) c -> p i c", i=2), filling), 16)
        e_pick(0)
        e_w1(0)
        wait(sp, (c_fill.sem, c_fill.value), (c_fill2.sem, c_fill2.value))
        c_b2 = counter("expert_b2")

        for j in range(NS + 3):
            if 1 <= j < NS:
                e_pick(j)
            if j < NS:
                e_in(j)
            if j == 0:
                t_b2 = load(b2_b, b2.rearrange("e d -> (e d)").unsqueeze(0).to_broadcast([P, E * D]).rearrange("p (e d) -> p e d", d=D), c_b2)
            if 1 <= j <= NS:
                e_w2(j - 1)
            if 1 <= j < NS:
                e_w1(j)
            if 1 <= j <= NS:
                e_turn(j - 1)
            steps = split_weights(j - 1, j - 2)
            if 2 <= j <= NS + 1:
                e_first(j - 2, steps)
            next(steps, None)
            if 1 <= j <= NS:
                e_low(j - 1)
            for _ in steps:
                pass
            if j >= 3:
                e_second(j - 3)
                if j == 3:
                    wait(dve, t_b2)
                e_add(j - 3)

        wait(sp, E_["added"])
        c_out = counter("out_written")
        wait(sp, load(out, sums[0:N, :], c_out))


_INS = ["x", "src", "dst", "L0_gnn_W", "L0_gnn_att_src", "L0_gnn_att_dst", "L0_gnn_bias", "L0_gnn_W_res",
        "L0_gnn_ln1_g", "L0_gnn_ln1_b", "L0_gnn_ln2_g", "L0_gnn_ln2_b", "L0_gnn_ffn_w1", "L0_gnn_ffn_b1",
        "L0_gnn_ffn_w2", "L0_gnn_ffn_b2", "L0_ffn_Wr", "L0_ffn_br", "L0_ffn_ln_g", "L0_ffn_ln_b", "L0_ffn_W1",
        "L0_ffn_b1", "L0_ffn_W2", "L0_ffn_b2"]


def kernel(**inputs):
    import numpy as np
    import concourse.bacc as bacc
    from concourse.bass_utils import run_bass_kernel_spmd

    nc = bacc.Bacc("TRN2", target_bir_lowering=False, num_devices=1)
    arrays, args = {}, []
    for name in _INS:
        a = np.ascontiguousarray(inputs[name])
        if name in ("src", "dst"):
            a = np.pad(a, (0, -len(a) % 256), constant_values=(1 << 20) if name == "dst" else 0)
        arrays[f"in_{name}"] = a
        args.append(nc.dram_tensor(f"in_{name}", a.shape, mybir.dt.from_np(a.dtype), kind="ExternalInput").ap())
    shape = inputs["x"].shape
    args.append(nc.dram_tensor("out", shape, F32, kind="ExternalOutput").ap())
    build(nc, *args)
    result = run_bass_kernel_spmd(nc, [arrays], core_ids=[0])
    return result.results[0]["out"]
```
